# Optimizing a Trainium2 kernel written in Bass

```python
import numpy as np
import jax
import jax.numpy as jnp

def _softmax(x, axis=-1):
    return jax.nn.softmax(x, axis=axis)

def _gelu(x):
    return jax.nn.gelu(x, approximate=True)

def _silu(x):
    return jax.nn.silu(x)

def _sigmoid(x):
    return jax.nn.sigmoid(x)

def _layernorm(x, axis=-1, eps=1e-05):
    m = jnp.mean(x, axis=axis, keepdims=True)
    v = jnp.var(x, axis=axis, keepdims=True)
    return (x - m) / jnp.sqrt(v + eps)

def _scatter_add(tgt, idx, src, axis=0):
    return tgt.at[idx].add(src)

def _segment_sum(src, seg, n):
    return jax.ops.segment_sum(src, seg, n)
kernel_name = 'mk_decoder_postln_d2_seqx_r8_3d9fde'

def setup_inputs(seed: int=0):
    np.random.seed(seed)
    _w = jnp.asarray

    def _rec_inputs():
        import jax
        import jax.numpy as jnp
        _rk = jax.random.key(seed)
        x = 4.136e-05 + 0.9999 * jax.random.normal(jax.random.fold_in(_rk, 1), (32, 128, 128), jnp.float32)
        _lenS = 128 - jax.random.randint(jax.random.fold_in(_rk, 7), (32,), 0, max(1, 128 // 4) + 1, jnp.int32)
        _lenS2 = 128 - jax.random.randint(jax.random.fold_in(_rk, 8), (32,), 0, max(1, 128 // 4) + 1, jnp.int32)
        _ctx_1024P = jax.random.normal(jax.random.fold_in(_rk, 11), (32, 16, 128), jnp.float32)
        _ctx_1024c = jax.random.dirichlet(jax.random.fold_in(_rk, 511), 0.3 * jnp.ones((16,), jnp.float32), (32, 128))
        _ctx_1024t = jnp.einsum('bsk,bkd->bsd', _ctx_1024c, _ctx_1024P)
        _ctx_1024t = _ctx_1024t * jax.lax.rsqrt(jnp.mean(jnp.square(_ctx_1024t)) + 1e-12) * 0.953939
        ctx_1024 = 7.22013e-05 + 1.00017 * (_ctx_1024t + 0.3 * jax.random.normal(jax.random.fold_in(_rk, 611), (32, 128, 128), jnp.float32))
        _validS = jnp.arange(128)[None, :] < _lenS[:, None]
        _validS2 = jnp.arange(128)[None, :] < _lenS2[:, None]
        _causal = jnp.tril(jnp.ones((128, 128), dtype=bool))
        mask_BxSxS2_bf1 = jnp.ones((32, 128, 128), dtype=bool)
        return (x, ctx_1024, mask_BxSxS2_bf1)
    x, ctx_1024, mask_BxSxS2_bf1 = _rec_inputs()

    def _L0_attn_setup():
        import jax, jax.numpy as jnp
        import numpy as np
        import math
        EMBED_DIM = 128
        NUM_HEADS = 16
        HEAD_DIM = EMBED_DIM // NUM_HEADS
        MAX_POS = 64
        SPARSE_TOPK = 32
        B, T = (8, 64)
        key = jax.random.key(seed)
        ks = jax.random.split(key, 12)
        s = 1.0 / math.sqrt(EMBED_DIM)
        inp = {'x': jax.random.normal(ks[0], (B, T, EMBED_DIM), dtype=jnp.float32), 'Wq': jax.random.uniform(ks[1], (EMBED_DIM, EMBED_DIM), jnp.float32, -s, s), 'bq': jax.random.uniform(ks[2], (EMBED_DIM,), jnp.float32, -s, s), 'Wk': jax.random.uniform(ks[3], (EMBED_DIM, EMBED_DIM), jnp.float32, -s, s), 'bk': jax.random.uniform(ks[4], (EMBED_DIM,), jnp.float32, -s, s), 'Wv': jax.random.uniform(ks[5], (EMBED_DIM, EMBED_DIM), jnp.float32, -s, s), 'bv': jax.random.uniform(ks[6], (EMBED_DIM,), jnp.float32, -s, s), 'Wo': jax.random.uniform(ks[7], (EMBED_DIM, EMBED_DIM), jnp.float32, -s, s), 'bo': jax.random.uniform(ks[8], (EMBED_DIM,), jnp.float32, -s, s), 'head_gates': jnp.ones((NUM_HEADS,), dtype=jnp.float32), 'rel_bias': 0.02 * jax.random.normal(ks[9], (2 * MAX_POS - 1, NUM_HEADS), dtype=jnp.float32)}
        return inp
    _L0_attn_all = _L0_attn_setup()
    _L0_attn_in = {k: v for k, v in _L0_attn_all.items() if k in ('Wq', 'bq', 'Wk', 'bk', 'Wv', 'bv', 'Wo', 'bo', 'head_gates', 'rel_bias')}
    del _L0_attn_all

    def _L0_xattn_setup():
        import jax, jax.numpy as jnp
        import numpy as np
        B, T, C, H = (4, 256, 128, 16)
        HD = C // H
        key = jax.random.key(seed)
        ks = jax.random.split(key, 8)
        s = 0.02
        return {'k': jax.random.normal(ks[0], (B, T, C), jnp.float32), 'q': jax.random.normal(ks[1], (B, T, C), jnp.float32), 'v': jax.random.normal(ks[2], (B, T, C), jnp.float32), 'mask': jnp.ones((B, T, T), dtype=bool), 'Wk': jax.random.normal(ks[3], (C, C), jnp.float32) * s, 'bk': jnp.zeros((C,), jnp.float32), 'Wq': jax.random.normal(ks[4], (C, C), jnp.float32) * s, 'bq': jnp.zeros((C,), jnp.float32), 'Wv': jax.random.normal(ks[5], (C, C), jnp.float32) * s, 'bv': jnp.zeros((C,), jnp.float32), 'Wo': jax.random.normal(ks[6], (C, C), jnp.float32) * s, 'bo': jnp.zeros((C,), jnp.float32)}
    _L0_xattn_all = _L0_xattn_setup()
    _L0_xattn_in = {k: v for k, v in _L0_xattn_all.items() if k in ('Wk', 'bk', 'Wq', 'bq', 'Wv', 'bv', 'Wo', 'bo')}
    del _L0_xattn_all

    def _L0_ffn_setup():
        import jax, jax.numpy as jnp
        import numpy as np
        TOP_K = 2
        key = jax.random.key(seed)
        k1, k2, k3, k4, k5 = jax.random.split(key, 5)
        B, S, D, F, E = (2, 128, 128, 256, 8)
        return {'x': jax.random.normal(k1, (B, S, D), dtype=jnp.float32), 'router_kernel_DE': jax.random.normal(k2, (D, E), dtype=jnp.float32) * 0.02, 'kernel_gating_EDF': jax.random.normal(k3, (E, D, F), dtype=jnp.float32) * 0.02, 'kernel_up_EDF': jax.random.normal(k4, (E, D, F), dtype=jnp.float32) * 0.02, 'kernel_down_EFD': jax.random.normal(k5, (E, F, D), dtype=jnp.float32) * 0.02}
    _L0_ffn_all = _L0_ffn_setup()
    _L0_ffn_in = {k: v for k, v in _L0_ffn_all.items() if k in ('router_kernel_DE', 'kernel_gating_EDF', 'kernel_up_EDF', 'kernel_down_EFD')}
    del _L0_ffn_all

    def _L1_attn_setup():
        import jax, jax.numpy as jnp
        import numpy as np
        B, T, C, H = (4, 256, 128, 16)
        INIT_STD = 0.02
        key = jax.random.key(seed)
        ks = jax.random.split(key, 9)
        x = jax.random.normal(ks[0], (B, T, C), dtype=jnp.float32)

        def dense(kw):
            return jax.random.normal(kw, (C, C), dtype=jnp.float32) * INIT_STD
        return {'x': x, 'Wq': dense(ks[1]), 'bq': jnp.zeros((C,), jnp.float32), 'Wk': dense(ks[2]), 'bk': jnp.zeros((C,), jnp.float32), 'Wv': dense(ks[3]), 'bv': jnp.zeros((C,), jnp.float32), 'Wo': dense(ks[4]), 'bo': jnp.zeros((C,), jnp.float32)}
    _L1_attn_all = _L1_attn_setup()
    _L1_attn_in = {k: v for k, v in _L1_attn_all.items() if k in ('Wq', 'bq', 'Wk', 'bk', 'Wv', 'bv', 'Wo', 'bo')}
    del _L1_attn_all

    def _L1_xattn_setup():
        import jax, jax.numpy as jnp
        import numpy as np
        import math
        NUM_HEADS = 16
        TOPK = 64
        EMBED = 128

        def _topk_attention(Q, K, V, topk):
            d = Q.shape[-1]
            scores = jnp.einsum('bhqd,bhkd->bhqk', Q, K) / jnp.sqrt(jnp.asarray(d, Q.dtype))
            topk_scores, topk_idx = jax.lax.top_k(scores, topk)
            probs = jax.nn.softmax(topk_scores, axis=-1)
            gather = jax.vmap(jax.vmap(lambda Vbh, idx: Vbh[idx]))
            sel = gather(V, topk_idx)
            return jnp.einsum('bhqk,bhqkd->bhqd', probs, sel)
        key = jax.random.key(seed)
        ks = jax.random.split(key, 11)
        b, s, e = (2, 256, EMBED)
        scale = 1.0 / math.sqrt(e)
        inp = {'q': jax.random.normal(ks[0], (b, s, e), dtype=jnp.float32), 'k': jax.random.normal(ks[1], (b, s, e), dtype=jnp.float32), 'v': jax.random.normal(ks[2], (b, s, e), dtype=jnp.float32), 'Wq': jax.random.normal(ks[3], (e, e), dtype=jnp.float32) * scale, 'bq': jnp.zeros((e,), dtype=jnp.float32), 'Wk': jax.random.normal(ks[4], (e, e), dtype=jnp.float32) * scale, 'bk': jnp.zeros((e,), dtype=jnp.float32), 'Wv': jax.random.normal(ks[5], (e, e), dtype=jnp.float32) * scale, 'bv': jnp.zeros((e,), dtype=jnp.float32), 'Wo': jax.random.normal(ks[6], (e, e), dtype=jnp.float32) * scale, 'bo': jnp.zeros((e,), dtype=jnp.float32)}
        return inp
    _L1_xattn_all = _L1_xattn_setup()
    _L1_xattn_in = {k: v for k, v in _L1_xattn_all.items() if k in ('Wq', 'bq', 'Wk', 'bk', 'Wv', 'bv', 'Wo', 'bo')}
    del _L1_xattn_all

    def _L1_ffn_setup():
        import jax, jax.numpy as jnp
        import numpy as np
        B, S, D = (4, 256, 128)
        E, K = (8, 2)
        H = 176
        key = jax.random.key(seed)
        kx, kr, k1, k2, k3 = jax.random.split(key, 5)
        s = 0.02
        return {'x': jax.random.normal(kx, (B, S, D), dtype=jnp.float32), 'w_router': jax.random.normal(kr, (E, D), dtype=jnp.float32) * s, 'w1': jax.random.normal(k1, (E, D, H), dtype=jnp.float32) * s, 'w2': jax.random.normal(k2, (E, H, D), dtype=jnp.float32) * s, 'w3': jax.random.normal(k3, (E, D, H), dtype=jnp.float32) * s}
    _L1_ffn_all = _L1_ffn_setup()
    _L1_ffn_in = {k: v for k, v in _L1_ffn_all.items() if k in ('w_router', 'w1', 'w2', 'w3')}
    del _L1_ffn_all
    return {'x': x, 'ctx_1024': ctx_1024, 'mask_BxSxS2_bf1': mask_BxSxS2_bf1, 'L0_attn_Wq': _L0_attn_in['Wq'], 'L0_attn_bq': _L0_attn_in['bq'], 'L0_attn_Wk': _L0_attn_in['Wk'], 'L0_attn_bk': _L0_attn_in['bk'], 'L0_attn_Wv': _L0_attn_in['Wv'], 'L0_attn_bv': _L0_attn_in['bv'], 'L0_attn_Wo': _L0_attn_in['Wo'], 'L0_attn_bo': _L0_attn_in['bo'], 'L0_attn_head_gates': _L0_attn_in['head_gates'], 'L0_attn_rel_bias': _L0_attn_in['rel_bias'], 'L0_xattn_Wk': _L0_xattn_in['Wk'], 'L0_xattn_bk': _L0_xattn_in['bk'], 'L0_xattn_Wq': _L0_xattn_in['Wq'], 'L0_xattn_bq': _L0_xattn_in['bq'], 'L0_xattn_Wv': _L0_xattn_in['Wv'], 'L0_xattn_bv': _L0_xattn_in['bv'], 'L0_xattn_Wo': _L0_xattn_in['Wo'], 'L0_xattn_bo': _L0_xattn_in['bo'], 'L0_ffn_router_kernel_DE': _L0_ffn_in['router_kernel_DE'], 'L0_ffn_kernel_gating_EDF': _L0_ffn_in['kernel_gating_EDF'], 'L0_ffn_kernel_up_EDF': _L0_ffn_in['kernel_up_EDF'], 'L0_ffn_kernel_down_EFD': _L0_ffn_in['kernel_down_EFD'], 'L1_attn_Wq': _L1_attn_in['Wq'], 'L1_attn_bq': _L1_attn_in['bq'], 'L1_attn_Wk': _L1_attn_in['Wk'], 'L1_attn_bk': _L1_attn_in['bk'], 'L1_attn_Wv': _L1_attn_in['Wv'], 'L1_attn_bv': _L1_attn_in['bv'], 'L1_attn_Wo': _L1_attn_in['Wo'], 'L1_attn_bo': _L1_attn_in['bo'], 'L1_xattn_Wq': _L1_xattn_in['Wq'], 'L1_xattn_bq': _L1_xattn_in['bq'], 'L1_xattn_Wk': _L1_xattn_in['Wk'], 'L1_xattn_bk': _L1_xattn_in['bk'], 'L1_xattn_Wv': _L1_xattn_in['Wv'], 'L1_xattn_bv': _L1_xattn_in['bv'], 'L1_xattn_Wo': _L1_xattn_in['Wo'], 'L1_xattn_bo': _L1_xattn_in['bo'], 'L1_ffn_w_router': _L1_ffn_in['w_router'], 'L1_ffn_w1': _L1_ffn_in['w1'], 'L1_ffn_w2': _L1_ffn_in['w2'], 'L1_ffn_w3': _L1_ffn_in['w3']}

def reference(x, ctx_1024, mask_BxSxS2_bf1, L0_attn_Wq, L0_attn_bq, L0_attn_Wk, L0_attn_bk, L0_attn_Wv, L0_attn_bv, L0_attn_Wo, L0_attn_bo, L0_attn_head_gates, L0_attn_rel_bias, L0_xattn_Wk, L0_xattn_bk, L0_xattn_Wq, L0_xattn_bq, L0_xattn_Wv, L0_xattn_bv, L0_xattn_Wo, L0_xattn_bo, L0_ffn_router_kernel_DE, L0_ffn_kernel_gating_EDF, L0_ffn_kernel_up_EDF, L0_ffn_kernel_down_EFD, L1_attn_Wq, L1_attn_bq, L1_attn_Wk, L1_attn_bk, L1_attn_Wv, L1_attn_bv, L1_attn_Wo, L1_attn_bo, L1_xattn_Wq, L1_xattn_bq, L1_xattn_Wk, L1_xattn_bk, L1_xattn_Wv, L1_xattn_bv, L1_xattn_Wo, L1_xattn_bo, L1_ffn_w_router, L1_ffn_w1, L1_ffn_w2, L1_ffn_w3):
    import jax
    import jax.numpy as jnp

    def _L0_attn_ref(x, Wq, bq, Wk, bk, Wv, bv, Wo, bo, head_gates, rel_bias):
        import jax, jax.numpy as jnp
        import numpy as np
        import math
        EMBED_DIM = 128
        NUM_HEADS = 16
        HEAD_DIM = EMBED_DIM // NUM_HEADS
        MAX_POS = 64
        SPARSE_TOPK = 32
        B, T = (8, 64)
        Bb, Tt, C = x.shape
        H, D = (NUM_HEADS, HEAD_DIM)
        q = (x @ Wq.T + bq).reshape(Bb, Tt, H, D).transpose(0, 2, 1, 3)
        k = (x @ Wk.T + bk).reshape(Bb, Tt, H, D).transpose(0, 2, 1, 3)
        v = (x @ Wv.T + bv).reshape(Bb, Tt, H, D).transpose(0, 2, 1, 3)
        scores = jnp.einsum('bhqd,bhkd->bhqk', q, k) / math.sqrt(D)
        idx = jnp.arange(Tt)
        rel = idx[None, :] - idx[:, None] + (MAX_POS - 1)
        pos_bias = rel_bias[rel].transpose(2, 0, 1)[None]
        scores = scores + pos_bias
        if SPARSE_TOPK > 0:
            topk_vals, _ = jax.lax.top_k(scores, SPARSE_TOPK)
            thresh = topk_vals[..., -1:]
            scores = jnp.where(scores >= thresh, scores, -jnp.inf)
        weights = jax.nn.softmax(scores, axis=-1)
        gated = weights * head_gates[None, :, None, None]
        attn_out = jnp.einsum('bhqk,bhkd->bhqd', gated, v)
        attn_out = attn_out.transpose(0, 2, 1, 3).reshape(Bb, Tt, C)
        return attn_out @ Wo.T + bo

    def _L0_xattn_ref(k, q, v, mask, Wk, bk, Wq, bq, Wv, bv, Wo, bo):
        import jax, jax.numpy as jnp
        import numpy as np
        B, T, C, H = (4, 256, 128, 16)
        HD = C // H
        Bn, Tk, Cn = k.shape
        Tq = q.shape[1]
        hd = Cn // H
        kp = (k @ Wk + bk).reshape(Bn, Tk, H, hd).transpose(0, 2, 1, 3)
        qp = (q @ Wq + bq).reshape(Bn, Tq, H, hd).transpose(0, 2, 1, 3)
        vp = (v @ Wv + bv).reshape(Bn, Tk, H, hd).transpose(0, 2, 1, 3)
        att = jnp.einsum('bhqd,bhkd->bhqk', qp, kp) * (1.0 / jnp.sqrt(jnp.float32(hd)))
        causal = jnp.tril(jnp.ones((Tq, Tk), dtype=bool))
        m = causal[None, None, :, :] & mask[:, None, :, :]
        att = jnp.where(m, att, jnp.float32(-1000000000.0))
        att = jax.nn.softmax(att, axis=-1)
        y = jnp.einsum('bhqk,bhkd->bhqd', att, vp)
        y = y.transpose(0, 2, 1, 3).reshape(Bn, Tq, Cn)
        return y @ Wo + bo

    def _L0_ffn_ref(x, router_kernel_DE, kernel_gating_EDF, kernel_up_EDF, kernel_down_EFD):
        import jax, jax.numpy as jnp
        import numpy as np
        TOP_K = 2
        E = router_kernel_DE.shape[-1]
        x = x.astype(jnp.float32)
        logits_BSE = jnp.einsum('BSD,DE->BSE', x, router_kernel_DE)
        probs_BSE = jax.nn.softmax(logits_BSE.astype(jnp.float32), axis=-1)
        weights_BSK, indices_BSK = jax.lax.top_k(probs_BSE, TOP_K)
        norm_weights_BSK = jax.nn.softmax(weights_BSK, axis=-1)
        one_hot_BSKE = jax.nn.one_hot(indices_BSK, num_classes=E, dtype=x.dtype)
        full_weights_BSE = jnp.sum(one_hot_BSKE * norm_weights_BSK[..., None], axis=2)
        gating_BSEF = jnp.einsum('BSD,EDF->BSEF', x, kernel_gating_EDF)
        act_BSEF = jax.nn.silu(gating_BSEF)
        up_BSEF = jnp.einsum('BSD,EDF->BSEF', x, kernel_up_EDF)
        fuse_BSEF = act_BSEF * up_BSEF
        down_BSED = jnp.einsum('BSEF,EFD->BSED', fuse_BSEF, kernel_down_EFD)
        out_BSD = jnp.einsum('BSED,BSE->BSD', down_BSED, full_weights_BSE)
        return out_BSD.astype(jnp.float32)

    def _L1_attn_ref(x, Wq, bq, Wk, bk, Wv, bv, Wo, bo):
        import jax, jax.numpy as jnp
        import numpy as np
        B, T, C, H = (4, 256, 128, 16)
        INIT_STD = 0.02
        b, t, c = x.shape
        hd = c // H

        def split_heads(y):
            return jnp.transpose(y.reshape(b, t, H, hd), (0, 2, 1, 3))
        q = split_heads(x @ Wq + bq)
        k = split_heads(x @ Wk + bk)
        v = split_heads(x @ Wv + bv)
        scale = 1.0 / jnp.sqrt(jnp.float32(hd))
        att = jnp.einsum('bhqd,bhkd->bhqk', q, k) * scale
        mask = jnp.tril(jnp.ones((t, t), dtype=bool))[None, None]
        att = jnp.where(mask, att, jnp.float32(-jnp.inf))
        att = jax.nn.softmax(att, axis=-1)
        y = jnp.einsum('bhqk,bhkd->bhqd', att, v)
        y = jnp.transpose(y, (0, 2, 1, 3)).reshape(b, t, c)
        return y @ Wo + bo

    def _L1_xattn_ref(q, k, v, Wq, bq, Wk, bk, Wv, bv, Wo, bo):
        import jax, jax.numpy as jnp
        import numpy as np
        import math
        NUM_HEADS = 16
        TOPK = 64
        EMBED = 128

        def _topk_attention(Q, K, V, topk):
            d = Q.shape[-1]
            scores = jnp.einsum('bhqd,bhkd->bhqk', Q, K) / jnp.sqrt(jnp.asarray(d, Q.dtype))
            topk_scores, topk_idx = jax.lax.top_k(scores, topk)
            probs = jax.nn.softmax(topk_scores, axis=-1)
            gather = jax.vmap(jax.vmap(lambda Vbh, idx: Vbh[idx]))
            sel = gather(V, topk_idx)
            return jnp.einsum('bhqk,bhqkd->bhqd', probs, sel)
        b, s, e = q.shape
        h = NUM_HEADS
        d = e // h
        Q = (q @ Wq.T + bq).reshape(b, h, s, d)
        K = (k @ Wk.T + bk).reshape(b, h, s, d)
        V = (v @ Wv.T + bv).reshape(b, h, s, d)
        attn = _topk_attention(Q, K, V, TOPK)
        out = attn.reshape(b, s, e)
        return out @ Wo.T + bo

    def _L1_ffn_ref(x, w_router, w1, w2, w3):
        import jax, jax.numpy as jnp
        import numpy as np
        B, S, D = (4, 256, 128)
        E, K = (8, 2)
        H = 176
        bsz, seqlen, dim = x.shape
        xf = x.reshape(-1, dim)
        scores = jax.nn.softmax(xf @ w_router.T, axis=-1)
        expert_weights, expert_indices = jax.lax.top_k(scores, K)
        h = jax.nn.silu(jnp.einsum('td,edh->eth', xf, w1)) * jnp.einsum('td,edh->eth', xf, w3)
        y = jnp.einsum('eth,ehd->etd', h, w2)
        y_t = jnp.swapaxes(y, 0, 1)
        sel = jnp.take_along_axis(y_t, expert_indices[:, :, None], axis=1)
        out = jnp.sum(expert_weights[:, :, None] * sel, axis=1)
        return out.reshape(bsz, seqlen, dim)
    x = _layernorm(x + _L0_attn_ref(x, L0_attn_Wq, L0_attn_bq, L0_attn_Wk, L0_attn_bk, L0_attn_Wv, L0_attn_bv, L0_attn_Wo, L0_attn_bo, L0_attn_head_gates, L0_attn_rel_bias), axis=-1)
    x = _layernorm(x + _L0_xattn_ref(ctx_1024, x, ctx_1024, mask_BxSxS2_bf1, L0_xattn_Wk, L0_xattn_bk, L0_xattn_Wq, L0_xattn_bq, L0_xattn_Wv, L0_xattn_bv, L0_xattn_Wo, L0_xattn_bo), axis=-1)
    x = _layernorm(x + _L0_ffn_ref(x, L0_ffn_router_kernel_DE, L0_ffn_kernel_gating_EDF, L0_ffn_kernel_up_EDF, L0_ffn_kernel_down_EFD), axis=-1)
    x = _layernorm(x + _L1_attn_ref(x, L1_attn_Wq, L1_attn_bq, L1_attn_Wk, L1_attn_bk, L1_attn_Wv, L1_attn_bv, L1_attn_Wo, L1_attn_bo), axis=-1)
    x = _layernorm(x + _L1_xattn_ref(x, ctx_1024, ctx_1024, L1_xattn_Wq, L1_xattn_bq, L1_xattn_Wk, L1_xattn_bk, L1_xattn_Wv, L1_xattn_bv, L1_xattn_Wo, L1_xattn_bo), axis=-1)
    x = _layernorm(x + _L1_ffn_ref(x, L1_ffn_w_router, L1_ffn_w1, L1_ffn_w2, L1_ffn_w3), axis=-1)
    return x

_drawn_inputs = setup_inputs


def setup_inputs(seed=0):
    import zlib

    import numpy as np

    out = dict(_drawn_inputs(seed))
    spreads = {'L0_attn_head_gates': (1.0, 0.6),
     'L0_xattn_bk': (0.0, 0.8),
     'L0_xattn_bq': (0.0, 0.8),
     'L0_xattn_bv': (0.0, 0.349),
     'L0_xattn_bo': (0.0, 0.1),
     'L1_attn_bq': (0.0, 0.8),
     'L1_attn_bk': (0.0, 0.8),
     'L1_attn_bv': (0.0, 0.32),
     'L1_attn_bo': (0.0, 0.1),
     'L1_xattn_bq': (0.0, 0.303),
     'L1_xattn_bk': (0.0, 0.288),
     'L1_xattn_bv': (0.0, 0.364),
     'L1_xattn_bo': (0.0, 0.1)}
    factors = {'L0_attn_bq': 4.399,
     'L0_attn_bk': 8.0,
     'L0_attn_rel_bias': 5.323,
     'L0_xattn_Wk': 8.0,
     'L0_xattn_Wq': 8.0,
     'L0_ffn_router_kernel_DE': 8.0,
     'L0_ffn_kernel_gating_EDF': 8.0,
     'L0_ffn_kernel_up_EDF': 8.0,
     'L0_ffn_kernel_down_EFD': 8.0,
     'L1_attn_Wq': 8.0,
     'L1_attn_Wk': 8.0,
     'L1_attn_Wv': 4.438,
     'L1_ffn_w_router': 8.0,
     'L1_ffn_w1': 8.0,
     'L1_ffn_w2': 8.0,
     'L1_ffn_w3': 8.0}
    for name, (base, spread) in spreads.items():
        noise = np.random.default_rng([zlib.crc32(name.encode()), seed]).standard_normal(out[name].shape)
        drawn = base * np.exp(spread * noise) if base else spread * noise
        out[name] = jnp.asarray(drawn.astype(out[name].dtype))
    for name, factor in factors.items():
        out[name] = (out[name] * factor).astype(out[name].dtype)
    return out
```

```python
from contextlib import ExitStack

import numpy as np

import concourse.bass as bass
from concourse import mybir

F32 = mybir.dt.float32
BF16 = mybir.dt.bfloat16
ALU = mybir.AluOpType
ACT = mybir.ActivationFunctionType
AX = mybir.AxisListType

P = 128
H = 16
HD = 8
NQ = 4
QH = 4
BIG = float(2.0 ** 60)
TAKEN = -3.0e38
EPS = 1e-5


class Batch:

    def __init__(self, off, reg=None, step=2):
        self.off, self.reg, self.step = off, reg, step

    def plus(self, n):
        return Batch(self.off + n, self.reg, self.step)

    @property
    def par(self):
        return self.off % 2

    def within(self, n):
        return self.reg is not None or 0 <= self.off < n

    def count(self, each, more=0):
        if self.reg is None:
            return each * self.off + more
        return self.reg * (self.step * each) + (each * self.off + more)

    def count_par(self, each):
        if self.reg is None:
            return each * (self.off // 2 + 1)
        return self.reg * each + each * (self.off // 2 + 1)

    @property
    def index(self):
        return self.off if self.reg is None else self.reg * 2 + self.off


def wait(eng, sem, batch, each, more):
    if batch.reg is None and batch.off < 0:
        return
    eng.wait_ge(sem, batch.count(each, more))


def wait_par(eng, sems, batch, each):
    if batch.reg is None and batch.off < 0:
        return
    eng.wait_ge(sems[batch.par], batch.count_par(each))


def slots(eng, body, nb):
    first, last = 4, nb - 2
    for t in range(-2, first):
        body(Batch(t))
    with eng.Fori(0, (last - first) // 2) as i:
        body(Batch(first, i))
        body(Batch(first + 1, i))
    for t in range(last, nb + 2):
        body(Batch(t))


def bcast(ap, axis, n):
    return ap.unsqueeze(axis).to_broadcast([*ap.shape[:axis], n, *ap.shape[axis:]])


class Consts:
    pass


def clear(nc, sems):
    with nc.Block() as block:
        @block.sync
        def _(sp):
            for s in sems:
                sp.sem_clear(s)


def constants(nc, ctx):
    c = Consts()

    def sb(name, shape, dt=F32):
        return ctx.enter_context(nc.sbuf_tensor(name, shape, dt))

    c.ident = sb("ident", [P, P])
    c.flip = sb("flip", [P, P])
    c.identbig = sb("identbig", [P, P], BF16)
    c.causal = sb("causal", [P, P], BF16)
    c.onesrow = sb("onesrow", [P, P])
    c.eps = sb("eps", [P, 1])
    c.minushalf = sb("minushalf", [P, 1])
    c.headmask = sb("headmask", [P, H])
    c.groupmask = sb("groupmask", [P, QH])
    c.banks = [ctx.enter_context(nc.psum_tensor(f"bank{n}", [P, 512], F32)) for n in range(8)]
    built = ctx.enter_context(nc.semaphore("const_built"))
    vbuilt = ctx.enter_context(nc.semaphore("const_derived"))
    with nc.Block() as block:
        @block.gpsimd
        def _(pool):
            pool.memset(c.ident[:], 0.0).then_inc(built, 1)
            pool.memset(c.flip[:], 0.0).then_inc(built, 1)
            pool.memset(c.causal[:], 0.0).then_inc(built, 1)
            pool.memset(c.headmask[:], 1.0).then_inc(built, 1)
            pool.memset(c.groupmask[:], 1.0).then_inc(built, 1)
            pool.memset(c.onesrow[:], 1.0).then_inc(built, 1)
            pool.memset(c.eps[:], EPS).then_inc(built, 1)
            pool.memset(c.minushalf[:], -0.5).then_inc(built, 1)
            pool.wait_ge(built, 8)
            pool.affine_select(out=c.ident[:], in_=c.ident[:], compare_op=ALU.not_equal, fill=1.0,
                               base=0, pattern=[[-1, P]], channel_multiplier=1).then_inc(built, 1)
            pool.affine_select(out=c.flip[:], in_=c.flip[:], compare_op=ALU.not_equal, fill=1.0,
                               base=1 - P, pattern=[[1, P]], channel_multiplier=1).then_inc(built, 1)
            pool.affine_select(out=c.causal[:], in_=c.causal[:], compare_op=ALU.is_ge, fill=-1.0,
                               base=0, pattern=[[-1, P]], channel_multiplier=1).then_inc(built, 1)
            pool.affine_select(out=c.headmask[:], in_=c.headmask[:], compare_op=ALU.is_ge, fill=0.0,
                               base=0, pattern=[[-HD, H]], channel_multiplier=1).then_inc(built, 1)
            pool.affine_select(out=c.groupmask[:], in_=c.groupmask[:], compare_op=ALU.is_ge, fill=0.0,
                               base=0, pattern=[[-32, QH]], channel_multiplier=1).then_inc(built, 1)
            pool.wait_ge(built, 13)
            pool.affine_select(out=c.headmask[:], in_=c.headmask[:], compare_op=ALU.is_ge, fill=0.0,
                               base=HD - 1, pattern=[[HD, H]], channel_multiplier=-1).then_inc(built, 1)
            pool.affine_select(out=c.groupmask[:], in_=c.groupmask[:], compare_op=ALU.is_ge, fill=0.0,
                               base=31, pattern=[[32, QH]], channel_multiplier=-1).then_inc(built, 1)

        @block.vector
        def _(dve):
            dve.wait_ge(built, 15)
            dve.tensor_scalar(c.identbig[:], c.ident[:], BIG, None, ALU.mult).then_inc(vbuilt, 1)
    return c


def attention(nc, name, c, x, kv, out, wq, bq, wk, bk, wv, bv, wo, bo, *,
              transposed, mask=None, causal=False, topk=0, gates=None, rel_bias=None, bias_rows=None,
              scrambled=False):
    NB = x.shape[0]
    ROUNDS = topk // 8
    scale = float(HD) ** -0.5
    with ExitStack() as ctx:
        def sb(nm, shape, dt=F32):
            return ctx.enter_context(nc.sbuf_tensor(f"{name}_{nm}", shape, dt))

        sems = []

        def sem(nm):
            sems.append(ctx.enter_context(nc.semaphore(f"{name}_{nm}")))
            return sems[-1]

        w_raw = sb("w_raw", [P, 4, P])
        w_t = sb("w_t", [P, 4, P]) if transposed else w_raw
        Wq, Wk, Wv, Wo = (w_t[:, n, :] for n in range(4))
        bcol = sb("bcol", [P, 4])
        bq_s = sb("bq_s", [P, 1])
        bv_g = sb("bv_g", [P, 1])
        bo_pad = sb("bo_pad", [P, P])
        x_tok = sb("x_tok", [P, 2, P])
        kv_tok = sb("kv_tok", [P, 2, P]) if kv is not None else None
        x_res = sb("x_res", [P, 2, P])
        xkT = sb("xkT", [P, 2, P])
        q_t = sb("q_t", [P, 2, P])
        k_t = sb("k_t", [P, P])
        k_bd = sb("k_bd", [P, 2, H, P])
        v_pad = sb("v_pad", [P, 2, H, 32])
        p_sb = sb("p", [P, NQ, QH, P])
        pT = sb("pT", [P, 2, QH, P])
        neg_max = sb("neg_max", [P, NQ, QH])
        o_raw = sb("o_raw", [P, NQ, P])
        r_sum = sb("r_sum", [P, H])
        o_n = sb("o_n", [P, P])
        oT = sb("oT", [P, P])
        stats = sb("stats", [P, 6])
        mv = sb("mv", [P, 2])
        var_eps = sb("var_eps", [P, 1])
        rstd = sb("rstd", [P, 1])
        x_new = sb("x_new", [P, 2, P])
        if topk:
            s_sb = sb("s", [P, NQ, QH, P])
            work = sb("work", [P, NQ, QH, P])
            top8 = sb("top8", [P, NQ, QH, ROUNDS, 8])
            keep = sb("keep", [P, QH, P])
        if rel_bias is not None:
            bias_sb = sb("bias_sb", [P, H, P])
            R = rel_bias.shape[0]
            LO = (R + 1) // 2
            table = sb("table", [R, H])
            rows_sb = sb("rows", [H, 2 * LO + R])
        if mask is not None:
            m_raw = sb("m_raw", [P, 2, P], mybir.dt.uint8)
            m_add = sb("m_add", [P, 2, P], BF16)
        if scrambled:
            pick = sb("pick", [P, H, 32])
            lin = sb("lin", [P, 3, P])
            q32 = sb("q32", [P, 2, NQ, P])
            k32 = sb("k32", [P, NQ, P])
            v32 = sb("v32", [P, NQ, P])
            rowmask = sb("rowmask", [P, H])
            place = sb("place", [P, 4, 32])
            o_x = sb("o_x", [P, H, H, HD])
            o_tok = sb("o_tok", [P, P])

        S = c.banks[0:2]
        PT = c.banks[2:4]
        PROJ = c.banks[4]
        O = c.banks[5]
        OT = c.banks[6]
        Y = c.banks[7]

        weights_in = sem("weights_in")
        tok_in = [sem("tok_in0"), sem("tok_in1")]
        res_in = [sem("res_in0"), sem("res_in1")]
        stored = [sem("stored0"), sem("stored1")]
        set_pool = sem("set_pool")
        set_pe = sem("set_pe")
        set_act = sem("set_act")
        set_dve = sem("set_dve")
        if rel_bias is not None:
            table_in = sem("table_in")
            table_turned = sem("table_turned")
            rows_ready = sem("rows_ready")
            rows_out = sem("rows_out")
            bias_in = sem("bias_in")
        tr_done = sem("tr_done")
        proj_done = sem("proj_done")
        s_done = sem("s_done")
        pt_done = sem("pt_done")
        pv_done = sem("pv_done")
        ot_done = sem("ot_done")
        ont_done = sem("ont_done")
        y_done = sem("y_done")
        xkT_ready = sem("xkT_ready")
        qk_ready = sem("qk_ready")
        v_ready = sem("v_ready")
        s_copied = sem("s_copied")
        exp_done = sem("exp_done")
        pT_ready = sem("pT_ready")
        o_copied = sem("o_copied")
        oT_ready = sem("oT_ready")
        chain = sem("chain")
        quad_begun = sem("quad_begun")
        max_ready = sem("max_ready")
        top_ready = sem("top_ready")
        on_ready = sem("on_ready")
        stats_ready = sem("stats_ready")
        x_ready = sem("x_ready")
        m_ready = sem("m_ready")
        kbd_ready = sem("kbd_ready")
        p_ready = sem("p_ready")
        keep_ready = sem("keep_ready")
        step_begun = sem("step_begun")
        var_ready = sem("var_ready")
        rstd_ready = sem("rstd_ready")
        if scrambled:
            pick_done = sem("pick_done")
            picked = sem("picked")
            ox_ready = sem("ox_ready")
            r_done = sem("r_done")
            otok_ready = sem("otok_ready")

        n_weight_dmas = 4 + 4 + (1 if gates is not None else 0)
        tok_dmas = 1 + (kv is not None) + (mask is not None)
        n_set_act = 1 + (gates is not None) + transposed

        with nc.Block() as block:
            @block.sync
            def _(sp):
                if rel_bias is not None:
                    sp.dma_start(table[:], rel_bias).then_inc(table_in, 16)
                for n, w in enumerate((wq, wk, wv, wo)):
                    sp.dma_start(w_raw[:, n, :], w).then_inc(weights_in, 16)
                for n, b in enumerate((bq, bk, bv)):
                    sp.dma_start(bcol[:, n:n + 1], b.rearrange("(p a) -> p a", a=1)).then_inc(weights_in, 16)
                if gates is not None:
                    sp.dma_start(bcol[:, 3:4], bcast(gates, 1, HD).unsqueeze(2)).then_inc(weights_in, 16)
                sp.wait_ge(set_pool, 1)
                sp.dma_start(bo_pad[0:1, :], bo.rearrange("(a n) -> a n", a=1)).then_inc(weights_in, 16)
                if rel_bias is not None:
                    sp.wait_ge(rows_ready, 3)
                    sp.dma_start(bias_rows, rows_sb[:]).then_inc(rows_out, 16)
                    sp.wait_ge(rows_out, 16)
                    rows = bass.AP(bias_rows.tensor, 0, [[1, P], [bias_rows.shape[1], H], [1, P]])
                    sp.dma_start(bias_sb[:], rows).then_inc(bias_in, 16)

                def slot(t):
                    load = t.plus(2)
                    if load.within(NB):
                        wait(sp, tr_done, t, 1, 1)
                        if mask is not None:
                            wait(sp, m_ready, t, 1, 1)
                        sp.dma_start(x_tok[:, t.par, :], x[load.index]).then_inc(tok_in[t.par], 16)
                        if kv is not None:
                            sp.dma_start(kv_tok[:, t.par, :], kv[load.index]).then_inc(tok_in[t.par], 16)
                        if mask is not None:
                            sp.dma_start(m_raw[:, t.par, :], mask[load.index]).then_inc(tok_in[t.par], 16)
                    if t.within(NB):
                        wait(sp, y_done, t.plus(-2), 1, 1)
                        sp.dma_start(x_res[:, t.par, :], x[t.index]).then_inc(res_in[t.par], 16)
                    done = t.plus(-2)
                    if done.within(NB):
                        wait(sp, x_ready, done, 1, 1)
                        sp.dma_start(out[done.index], x_new[:, t.par, :]).then_inc(stored[t.par], 16)

                slots(sp, slot, NB)
                for par in range(2):
                    sp.wait_ge(stored[par], 16 * (NB // 2))

            @block.gpsimd
            def _(pool):
                pool.memset(bo_pad[:], 0.0).then_inc(set_pool, 1)
                pool.memset(v_pad[:], 0.0).then_inc(set_pool, 1)
                pool.wait_ge(set_pool, 2)
                pool.memset(v_pad[:, :, :, HD:HD + 1], 1.0).then_inc(set_pool, 1)
                if scrambled:
                    pool.memset(pick[:], 0.0).then_inc(set_pool, 1)
                    pool.memset(place[:], 0.0).then_inc(set_pool, 1)

                def slot(t):
                    for q in range(NQ):
                        b, j = (t, q - 1) if q else (t.plus(-1), NQ - 1)
                        if topk and b.within(NB):
                            wait(pool, top_ready, b, NQ, j + 1)
                            p, n = (b, j - 1) if j else (b.plus(-1), NQ - 1)
                            wait(pool, p_ready, p, NQ, n + 1)
                            pool.sem_inc(step_begun, 1)
                            if scrambled:
                                pool.tensor_scalar(keep[:], work[:, j, :, :], 0.5 * TAKEN, None, ALU.is_lt)\
                                    .then_inc(keep_ready, 1)
                            else:
                                for h in range(QH):
                                    op = pool.tensor_scalar(keep[:, h, :], s_sb[:, j, h, :],
                                                            top8[:, j, h, ROUNDS - 1, 7:8], None, ALU.is_ge)
                                op.then_inc(keep_ready, 1)
                            wait(pool, exp_done, b, NQ, j + 1)
                            wait(pool, keep_ready, b, NQ, j + 1)
                            op = pool.tensor_tensor(p_sb[:, j, :, :], p_sb[:, j, :, :], keep[:], ALU.mult)
                            op.then_inc(p_ready, 1)
                        b = t.plus(-2)
                        if scrambled and q == 0 and b.within(NB):
                            wait(pool, on_ready, b, 1, 1)
                            wait(pool, r_done, b.plus(-1), 1, 1)
                            pool.tensor_tensor(
                                o_x[:], bcast(o_n[:].rearrange("p (h d) -> p h d", h=H), 2, H),
                                bcast(bcast(rowmask[:], 1, H), 3, HD), ALU.mult).then_inc(ox_ready, 1)
                        if q == 2 and b.within(NB):
                            wait(pool, stats_ready, b, 1, 1)
                            pool.tensor_tensor(var_eps[:], mv[:, 1:2], c.eps[:], ALU.add).then_inc(var_ready, 1)
                            wait(pool, var_ready, b, 1, 1)
                            pool.tensor_tensor(rstd[:], var_eps[:], c.minushalf[:], ALU.pow)\
                                .then_inc(rstd_ready, 1)
                        b = t.plus(1)
                        if q >= 2 and b.within(NB):
                            if q == 2:
                                if scrambled:
                                    wait(pool, picked, b, 3, 2)
                                else:
                                    wait(pool, qk_ready, b, 2, 2)
                            for j in (0, 1) if q == 2 else (2, 3):
                                if scrambled:
                                    kk, mm = k32[:, j, :], c.groupmask[:]
                                else:
                                    kk, mm = k_t[:], c.headmask[:, QH * j:QH * j + QH]
                                pool.tensor_tensor(k_bd[:, b.par, QH * j:QH * j + QH, :], bcast(kk, 1, QH),
                                                   bcast(mm, 2, P), ALU.mult).then_inc(kbd_ready, 1)

                slots(pool, slot, NB)

            @block.tensor
            def _(pe):
                if rel_bias is not None:
                    pe.wait_ge(table_in, 16)
                    pe.transpose(Y[0:H, 0:R], table[:], c.ident[0:R, 0:R]).then_inc(table_turned, 1)
                pe.wait_ge(weights_in, 16 * n_weight_dmas)
                if transposed:
                    for n in range(4):
                        mm = pe.transpose(PROJ[:, P * n:P * n + P], w_raw[:, n, :], c.ident[:])
                    mm.then_inc(set_pe, 1)
                pe.wait_ge(set_act, n_set_act)
                pe.wait_ge(set_pool, 3)
                if scrambled:
                    pe.wait_ge(set_dve, 4)
                if rel_bias is not None:
                    pe.wait_ge(bias_in, 16)

                def transposes(b):
                    wait_par(pe, tok_in, b, 16 * tok_dmas)
                    wait(pe, v_ready, b.plus(-1), 1, 1)
                    mm = pe.transpose(PROJ[:, 0:P], x_tok[:, b.par, :], c.ident[:])
                    if kv is not None:
                        mm = pe.transpose(PROJ[:, P:2 * P], kv_tok[:, b.par, :], c.ident[:])
                    mm.then_inc(tr_done, 1)

                def project(b):
                    xT, kT = xkT[:, 0, :], xkT[:, 1 if kv is not None else 0, :]
                    wait(pe, xkT_ready, b, 1, 1)
                    pe.matmul(PROJ[:, 0:P], Wq, xT, start=True, stop=True)
                    pe.matmul(PROJ[:, P:2 * P], Wk, kT, start=True, stop=True)
                    if scrambled:
                        mm = pe.matmul(PROJ[:, 2 * P:3 * P], Wv, kT, start=True, stop=True)
                    else:
                        mm = pe.matmul(PROJ[:, 2 * P:3 * P], kT, Wv, start=True, stop=True)
                    mm.then_inc(proj_done, 1)

                def pick_heads(b, n):
                    src = lin[:, n, :].rearrange("p (j g t) -> p g j t", j=NQ, g=QH)
                    dst = PROJ[:].rearrange("p (j t r) -> p j t r", j=NQ, r=H)
                    if n == 0:
                        wait(pe, qk_ready, b, 3, 3)
                    else:
                        wait(pe, picked, b, 3, n)
                    for r in range(H):
                        for g in range(QH):
                            mm = pe.matmul(dst[32 * g:32 * g + 32, :, :, r], pick[:, r, :], src[:, g],
                                           start=True, stop=True)
                    mm.then_inc(pick_done, 1)

                def transpose_v(b):
                    wait(pe, picked, b, 3, 3)
                    for j in range(NQ):
                        mm = pe.transpose(PROJ[:, P * j:P * j + P], v32[:, j, :], c.ident[:])
                    mm.then_inc(pick_done, 1)

                def scores(b, j):
                    wait(pe, kbd_ready, b, NQ, j + 1)
                    if mask is not None and j == 0:
                        wait(pe, m_ready, b, 1, 1)
                    p, n = (b, j - 2) if j >= 2 else (b.plus(-1), j + 2)
                    wait(pe, s_copied if topk else exp_done, p, NQ, n + 1)
                    lhs = q32[:, b.par, j, :] if scrambled else q_t[:, b.par, :]
                    dst = S[j % 2][:]
                    added = mask is not None or causal or rel_bias is not None
                    mm = pe.matmul(dst, lhs, k_bd[:, b.par, QH * j:QH * j + QH, :], start=True, stop=not added)
                    if mask is not None:
                        mm = pe.matmul(dst, c.identbig[:], bcast(m_add[:, b.par, :], 1, QH), start=False, stop=True)
                    elif causal:
                        mm = pe.matmul(dst, c.identbig[:], bcast(c.causal[:], 1, QH), start=False, stop=True)
                    elif rel_bias is not None:
                        mm = pe.matmul(dst, c.flip[:], bias_sb[:, QH * j:QH * j + QH, :], start=False, stop=True)
                    mm.then_inc(s_done, 1)

                def transpose_p(b, j):
                    wait(pe, p_ready if topk else exp_done, b, NQ, j + 1)
                    p, n = (b, j - 2) if j >= 2 else (b.plus(-1), j + 2)
                    wait(pe, pT_ready, p, NQ, n + 1)
                    for h in range(QH):
                        mm = pe.transpose(PT[j % 2][:, P * h:P * h + P], p_sb[:, j, h, :], c.ident[:])
                    mm.then_inc(pt_done, 1)

                def weigh_v(b, j):
                    wait(pe, pT_ready, b, NQ, j + 1)
                    if j == 0:
                        wait(pe, v_ready, b, 1, 1)
                        wait(pe, o_copied, b.plus(-1), 1, 1)
                    for g in range(QH):
                        mm = pe.matmul(O[32 * g:32 * g + 32, P * j:P * j + P], v_pad[:, b.par, QH * j + g, :],
                                       pT[:, j % 2, g, :], start=True, stop=True)
                    mm.then_inc(pv_done, 1)

                def transpose_o(b):
                    wait(pe, o_copied, b, 1, 1)
                    wait(pe, on_ready, b.plus(-1), 1, 1)
                    for j in range(NQ):
                        mm = pe.transpose(OT[:, P * j:P * j + P], o_raw[:, j, :], c.ident[:])
                    mm.then_inc(ot_done, 1)

                def unscramble(b):
                    wait(pe, ox_ready, b, 1, 1)
                    wait(pe, x_ready, b.plus(-1), 1, 1)
                    for hh in range(4):
                        for j in range(NQ):
                            mm = pe.matmul(Y[32 * j:32 * j + 32, 0:P], place[:, hh, :],
                                           o_x[:, 4 * j + hh, :, :], start=(hh == 0), stop=(hh == 3),
                                           skip_group_check=True)
                    mm.then_inc(r_done, 1)

                def transpose_on(b):
                    if scrambled:
                        wait(pe, otok_ready, b, 1, 1)
                    else:
                        wait(pe, on_ready, b, 1, 1)
                        wait(pe, x_ready, b.plus(-1), 1, 1)
                    pe.transpose(Y[:, 0:P], (o_tok if scrambled else o_n)[:], c.ident[:]).then_inc(ont_done, 1)

                def project_out(b):
                    wait(pe, oT_ready, b, 1, 1)
                    wait_par(pe, res_in, b, 16)
                    pe.matmul(Y[:, 0:P], oT[:], Wo, start=True, stop=False)
                    pe.matmul(Y[:, 0:P], c.onesrow[:], bo_pad[:], start=False, stop=False)
                    pe.matmul(Y[:, 0:P], c.ident[:], x_res[:, b.par, :], start=False, stop=True)\
                        .then_inc(y_done, 1)

                def slot(t):
                    ahead, prev, prev2 = t.plus(1), t.plus(-1), t.plus(-2)
                    for q in range(NQ):
                        if q == 0 and ahead.within(NB):
                            transposes(ahead)
                        if t.within(NB):
                            scores(t, q)
                        b, j = (t, q - 2) if q >= 2 else (prev, q + 2)
                        if b.within(NB):
                            transpose_p(b, j)
                        b, j = (t, q - 3) if q >= 3 else (prev, q + 1)
                        if b.within(NB):
                            weigh_v(b, j)
                        if q == 0 and prev2.within(NB) and not scrambled:
                            transpose_on(prev2)
                        if q == 1 and prev2.within(NB):
                            if scrambled:
                                unscramble(prev2)
                                transpose_on(prev2)
                            project_out(prev2)
                        if q == 1 and ahead.within(NB):
                            project(ahead)
                            if scrambled:
                                pick_heads(ahead, 0)
                        if scrambled and q == 2 and ahead.within(NB):
                            pick_heads(ahead, 1)
                        if q == 3 and prev.within(NB):
                            transpose_o(prev)
                        if scrambled and q == 3 and ahead.within(NB):
                            pick_heads(ahead, 2)
                            transpose_v(ahead)

                slots(pe, slot, NB)

            @block.scalar
            def _(act):
                act.wait_ge(weights_in, 16 * n_weight_dmas)
                act.mul(bq_s[:], bcol[:, 0:1], scale).then_inc(set_act, 1)
                if gates is not None:
                    act.activation(bv_g[:], bcol[:, 2:3], ACT.Identity, scale=bcol[:, 3:4]).then_inc(set_act, 1)
                if transposed:
                    act.wait_ge(set_pe, 1)
                    act.activation(w_t[:].rearrange("p a b -> p (a b)"), PROJ[:], ACT.Copy).then_inc(set_act, 1)

                def slot(t):
                    ahead, prev, prev2 = t.plus(1), t.plus(-1), t.plus(-2)
                    for q in range(NQ):
                        if q == 0 and ahead.within(NB):
                            n = 2 if kv is not None else 1
                            wait(act, tr_done, ahead, 1, 1)
                            act.activation(xkT[:, 0:n, :], PROJ[:, 0:n * P], ACT.Copy).then_inc(xkT_ready, 1)
                        if topk and t.within(NB):
                            wait(act, s_done, t, NQ, q + 1)
                            act.activation(s_sb[:, q, :, :], S[q % 2][:], ACT.Copy).then_inc(s_copied, 1)
                        if topk:
                            b, j = (t, q - 1) if q else (prev, NQ - 1)
                        else:
                            b, j = t, q
                        if b.within(NB):
                            wait(act, max_ready, b, NQ, j + 1)
                            for h in range(QH):
                                src = s_sb[:, j, h, :] if topk else S[j % 2][:, P * h:P * h + P]
                                op = act.activation(p_sb[:, j, h, :], src, ACT.Exp, bias=neg_max[:, j, h:h + 1])
                            op.then_inc(exp_done, 1)
                        b, j = (t, q - 2) if q >= 2 else (prev, q + 2)
                        if topk and b.within(NB):
                            wait(act, pt_done, b, NQ, j + 1)
                            p, n = (b, j - 2) if j >= 2 else (b.plus(-1), j + 2)
                            wait(act, pv_done, p, NQ, n + 1)
                            act.activation(pT[:, j % 2, :, :], PT[j % 2][:], ACT.Copy).then_inc(pT_ready, 1)
                        if q == 1 and scrambled and prev2.within(NB):
                            wait(act, r_done, prev2, 1, 1)
                            act.activation(o_tok[:], Y[:, 0:P], ACT.Copy).then_inc(otok_ready, 1)
                        if q == (1 if scrambled else 0) and prev2.within(NB):
                            wait(act, ont_done, prev2, 1, 1)
                            if scrambled:
                                op = act.activation(oT[:], Y[:, 0:P], ACT.Copy)
                            elif gates is not None:
                                op = act.activation(oT[:], Y[:, 0:P], ACT.Identity, bias=bv_g[:], scale=bcol[:, 3:4])
                            else:
                                op = act.activation(oT[:], Y[:, 0:P], ACT.Identity, bias=bcol[:, 2:3])
                            op.then_inc(oT_ready, 1)
                        if q == 1 and ahead.within(NB):
                            wait(act, proj_done, ahead, 1, 1)
                            if scrambled:
                                act.activation(lin[:, 0, :], PROJ[:, 0:P], ACT.Identity, bias=bq_s[:], scale=scale)\
                                    .then_inc(qk_ready, 1)
                                for n in (1, 2):
                                    act.activation(lin[:, n, :], PROJ[:, P * n:P * n + P], ACT.Identity,
                                                   bias=bcol[:, n:n + 1]).then_inc(qk_ready, 1)
                                wait(act, pick_done, ahead, 4, 1)
                                act.activation(q32[:, ahead.par, :, :], PROJ[:], ACT.Copy).then_inc(picked, 1)
                            else:
                                act.activation(q_t[:, ahead.par, :], PROJ[:, 0:P], ACT.Identity,
                                               bias=bq_s[:], scale=scale).then_inc(qk_ready, 1)
                                wait(act, kbd_ready, t, NQ, NQ)
                                act.activation(k_t[:], PROJ[:, P:2 * P], ACT.Identity, bias=bcol[:, 1:2])\
                                    .then_inc(qk_ready, 1)
                        if q == 2 and scrambled and ahead.within(NB):
                            wait(act, pick_done, ahead, 4, 2)
                            wait(act, kbd_ready, t, NQ, NQ)
                            act.activation(k32[:], PROJ[:], ACT.Copy).then_inc(picked, 1)
                        if q == 2 and prev.within(NB):
                            wait(act, pv_done, prev, NQ, NQ)
                            wait(act, ot_done, prev2, 1, 1)
                            act.activation(o_raw[:], O[:], ACT.Copy).then_inc(o_copied, 1)
                        if q == 3 and ahead.within(NB):
                            src = PROJ[:, 2 * P:3 * P].rearrange("p (h d) -> p h d", h=H)
                            if scrambled:
                                wait(act, pick_done, ahead, 4, 3)
                                act.activation(v32[:], PROJ[:], ACT.Copy).then_inc(picked, 1)
                                wait(act, pick_done, ahead, 4, 4)
                                src = PROJ[:].rearrange("p (h d) -> p h d", h=H)[:, :, 0:HD]
                            wait(act, pv_done, prev, NQ, NQ)
                            act.activation(v_pad[:, ahead.par, :, 0:HD], src, ACT.Copy).then_inc(v_ready, 1)

                act.wait_ge(set_act, n_set_act)
                act.wait_ge(set_pool, 3)
                slots(act, slot, NB)

            @block.vector
            def _(dve):
                steps = [0]

                def own(ins):
                    ins.then_inc(chain, 1)
                    steps[0] += 1
                    return steps[0]

                if scrambled:
                    dve.wait_ge(set_pool, 5)
                    dve.tensor_copy(pick[:, :, 0:HD], c.ident[:].rearrange("p (r d) -> p r d", r=H)).then_inc(set_dve, 1)
                    dve.tensor_reduce(rowmask[:], c.ident[:].rearrange("p (t r) -> p r t", t=HD), AX.X, ALU.add)\
                        .then_inc(set_dve, 1)
                    for hh in range(4):
                        op = dve.tensor_reduce(place[:, hh, HD * hh:HD * hh + HD],
                                               c.ident[:].rearrange("p (t r) -> p t r", t=HD), AX.X, ALU.add)
                        if hh >= 2:
                            op.then_inc(set_dve, 1)

                if rel_bias is not None:
                    dve.wait_ge(table_turned, 1)
                    dve.tensor_copy(rows_sb[:, 0:LO], Y[0:H, R - LO:R]).then_inc(rows_ready, 1)
                    dve.tensor_copy(rows_sb[:, LO:LO + R], Y[0:H, 0:R]).then_inc(rows_ready, 1)
                    dve.tensor_copy(rows_sb[:, LO + R:], Y[0:H, R - 1:R].to_broadcast([H, LO])).then_inc(rows_ready, 1)

                def top_k(b, j):
                    wait(dve, s_copied, b, NQ, j + 1)
                    dve.sem_inc(quad_begun, 1)
                    replaced = [0] * QH
                    for r in range(ROUNDS):
                        found = []
                        for h in range(QH):
                            src = work if r else s_sb
                            if r:
                                dve.wait_ge(chain, replaced[h])
                            op = dve.max(top8[:, j, h, r, :], src[:, j, h, :])
                            if r == ROUNDS - 1 and not scrambled and h == QH - 1:
                                op.then_inc(top_ready, 1)
                            else:
                                found.append(own(op))
                        if r == ROUNDS - 1 and not scrambled:
                            break
                        for h in range(QH):
                            dve.wait_ge(chain, found[h])
                            op = dve.match_replace(out=work[:, j, h, :], in_to_replace=top8[:, j, h, r, :],
                                                   in_values=(work if r else s_sb)[:, j, h, :], imm_value=TAKEN)
                            if r == ROUNDS - 1 and h == QH - 1:
                                op.then_inc(top_ready, 1)
                            else:
                                replaced[h] = own(op)
                        if r == 0:
                            dve.tensor_scalar(neg_max[:, j, :], top8[:, j, :, 0, 0], -1.0, None, ALU.mult)\
                                .then_inc(max_ready, 1)

                def slot(t):
                    prev, prev2 = t.plus(-1), t.plus(-2)
                    if steps[0]:
                        dve.wait_ge(chain, steps[0])
                        dve.sem_clear(chain)
                    steps[0] = 0
                    if mask is not None and t.plus(1).within(NB):
                        b = t.plus(1)
                        wait_par(dve, tok_in, b, 16 * tok_dmas)
                        wait(dve, s_done, prev, NQ, NQ)
                        dve.scalar_tensor_tensor(out=m_add[:, b.par, :], in0=m_raw[:, b.par, :], scalar=1.0,
                                                 in1=c.causal[:], op0=ALU.subtract, op1=ALU.min)\
                            .then_inc(m_ready, 1)
                    for q in range(NQ):
                        if q == 0 and prev2.within(NB):
                            wait(dve, ot_done, prev2, 1, 1)
                            o4 = OT[:].rearrange("p (h e) -> p h e", h=H)
                            n = own(dve.reciprocal(r_sum[:], o4[:, :, HD]))
                            dve.wait_ge(chain, n)
                            dve.tensor_tensor(o_n[:].rearrange("p (h d) -> p h d", h=H), o4[:, :, 0:HD],
                                              bcast(r_sum[:], 2, HD), ALU.mult).then_inc(on_ready, 1)
                        if q == 2 and prev2.within(NB):
                            wait(dve, y_done, prev2, 1, 1)
                            n = own(dve.bn_stats(stats[:], Y[:, 0:P]))
                            dve.wait_ge(chain, n)
                            dve.bn_aggr(mv[:], stats[:]).then_inc(stats_ready, 1)
                        if q == 3 and prev2.within(NB):
                            wait_par(dve, stored, t.plus(-4), 16)
                            wait(dve, rstd_ready, prev2, 1, 1)
                            dve.tensor_scalar(x_new[:, t.par, :], Y[:, 0:P], mv[:, 0:1], rstd[:, 0:1],
                                              ALU.subtract, ALU.mult).then_inc(x_ready, 1)
                        if t.within(NB) and topk:
                            top_k(t, q)
                        elif t.within(NB):
                            wait(dve, s_done, t, NQ, q + 1)
                            dve.tensor_reduce(neg_max[:, q, :], S[q % 2][:].rearrange("p (h k) -> p h k", h=QH),
                                              AX.X, ALU.max, negate=True).then_inc(max_ready, 1)
                        b, j = (t, q - 2) if q >= 2 else (prev, q + 2)
                        if not topk and b.within(NB):
                            wait(dve, pt_done, b, NQ, j + 1)
                            p, n = (b, j - 2) if j >= 2 else (b.plus(-1), j + 2)
                            wait(dve, pv_done, p, NQ, n + 1)
                            dve.tensor_copy(pT[:, j % 2, :, :], PT[j % 2][:]).then_inc(pT_ready, 1)

                slots(dve, slot, NB)

        clear(nc, sems)


def experts(nc, name, c, x, out, router, wgate, wup, wdown, *, renormalise):
    NB = x.shape[0]
    TB = 4
    NT = NB // TB
    TW = TB * P
    E, _, F = wgate.shape
    NC = E * F // P
    PER = F // P if F % P == 0 else 1
    SPAN = P if F % P == 0 else F
    NW = NC // PER
    PARTS = 3
    with ExitStack() as ctx:
        def sb(nm, shape, dt=F32):
            return ctx.enter_context(nc.sbuf_tensor(f"{name}_{nm}", shape, dt))

        sems = []

        def sem(nm):
            sems.append(ctx.enter_context(nc.semaphore(f"{name}_{nm}")))
            return sems[-1]

        w_router = sb("w_router", [P, E])
        w_gate = sb("w_gate", [P, E, F])
        w_up = sb("w_up", [P, E, F])
        w_down = sb("w_down", [P, NC, P])
        x_all = sb("x_all", [P, NB, P])
        xT_all = sb("xT_all", [P, NT, TW])
        wT = sb("wT", [32 * PARTS, NT, TW], BF16)
        spread = sb("spread", [32 * PARTS, NW, P], BF16)

        x_in = [sem(f"x_in{u}") for u in range(NT)]
        w_in = sem("w_in")
        stored = [sem("stored0"), sem("stored1")]
        router_in = sem("router_in")

        gate_cols = w_gate[:].rearrange("p e f -> p (e f)")
        up_cols = w_up[:].rearrange("p e f -> p (e f)")

        with ExitStack() as rctx:
            def rsb(nm, shape, dt=F32):
                return rctx.enter_context(nc.sbuf_tensor(f"{name}_{nm}", shape, dt))

            logit = rsb("logit", [P, NB, E])
            prob = rsb("prob", [P, NB, E])
            order = rsb("order", [P, E])
            best = rsb("best", [P, 2, NB])
            hit = rsb("hit", [P, 2, NB, E])
            rank = rsb("rank", [P, NB, E])
            red = rsb("red", [P, NB])
            gap = rsb("gap", [P, NB])
            share = rsb("share", [P, 2, NB])
            weight = rsb("weight", [P, NB, E])
            part = rsb("part", [P, NB, PARTS, 32], BF16)
            identb = rsb("identb", [P, P], BF16)
            XT = c.banks[0:2]
            LG = c.banks[2]
            WT = [b[:].bitcast(BF16) for b in c.banks[3:7]]
            t_done = sem("t_done")
            t_copied = sem("t_copied")
            lg_done = sem("lg_done")
            shifted = sem("shifted")
            expd = sem("expd")
            gap_ready = sem("gap_ready")
            gap_expd = sem("gap_expd")
            step = sem("step")
            part_ready = sem("part_ready")
            wt_done = sem("wt_done")
            wt_copied = sem("wt_copied")
            base_set = sem("base_set")
            WB_PER = 1024 // P
            NWT = (NB + WB_PER - 1) // WB_PER

            with nc.Block() as block:
                @block.sync
                def _(sp):
                    with nc.allow_non_contiguous_dma("4 KB, once"):
                        sp.dma_start(w_router[:].unsqueeze(2), router.unsqueeze(2)).then_inc(router_in, 16)
                    for u in range(NT):
                        sp.dma_start(x_all[:, TB * u:TB * u + TB, :],
                                     x[TB * u:TB * u + TB].rearrange("b t d -> t b d")).then_inc(x_in[u], 16)
                    sp.dma_start(w_gate[:], wgate.rearrange("e d f -> d e f")).then_inc(w_in, 16)
                    sp.dma_start(w_up[:], wup.rearrange("e d f -> d e f")).then_inc(w_in, 16)
                    sp.dma_start(w_down[:], wdown.rearrange("e f d -> (e f) d").rearrange("(c p) d -> p c d", p=P))\
                        .then_inc(w_in, 16)

                @block.gpsimd
                def _(pool):
                    pool.memset(spread[:], 0.0).then_inc(base_set, 1)
                    pool.memset(part[:], 0.0).then_inc(base_set, 1)
                    pool.iota(order[:], pattern=[[-1, E]], base=E, channel_multiplier=0,
                              allow_small_or_imprecise_dtypes=True).then_inc(base_set, 1)
                    pool.wait_ge(base_set, 3)
                    first = spread[0:E]
                    pool.memset(first, 1.0).then_inc(base_set, 1)
                    pool.wait_ge(base_set, 4)
                    pool.affine_select(out=first, in_=first, compare_op=ALU.is_ge, fill=0.0,
                                       base=0, pattern=[[P, NW], [1, P]], channel_multiplier=-SPAN).then_inc(base_set, 1)
                    pool.wait_ge(base_set, 5)
                    pool.affine_select(out=first, in_=first, compare_op=ALU.is_ge, fill=0.0,
                                       base=SPAN - 1, pattern=[[-P, NW], [-1, P]], channel_multiplier=SPAN)\
                        .then_inc(base_set, 1)

                @block.tensor
                def _(pe):
                    for u in range(NT):
                        pe.wait_ge(x_in[u], 16)
                        if u >= 2:
                            pe.wait_ge(t_copied, u - 1)
                        for s in range(TB):
                            mm = pe.transpose(XT[u % 2][:, P * s:P * s + P], x_all[:, TB * u + s, :], c.ident[:])
                        mm.then_inc(t_done, 1)
                    pe.wait_ge(router_in, 16)
                    for b in range(NB):
                        if b % TB == 0:
                            pe.wait_ge(t_copied, b // TB + 1)
                        mm = pe.matmul(LG[:, E * b:E * b + E], xT_all[:, b // TB, P * (b % TB):P * (b % TB) + P],
                                       w_router[:], start=True, stop=True)
                    mm.then_inc(lg_done, 1)
                    pe.wait_ge(part_ready, PARTS)
                    for b in range(NB):
                        mm = pe.transpose(WT[b // WB_PER][0:32 * PARTS, P * (b % WB_PER):P * (b % WB_PER) + P],
                                          part[:, b, :, :].rearrange("p n e -> p (n e)"), identb[:])
                    mm.then_inc(wt_done, 1)

                @block.scalar
                def _(act):
                    for u in range(NT):
                        act.wait_ge(t_done, u + 1)
                        act.activation(xT_all[:, u, :], XT[u % 2][:], ACT.Copy).then_inc(t_copied, 1)
                    act.wait_ge(shifted, 1)
                    act.activation(prob[:], logit[:], ACT.Exp).then_inc(expd, 1)
                    if renormalise:
                        act.wait_ge(gap_ready, 1)
                        act.activation(share[:, 1, :], gap[:], ACT.Exp).then_inc(gap_expd, 1)

                @block.vector
                def _(dve):
                    steps = [0]

                    def then(ins):
                        ins.then_inc(step, 1)
                        steps[0] += 1
                        dve.wait_ge(step, steps[0])

                    def rows(ap):
                        return bcast(ap, 2, E)

                    then(dve.tensor_copy(identb[:], c.ident[:]))
                    dve.wait_ge(lg_done, 1)
                    lg = LG[:, 0:NB * E].rearrange("p (b e) -> p b e", b=NB)
                    then(dve.tensor_reduce(red[:], lg, AX.X, ALU.max))
                    dve.tensor_tensor(logit[:], lg, rows(red[:]), ALU.subtract).then_inc(shifted, 1)
                    dve.wait_ge(expd, 1)
                    then(dve.tensor_reduce(red[:], prob[:], AX.X, ALU.add))
                    then(dve.reciprocal(red[:], red[:]))
                    then(dve.tensor_tensor(prob[:], prob[:], rows(red[:]), ALU.mult))
                    dve.wait_ge(base_set, 6)
                    src = prob
                    for n in range(2):
                        then(dve.tensor_reduce(best[:, n, :], src[:], AX.X, ALU.max))
                        then(dve.tensor_tensor(rank[:], src[:], rows(best[:, n, :]), ALU.is_equal))
                        then(dve.tensor_tensor(rank[:], rank[:], bcast(order[:], 1, NB), ALU.mult))
                        then(dve.tensor_reduce(red[:], rank[:], AX.X, ALU.max))
                        then(dve.tensor_tensor(hit[:, n], rank[:], rows(red[:]), ALU.is_equal))
                        if n == 0:
                            then(dve.scalar_tensor_tensor(out=logit[:], in0=hit[:, 0], scalar=-2.0, in1=prob[:],
                                                          op0=ALU.mult, op1=ALU.add))
                            src = logit
                    if renormalise:
                        dve.tensor_tensor(gap[:], best[:, 1, :], best[:, 0, :], ALU.subtract).then_inc(gap_ready, 1)
                        dve.wait_ge(gap_expd, 1)
                        then(dve.tensor_scalar(red[:], share[:, 1, :], 1.0, None, ALU.add))
                        then(dve.reciprocal(share[:, 0, :], red[:]))
                        then(dve.tensor_tensor(share[:, 1, :], share[:, 1, :], share[:, 0, :], ALU.mult))
                    two = share if renormalise else best
                    then(dve.tensor_tensor(weight[:], hit[:, 0], rows(two[:, 0, :]), ALU.mult))
                    then(dve.tensor_tensor(rank[:], hit[:, 1], rows(two[:, 1, :]), ALU.mult))
                    then(dve.tensor_tensor(weight[:], weight[:], rank[:], ALU.add))
                    for n in range(PARTS):
                        dve.tensor_copy(part[:, :, n, 0:E], weight[:]).then_inc(part_ready, 1)
                        if n < PARTS - 1:
                            dve.wait_ge(part_ready, n + 1)
                            then(dve.tensor_tensor(weight[:], weight[:], part[:, :, n, 0:E], ALU.subtract))
                    for n in range(1, PARTS):
                        then(dve.tensor_copy(spread[32 * n:32 * n + E], spread[0:E]))
                    dve.wait_ge(wt_done, 1)
                    flat = wT[:].rearrange("p u t -> p (u t)")
                    for n in range(NWT):
                        w = min(1024, NB * P - 1024 * n)
                        dve.tensor_copy(flat[:, 1024 * n:1024 * n + w], WT[n][0:32 * PARTS, 0:w]).then_inc(wt_copied, 1)

        silu = sb("silu", [P, 2, TW])
        prod = sb("prod", [P, 2, TW])
        hid = sb("hid", [P, 2, TW])
        oT = sb("oT", [P, TW])
        z = sb("z", [P, TB, P])
        stats = sb("stats", [P, TB, 6])
        mv = sb("mv", [P, TB, 2])
        var_eps = sb("var_eps", [P, TB])
        rstd = sb("rstd", [P, TB])
        x_new = sb("x_new", [P, 2, TB, P])
        G, U, WB = c.banks[0:2], c.banks[2:4], c.banks[4:6]
        OUT, TOK = c.banks[6], c.banks[7]
        g_done = sem("g_done")
        u_done = sem("u_done")
        wb_done = sem("wb_done")
        d_done = sem("d_done")
        tok_done = sem("tok_done")
        silu_ready = sem("silu_ready")
        out_copied = sem("out_copied")
        prod_ready = sem("prod_ready")
        hid_ready = sem("hid_ready")
        z_ready = sem("z_ready")
        stats_ready = sem("stats_ready")
        x_ready = sem("x_ready")
        var_ready = sem("var_ready")
        rstd_ready = sem("rstd_ready")
        chain = sem("chain")

        def pairs(eng, body):
            body(Batch(0))
            if NT > 2:
                with eng.Fori(0, NT // 2 - 1) as i:
                    body(Batch(1, i, 1))

        def before(eng, sem, pair, each, n):
            if pair.reg is not None or n > 0:
                eng.wait_ge(sem, pair.count(each, n))

        def tile(pair, par):
            return par if pair.reg is None else pair.reg * 2 + (2 * pair.off + par)

        with nc.Block() as block:
            @block.sync
            def _(sp):
                def body(pair):
                    for par in range(2):
                        u = tile(pair, par)
                        before(sp, x_ready, pair, 2, par + 1)
                        sp.dma_start(out[bass.ds(u * TB, TB)].rearrange("b t d -> t b d"), x_new[:, par])\
                            .then_inc(stored[par], 16)

                pairs(sp, body)
                for par in range(2):
                    sp.wait_ge(stored[par], 16 * (NT // 2))

            @block.gpsimd
            def _(pool):
                def body(pair):
                    for par in range(2):
                        before(pool, stats_ready, pair, 2, par + 1)
                        pool.tensor_tensor(var_eps[:], mv[:, :, 1], c.eps[:].to_broadcast([P, TB]), ALU.add)\
                            .then_inc(var_ready, 1)
                        before(pool, var_ready, pair, 2, par + 1)
                        pool.tensor_tensor(rstd[:], var_eps[:], c.minushalf[:].to_broadcast([P, TB]), ALU.pow)\
                            .then_inc(rstd_ready, 1)

                pairs(pool, body)

            @block.tensor
            def _(pe):
                pe.wait_ge(w_in, 48)

                def down(pair, n):
                    k = n % NC
                    before(pe, hid_ready, pair, 2 * NC, n + 1)
                    if k == 0:
                        before(pe, out_copied, pair, 2, n // NC)
                    pe.matmul(OUT[:], w_down[:, k, :], hid[:, n % 2, :], start=(k == 0), stop=(k == NC - 1))\
                        .then_inc(d_done, 1)

                def to_tokens(pair, par):
                    before(pe, out_copied, pair, 2, par + 1)
                    before(pe, z_ready, pair, 2, par)
                    for s in range(TB):
                        mm = pe.transpose(TOK[:, P * s:P * s + P], oT[:, P * s:P * s + P], c.ident[:])
                    mm.then_inc(tok_done, 1)

                def body(pair):
                    for n in range(2 * NC):
                        par, k = divmod(n, NC)
                        xT = xT_all[:, tile(pair, par), :]
                        before(pe, silu_ready, pair, 2 * NC, n - 1)
                        pe.matmul(G[n % 2][:], gate_cols[:, P * k:P * k + P], xT, start=True, stop=True)\
                            .then_inc(g_done, 1)
                        before(pe, prod_ready, pair, 2 * NC, n - 1)
                        pe.matmul(U[n % 2][:], up_cols[:, P * k:P * k + P], xT, start=True, stop=True)\
                            .then_inc(u_done, 1)
                        if k % PER == 0:
                            w = k // PER
                            m = par * NW + w
                            pm = m - 2
                            last = (pm // NW) * NC + (pm % NW) * PER + PER - 1
                            before(pe, hid_ready, pair, 2 * NC, last + 1)
                            pe.matmul(WB[m % 2][:], spread[:, w, :], wT[:, tile(pair, par), :],
                                      start=True, stop=True).then_inc(wb_done, 1)
                        if k:
                            down(pair, n - 1)
                        if k == NC - 1:
                            down(pair, n)
                        if par == 1 and k == 2:
                            to_tokens(pair, 0)
                    to_tokens(pair, 1)

                pairs(pe, body)

            @block.scalar
            def _(act):
                def copy_out(pair, par):
                    before(act, d_done, pair, 2 * NC, NC * (par + 1))
                    before(act, tok_done, pair, 2, par)
                    act.activation(oT[:], OUT[:], ACT.Copy).then_inc(out_copied, 1)

                def body(pair):
                    for n in range(2 * NC):
                        before(act, g_done, pair, 2 * NC, n + 1)
                        before(act, prod_ready, pair, 2 * NC, n - 1)
                        act.activation(silu[:, n % 2, :], G[n % 2][:], ACT.Silu).then_inc(silu_ready, 1)
                        if n == NC:
                            copy_out(pair, 0)
                    copy_out(pair, 1)

                pairs(act, body)

            @block.vector
            def _(dve):
                def finish(pair, par):
                    done = 0
                    before(dve, tok_done, pair, 2, par + 1)
                    dve.tensor_tensor(z[:], TOK[:].rearrange("p (b d) -> p b d", b=TB),
                                      x_all[:, bass.ds(tile(pair, par) * TB, TB), :], ALU.add).then_inc(z_ready, 1)
                    before(dve, z_ready, pair, 2, par + 1)
                    for s in range(TB):
                        dve.bn_stats(stats[:, s, :], z[:, s, :]).then_inc(chain, 1)
                    for s in range(TB):
                        dve.wait_ge(chain, s + 1)
                        op = dve.bn_aggr(mv[:, s, :], stats[:, s, :])
                        if s == TB - 1:
                            op.then_inc(stats_ready, 1)
                        else:
                            op.then_inc(chain, 1)
                    before(dve, rstd_ready, pair, 2, par + 1)
                    if pair.reg is not None:
                        dve.wait_ge(stored[par], pair.count(16, 0))
                    for s in range(TB):
                        op = dve.tensor_scalar(x_new[:, par, s, :], z[:, s, :], mv[:, s, 0:1], rstd[:, s:s + 1],
                                               ALU.subtract, ALU.mult)
                    op.then_inc(x_ready, 1)
                    dve.wait_ge(chain, 2 * TB - 1)
                    dve.sem_clear(chain)

                def body(pair):
                    for n in range(2 * NC):
                        par, k = divmod(n, NC)
                        before(dve, silu_ready, pair, 2 * NC, n + 1)
                        before(dve, u_done, pair, 2 * NC, n + 1)
                        before(dve, hid_ready, pair, 2 * NC, n - 1)
                        dve.tensor_tensor(prod[:, n % 2, :], silu[:, n % 2, :], U[n % 2][:], ALU.mult)\
                            .then_inc(prod_ready, 1)
                        before(dve, prod_ready, pair, 2 * NC, n + 1)
                        m = par * NW + k // PER
                        before(dve, wb_done, pair, 2 * NW, m + 1)
                        before(dve, d_done, pair, 2 * NC, n - 1)
                        dve.tensor_tensor(hid[:, n % 2, :], prod[:, n % 2, :], WB[m % 2][:], ALU.mult)\
                            .then_inc(hid_ready, 1)
                        if par == 1 and k == 3:
                            finish(pair, 0)
                    finish(pair, 1)

                pairs(dve, body)

        clear(nc, sems)


def decoder(nc, a, out):
    NB = a["x"].shape[0]
    hop = [nc.dram_tensor(f"x_after_{n}", (NB, P, P), F32, kind="Internal").ap() for n in range(5)]
    R = a["L0_attn_rel_bias"].shape[0]
    bias_rows = nc.dram_tensor("bias_rows", (H, 2 * ((R + 1) // 2) + R), F32, kind="Internal").ap()
    ctx_tokens = a["ctx_1024"]

    def weights(prefix):
        return [a[prefix + w] for w in ("Wq", "bq", "Wk", "bk", "Wv", "bv", "Wo", "bo")]

    with ExitStack() as ctx:
        c = constants(nc, ctx)
        attention(nc, "L0_attn", c, a["x"], None, hop[0], *weights("L0_attn_"), transposed=True, topk=32,
                  gates=a["L0_attn_head_gates"], rel_bias=a["L0_attn_rel_bias"], bias_rows=bias_rows)
        attention(nc, "L0_xattn", c, hop[0], ctx_tokens, hop[1], *weights("L0_xattn_"), transposed=False,
                  mask=a["mask_BxSxS2_bf1"])
        experts(nc, "L0_ffn", c, hop[1], hop[2], a["L0_ffn_router_kernel_DE"], a["L0_ffn_kernel_gating_EDF"],
                a["L0_ffn_kernel_up_EDF"], a["L0_ffn_kernel_down_EFD"], renormalise=True)
        attention(nc, "L1_attn", c, hop[2], None, hop[3], *weights("L1_attn_"), transposed=False, causal=True)
        attention(nc, "L1_xattn", c, hop[3], ctx_tokens, hop[4], *weights("L1_xattn_"), transposed=True, topk=64,
                  scrambled=True)
        experts(nc, "L1_ffn", c, hop[4], out, a["L1_ffn_w_router"].rearrange("e d -> d e"), a["L1_ffn_w1"],
                a["L1_ffn_w3"], a["L1_ffn_w2"], renormalise=False)


def kernel(**inputs):
    import numpy as _np
    import concourse.bacc as _bacc
    from concourse import mybir as _mybir
    from concourse.bass_utils import run_bass_kernel_spmd as _run

    nc = _bacc.Bacc("TRN2", target_bir_lowering=False, num_devices=1)
    arrays, args = {}, {}
    for name, value in inputs.items():
        v = _np.ascontiguousarray(value)
        arrays[f"in_{name}_dram"] = v
        args[name] = nc.dram_tensor(f"in_{name}_dram", v.shape, _mybir.dt.from_np(v.dtype), kind="ExternalInput").ap()
    out = nc.dram_tensor("out_0_dram", inputs["x"].shape, F32, kind="ExternalOutput").ap()
    decoder(nc, args, out)
    r = _run(nc, [arrays], core_ids=[0])
    return r.results[0]["out_0_dram"]
```

```python
from contextlib import ExitStack

import numpy as np

import concourse.bass as bass
from concourse import mybir

F32 = mybir.dt.float32
BF16 = mybir.dt.bfloat16
ALU = mybir.AluOpType
ACT = mybir.ActivationFunctionType
AX = mybir.AxisListType

P = 128
H = 16
HD = 8
NQ = 4
QH = 4
BIG = float(2.0 ** 60)
TAKEN = -3.0e38
EPS = 1e-5


class Batch:

    def __init__(self, off, reg=None, step=2):
        self.off, self.reg, self.step = off, reg, step

    def plus(self, n):
        return Batch(self.off + n, self.reg, self.step)

    @property
    def par(self):
        return self.off % 2

    def within(self, n):
        return self.reg is not None or 0 <= self.off < n

    def count(self, each, more=0):
        if self.reg is None:
            return each * self.off + more
        return self.reg * (self.step * each) + (each * self.off + more)

    def count_par(self, each):
        if self.reg is None:
            return each * (self.off // 2 + 1)
        return self.reg * each + each * (self.off // 2 + 1)

    @property
    def index(self):
        return self.off if self.reg is None else self.reg * 2 + self.off


def wait(eng, sem, batch, each, more):
    if batch.reg is None and batch.off < 0:
        return
    eng.wait_ge(sem, batch.count(each, more))


def wait_par(eng, sems, batch, each):
    if batch.reg is None and batch.off < 0:
        return
    eng.wait_ge(sems[batch.par], batch.count_par(each))


def slots(eng, body, nb):
    first, last = 4, nb - 2
    for t in range(-2, first):
        body(Batch(t))
    with eng.Fori(0, (last - first) // 2) as i:
        body(Batch(first, i))
        body(Batch(first + 1, i))
    for t in range(last, nb + 2):
        body(Batch(t))


def bcast(ap, axis, n):
    return ap.unsqueeze(axis).to_broadcast([*ap.shape[:axis], n, *ap.shape[axis:]])


class Consts:
    pass


def clear(nc, sems):
    with nc.Block() as block:
        @block.sync
        def _(sp):
            for s in sems:
                sp.sem_clear(s)


def constants(nc, ctx):
    c = Consts()

    def sb(name, shape, dt=F32):
        return ctx.enter_context(nc.sbuf_tensor(name, shape, dt))

    c.ident = sb("ident", [P, P])
    c.flip = sb("flip", [P, P])
    c.identbig = sb("identbig", [P, P], BF16)
    c.causal = sb("causal", [P, P], BF16)
    c.onesrow = sb("onesrow", [P, P])
    c.eps = sb("eps", [P, 1])
    c.minushalf = sb("minushalf", [P, 1])
    c.headmask = sb("headmask", [P, H])
    c.groupmask = sb("groupmask", [P, QH])
    c.banks = [ctx.enter_context(nc.psum_tensor(f"bank{n}", [P, 512], F32)) for n in range(8)]
    built = ctx.enter_context(nc.semaphore("const_built"))
    vbuilt = ctx.enter_context(nc.semaphore("const_derived"))
    with nc.Block() as block:
        @block.gpsimd
        def _(pool):
            pool.memset(c.ident[:], 0.0).then_inc(built, 1)
            pool.memset(c.flip[:], 0.0).then_inc(built, 1)
            pool.memset(c.causal[:], 0.0).then_inc(built, 1)
            pool.memset(c.headmask[:], 1.0).then_inc(built, 1)
            pool.memset(c.groupmask[:], 1.0).then_inc(built, 1)
            pool.memset(c.onesrow[:], 1.0).then_inc(built, 1)
            pool.memset(c.eps[:], EPS).then_inc(built, 1)
            pool.memset(c.minushalf[:], -0.5).then_inc(built, 1)
            pool.wait_ge(built, 8)
            pool.affine_select(out=c.ident[:], in_=c.ident[:], compare_op=ALU.not_equal, fill=1.0,
                               base=0, pattern=[[-1, P]], channel_multiplier=1).then_inc(built, 1)
            pool.affine_select(out=c.flip[:], in_=c.flip[:], compare_op=ALU.not_equal, fill=1.0,
                               base=1 - P, pattern=[[1, P]], channel_multiplier=1).then_inc(built, 1)
            pool.affine_select(out=c.causal[:], in_=c.causal[:], compare_op=ALU.is_ge, fill=-1.0,
                               base=0, pattern=[[-1, P]], channel_multiplier=1).then_inc(built, 1)
            pool.affine_select(out=c.headmask[:], in_=c.headmask[:], compare_op=ALU.is_ge, fill=0.0,
                               base=0, pattern=[[-HD, H]], channel_multiplier=1).then_inc(built, 1)
            pool.affine_select(out=c.groupmask[:], in_=c.groupmask[:], compare_op=ALU.is_ge, fill=0.0,
                               base=0, pattern=[[-32, QH]], channel_multiplier=1).then_inc(built, 1)
            pool.wait_ge(built, 13)
            pool.affine_select(out=c.headmask[:], in_=c.headmask[:], compare_op=ALU.is_ge, fill=0.0,
                               base=HD - 1, pattern=[[HD, H]], channel_multiplier=-1).then_inc(built, 1)
            pool.affine_select(out=c.groupmask[:], in_=c.groupmask[:], compare_op=ALU.is_ge, fill=0.0,
                               base=31, pattern=[[32, QH]], channel_multiplier=-1).then_inc(built, 1)

        @block.vector
        def _(dve):
            dve.wait_ge(built, 15)
            dve.tensor_scalar(c.identbig[:], c.ident[:], BIG, None, ALU.mult).then_inc(vbuilt, 1)
    return c


def attention(nc, name, c, x, kv, out, wq, bq, wk, bk, wv, bv, wo, bo, *,
              transposed, mask=None, causal=False, topk=0, gates=None, rel_bias=None, bias_rows=None,
              scrambled=False):
    NB = x.shape[0]
    ROUNDS = topk // 8
    halved = scrambled
    add_on_pe = topk > 0
    scale = float(HD) ** -0.5
    with ExitStack() as ctx:
        def sb(nm, shape, dt=F32):
            return ctx.enter_context(nc.sbuf_tensor(f"{name}_{nm}", shape, dt))

        sems = []

        def sem(nm):
            sems.append(ctx.enter_context(nc.semaphore(f"{name}_{nm}")))
            return sems[-1]

        w_raw = sb("w_raw", [P, 4, P])
        w_t = sb("w_t", [P, 4, P]) if transposed else w_raw
        Wq, Wk, Wv, Wo = (w_t[:, n, :] for n in range(4))
        bcol = sb("bcol", [P, 4])
        bq_s = sb("bq_s", [P, 1])
        bv_g = sb("bv_g", [P, 1])
        bo_pad = sb("bo_pad", [P, P])
        x_tok = sb("x_tok", [P, 2, P])
        kv_tok = sb("kv_tok", [P, 2, P]) if kv is not None else None
        x_res = sb("x_res", [P, 2, P])
        xkT = sb("xkT", [P, 2, P])
        q_t = sb("q_t", [P, 2, P])
        k_t = sb("k_t", [P, P])
        k_bd = sb("k_bd", [P, 2, H, P])
        v_pad = sb("v_pad", [P, 2, H, 32])
        p_sb = sb("p", [P, NQ, QH, P])
        pT = sb("pT", [P, 2, QH, P])
        neg_max = sb("neg_max", [P, NQ, QH])
        o_raw = sb("o_raw", [P, NQ, P])
        r_sum = sb("r_sum", [P, H])
        o_n = sb("o_n", [P, P])
        oT = sb("oT", [P, P])
        stats = sb("stats", [P, 6])
        mv = sb("mv", [P, 2])
        var_eps = sb("var_eps", [P, 1])
        rstd = sb("rstd", [P, 1])
        x_bo = sb("x_bo", [P, P])
        x_sum = sb("x_sum", [P, P])
        x_new = sb("x_new", [P, 2, P])
        if topk:
            s_sb = sb("s", [P, NQ, QH, P])
            work = sb("work", [P, QH, P] if halved else [P, NQ, QH, P])
            top8 = sb("top8", [P, QH, 8] if halved else [P, NQ, QH, ROUNDS, 8])
            keep = sb("keep", [P, QH, P])
        if halved:
            HALF = P // 2
            BEST = HALF // 2
            s_neg = sb("s_neg", [P, NQ, QH, HALF])
            pairs = sb("pairs", [P, 2, QH, HALF])
            best = sb("best", [P, 2, QH, BEST])
            cut = sb("cut", [P, 2, QH, BEST])
            edge = sb("edge", [P, NQ, 2, QH])
            tied = sb("tied", [P, QH])
            tie_count = sb("tie_count", [1, 1], mybir.dt.int32)
        if rel_bias is not None:
            bias_sb = sb("bias_sb", [P, H, P])
            R = rel_bias.shape[0]
            LO = (R + 1) // 2
            table = sb("table", [R, H])
            rows_sb = sb("rows", [H, 2 * LO + R])
        if mask is not None:
            m_raw = sb("m_raw", [P, 2, P], mybir.dt.uint8)
            m_add = sb("m_add", [P, 2, P], BF16)
        if scrambled:
            pick = sb("pick", [P, H, 32])
            lin = sb("lin", [P, 3, P])
            q32 = sb("q32", [P, 2, NQ, P])
            k32 = sb("k32", [P, NQ, P])
            v32 = sb("v32", [P, NQ, P])
            rowmask = sb("rowmask", [P, H])
            place = sb("place", [P, 4, 32])
            o_x = sb("o_x", [P, H, H, HD])
            o_tok = sb("o_tok", [P, P])

        S = c.banks[0:2]
        PT = c.banks[2:4]
        PROJ = c.banks[4]
        O = c.banks[5]
        OT = c.banks[6]
        TIES = slice(HD + 8, HD + 8 + QH)
        Y = c.banks[7]

        weights_in = sem("weights_in")
        tok_in = [sem("tok_in0"), sem("tok_in1")]
        res_in = [sem("res_in0"), sem("res_in1")]
        stored = [sem("stored0"), sem("stored1")]
        set_pool = sem("set_pool")
        set_pe = sem("set_pe")
        set_act = sem("set_act")
        set_dve = sem("set_dve")
        if rel_bias is not None:
            table_in = sem("table_in")
            table_turned = sem("table_turned")
            rows_ready = sem("rows_ready")
            rows_out = sem("rows_out")
            bias_in = sem("bias_in")
        tr_done = sem("tr_done")
        proj_done = sem("proj_done")
        s_done = sem("s_done")
        pt_done = sem("pt_done")
        pv_done = sem("pv_done")
        ot_done = sem("ot_done")
        ont_done = sem("ont_done")
        y_done = sem("y_done")
        xkT_ready = sem("xkT_ready")
        qk_ready = sem("qk_ready")
        v_ready = sem("v_ready")
        s_copied = sem("s_copied")
        exp_done = sem("exp_done")
        pT_ready = sem("pT_ready")
        o_copied = sem("o_copied")
        oT_ready = sem("oT_ready")
        chain = sem("chain")
        quad_begun = sem("quad_begun")
        max_ready = sem("max_ready")
        top_ready = sem("top_ready")
        on_ready = sem("on_ready")
        stats_ready = sem("stats_ready")
        x_ready = sem("x_ready")
        m_ready = sem("m_ready")
        if halved:
            tied_ready = sem("tied_ready")
            ties_counted = sem("ties_counted")
            ties_read = sem("ties_read")
            ties_seen = sem("ties_seen")
            redone = sem("redone")
        kbd_ready = sem("kbd_ready")
        p_ready = sem("p_ready")
        keep_ready = sem("keep_ready")
        step_begun = sem("step_begun")
        var_ready = sem("var_ready")
        rstd_ready = sem("rstd_ready")
        x_bo_ready = sem("x_bo_ready")
        if scrambled:
            pick_done = sem("pick_done")
            picked = sem("picked")
            ox_ready = sem("ox_ready")
            r_done = sem("r_done")
            otok_ready = sem("otok_ready")

        n_weight_dmas = 4 + 4 + (1 if gates is not None else 0)
        tok_dmas = 1 + (kv is not None) + (mask is not None)
        n_set_act = 1 + (gates is not None) + transposed

        def scored_at(t, q):
            if not halved:
                return t, q
            return (t, q + 1) if q < NQ - 1 else (t.plus(1), 0)

        with nc.Block() as block:
            @block.sync
            def _(sp):
                if rel_bias is not None:
                    sp.dma_start(table[:], rel_bias).then_inc(table_in, 16)
                for n, w in enumerate((wq, wk, wv, wo)):
                    sp.dma_start(w_raw[:, n, :], w).then_inc(weights_in, 16)
                for n, b in enumerate((bq, bk, bv)):
                    sp.dma_start(bcol[:, n:n + 1], b.rearrange("(p a) -> p a", a=1)).then_inc(weights_in, 16)
                if gates is not None:
                    sp.dma_start(bcol[:, 3:4], bcast(gates, 1, HD).unsqueeze(2)).then_inc(weights_in, 16)
                if add_on_pe:
                    sp.wait_ge(set_pool, 1)
                    sp.dma_start(bo_pad[0:1, :], bo.rearrange("(a n) -> a n", a=1)).then_inc(weights_in, 16)
                else:
                    sp.dma_start(bo_pad[:], bo.rearrange("(a n) -> a n", a=1).to_broadcast([P, P])).then_inc(weights_in, 16)
                if rel_bias is not None:
                    sp.wait_ge(rows_ready, 3)
                    sp.dma_start(bias_rows, rows_sb[:]).then_inc(rows_out, 16)
                    sp.wait_ge(rows_out, 16)
                    rows = bass.AP(bias_rows.tensor, 0, [[1, P], [bias_rows.shape[1], H], [1, P]])
                    sp.dma_start(bias_sb[:], rows).then_inc(bias_in, 16)

                def slot(t):
                    load = t.plus(2)
                    if load.within(NB):
                        wait(sp, tr_done, t, 1, 1)
                        if mask is not None:
                            wait(sp, m_ready, t, 1, 1)
                        sp.dma_start(x_tok[:, t.par, :], x[load.index]).then_inc(tok_in[t.par], 16)
                        if kv is not None:
                            sp.dma_start(kv_tok[:, t.par, :], kv[load.index]).then_inc(tok_in[t.par], 16)
                        if mask is not None:
                            sp.dma_start(m_raw[:, t.par, :], mask[load.index]).then_inc(tok_in[t.par], 16)
                    if t.within(NB):
                        wait(sp, y_done if add_on_pe else x_bo_ready, t.plus(-2), 1, 1)
                        sp.dma_start(x_res[:, t.par, :], x[t.index]).then_inc(res_in[t.par], 16)
                    done = t.plus(-2)
                    if done.within(NB):
                        wait(sp, x_ready, done, 1, 1)
                        sp.dma_start(out[done.index], x_new[:, t.par, :]).then_inc(stored[t.par], 16)

                slots(sp, slot, NB)
                for par in range(2):
                    sp.wait_ge(stored[par], 16 * (NB // 2))

            @block.gpsimd
            def _(pool):
                if add_on_pe:
                    pool.memset(bo_pad[:], 0.0).then_inc(set_pool, 1)
                else:
                    pool.wait_ge(weights_in, 16 * n_weight_dmas)
                    pool.sem_inc(set_pool, 1)
                pool.memset(v_pad[:], 0.0).then_inc(set_pool, 1)
                pool.wait_ge(set_pool, 2)
                pool.memset(v_pad[:, :, :, HD:HD + 1], 1.0).then_inc(set_pool, 1)
                if scrambled:
                    pool.memset(pick[:], 0.0).then_inc(set_pool, 1)
                    pool.memset(place[:], 0.0).then_inc(set_pool, 1)

                def keep_top(t, q):
                    b, j = (t, q - 1) if q else (t.plus(-1), NQ - 1)
                    if topk and b.within(NB):
                        wait(pool, top_ready, b, NQ, j + 1)
                        p, n = (b, j - 1) if j else (b.plus(-1), NQ - 1)
                        wait(pool, p_ready, p, NQ, n + 1)
                        pool.sem_inc(step_begun, 1)
                        for h in range(QH):
                            least = edge[:, j, 0, h:h + 1] if halved else top8[:, j, h, ROUNDS - 1, 7:8]
                            op = pool.tensor_scalar(keep[:, h, :], s_sb[:, j, h, :], least, None, ALU.is_ge)
                        op.then_inc(keep_ready, 1)
                        wait(pool, exp_done, b, NQ, j + 1)
                        wait(pool, keep_ready, b, NQ, j + 1)
                        op = pool.tensor_tensor(p_sb[:, j, :, :], p_sb[:, j, :, :], keep[:], ALU.mult)
                        op.then_inc(p_ready, 1)

                def slot(t):
                    for q in range(NQ):
                        if not halved:
                            keep_top(t, q)
                        b = t.plus(-2)
                        if q == 1 and not add_on_pe and b.within(NB):
                            wait_par(pool, res_in, b, 16)
                            wait(pool, stats_ready, b.plus(-1), 1, 1)
                            pool.tensor_tensor(x_bo[:], x_res[:, b.par, :], bo_pad[:], ALU.add)\
                                .then_inc(x_bo_ready, 1)
                        if scrambled and q == 0 and b.within(NB):
                            wait(pool, on_ready, b, 1, 1)
                            wait(pool, r_done, b.plus(-1), 1, 1)
                            pool.tensor_tensor(
                                o_x[:], bcast(o_n[:].rearrange("p (h d) -> p h d", h=H), 2, H),
                                bcast(bcast(rowmask[:], 1, H), 3, HD), ALU.mult).then_inc(ox_ready, 1)
                        if halved:
                            keep_top(t, q)
                        b = t.plus(1)
                        if q >= 2 and b.within(NB):
                            if q == 2:
                                if scrambled:
                                    wait(pool, picked, b, 3, 2)
                                else:
                                    wait(pool, qk_ready, b, 2, 2)
                            for j in (0, 1) if q == 2 else (2, 3):
                                if scrambled:
                                    kk, mm = k32[:, j, :], c.groupmask[:]
                                else:
                                    kk, mm = k_t[:], c.headmask[:, QH * j:QH * j + QH]
                                pool.tensor_tensor(k_bd[:, b.par, QH * j:QH * j + QH, :], bcast(kk, 1, QH),
                                                   bcast(mm, 2, P), ALU.mult).then_inc(kbd_ready, 1)
                        b = t.plus(-2)
                        if q == 2 and b.within(NB):
                            wait(pool, stats_ready, b, 1, 1)
                            pool.tensor_tensor(var_eps[:], mv[:, 1:2], c.eps[:], ALU.add).then_inc(var_ready, 1)
                            wait(pool, var_ready, b, 1, 1)
                            pool.tensor_tensor(rstd[:], var_eps[:], c.minushalf[:], ALU.pow)\
                                .then_inc(rstd_ready, 1)

                slots(pool, slot, NB)

            @block.tensor
            def _(pe):
                if rel_bias is not None:
                    pe.wait_ge(table_in, 16)
                    pe.transpose(Y[0:H, 0:R], table[:], c.ident[0:R, 0:R]).then_inc(table_turned, 1)
                pe.wait_ge(weights_in, 16 * n_weight_dmas)
                if transposed:
                    for n in range(4):
                        mm = pe.transpose(PROJ[:, P * n:P * n + P], w_raw[:, n, :], c.ident[:])
                    mm.then_inc(set_pe, 1)
                pe.wait_ge(set_act, n_set_act)
                pe.wait_ge(set_pool, 3)
                if scrambled:
                    pe.wait_ge(set_dve, 4)
                if rel_bias is not None:
                    pe.wait_ge(bias_in, 16)

                def transposes(b):
                    wait_par(pe, tok_in, b, 16 * tok_dmas)
                    wait(pe, v_ready, b.plus(-1), 1, 1)
                    mm = pe.transpose(PROJ[:, 0:P], x_tok[:, b.par, :], c.ident[:])
                    if kv is not None:
                        mm = pe.transpose(PROJ[:, P:2 * P], kv_tok[:, b.par, :], c.ident[:])
                    mm.then_inc(tr_done, 1)

                def project(b):
                    xT, kT = xkT[:, 0, :], xkT[:, 1 if kv is not None else 0, :]
                    wait(pe, xkT_ready, b, 1, 1)
                    pe.matmul(PROJ[:, 0:P], Wq, xT, start=True, stop=True)
                    pe.matmul(PROJ[:, P:2 * P], Wk, kT, start=True, stop=True)
                    if scrambled:
                        mm = pe.matmul(PROJ[:, 2 * P:3 * P], Wv, kT, start=True, stop=True)
                    else:
                        mm = pe.matmul(PROJ[:, 2 * P:3 * P], kT, Wv, start=True, stop=True)
                    mm.then_inc(proj_done, 1)

                def pick_heads(b, n):
                    src = lin[:, n, :].rearrange("p (j g t) -> p g j t", j=NQ, g=QH)
                    dst = PROJ[:].rearrange("p (j t r) -> p j t r", j=NQ, r=H)
                    if n == 0:
                        wait(pe, qk_ready, b, 3, 3)
                    else:
                        wait(pe, picked, b, 3, n)
                    for r in range(H):
                        for g in range(QH):
                            mm = pe.matmul(dst[32 * g:32 * g + 32, :, :, r], pick[:, r, :], src[:, g],
                                           start=True, stop=True)
                    mm.then_inc(pick_done, 1)

                def transpose_v(b):
                    wait(pe, picked, b, 3, 3)
                    for j in range(NQ):
                        mm = pe.transpose(PROJ[:, P * j:P * j + P], v32[:, j, :], c.ident[:])
                    mm.then_inc(pick_done, 1)

                def scores(b, j):
                    wait(pe, kbd_ready, b, NQ, j + 1)
                    if mask is not None and j == 0:
                        wait(pe, m_ready, b, 1, 1)
                    p, n = (b, j - 2) if j >= 2 else (b.plus(-1), j + 2)
                    wait(pe, s_copied if topk else exp_done, p, NQ, n + 1)
                    lhs = q32[:, b.par, j, :] if scrambled else q_t[:, b.par, :]
                    dst = S[j % 2][:]
                    added = mask is not None or causal or rel_bias is not None
                    mm = pe.matmul(dst, lhs, k_bd[:, b.par, QH * j:QH * j + QH, :], start=True, stop=not added)
                    if mask is not None:
                        mm = pe.matmul(dst, c.identbig[:], bcast(m_add[:, b.par, :], 1, QH), start=False, stop=True)
                    elif causal:
                        mm = pe.matmul(dst, c.identbig[:], bcast(c.causal[:], 1, QH), start=False, stop=True)
                    elif rel_bias is not None:
                        mm = pe.matmul(dst, c.flip[:], bias_sb[:, QH * j:QH * j + QH, :], start=False, stop=True)
                    mm.then_inc(s_done, 1)

                def count_ties(b, j):
                    wait(pe, tied_ready, b, NQ, j + 1)
                    if j == NQ - 1:
                        wait(pe, on_ready, b.plus(-1), 1, 1)
                    pe.matmul(OT[0:1, TIES], c.onesrow[:, 0:1], tied[:], start=True, stop=True)\
                        .then_inc(ties_counted, 1)

                def transpose_p(b, j):
                    wait(pe, p_ready if topk else exp_done, b, NQ, j + 1)
                    p, n = (b, j - 2) if j >= 2 else (b.plus(-1), j + 2)
                    wait(pe, pT_ready, p, NQ, n + 1)
                    for h in range(QH):
                        mm = pe.transpose(PT[j % 2][:, P * h:P * h + P], p_sb[:, j, h, :], c.ident[:])
                    mm.then_inc(pt_done, 1)

                def weigh_v(b, j):
                    wait(pe, pT_ready, b, NQ, j + 1)
                    if j == 0:
                        wait(pe, v_ready, b, 1, 1)
                        wait(pe, o_copied, b.plus(-1), 1, 1)
                    for g in range(QH):
                        mm = pe.matmul(O[32 * g:32 * g + 32, P * j:P * j + P], v_pad[:, b.par, QH * j + g, :],
                                       pT[:, j % 2, g, :], start=True, stop=True)
                    mm.then_inc(pv_done, 1)

                def transpose_o(b, last_quad):
                    wait(pe, o_copied, b, 1, 1)
                    if halved:
                        wait(pe, ties_read, last_quad[0], NQ, last_quad[1] + 1)
                    wait(pe, on_ready, b.plus(-1), 1, 1)
                    for j in range(NQ):
                        mm = pe.transpose(OT[:, P * j:P * j + P], o_raw[:, j, :], c.ident[:])
                    mm.then_inc(ot_done, 1)

                def unscramble(b):
                    wait(pe, ox_ready, b, 1, 1)
                    wait(pe, x_ready, b.plus(-1), 1, 1)
                    for hh in range(4):
                        for j in range(NQ):
                            mm = pe.matmul(Y[32 * j:32 * j + 32, 0:P], place[:, hh, :],
                                           o_x[:, 4 * j + hh, :, :], start=(hh == 0), stop=(hh == 3),
                                           skip_group_check=True)
                    mm.then_inc(r_done, 1)

                def transpose_on(b):
                    if scrambled:
                        wait(pe, otok_ready, b, 1, 1)
                    else:
                        wait(pe, on_ready, b, 1, 1)
                        wait(pe, x_ready, b.plus(-1), 1, 1)
                    pe.transpose(Y[:, 0:P], (o_tok if scrambled else o_n)[:], c.ident[:]).then_inc(ont_done, 1)

                def project_out(b):
                    wait(pe, oT_ready, b, 1, 1)
                    if not add_on_pe:
                        pe.matmul(Y[:, 0:P], oT[:], Wo, start=True, stop=True).then_inc(y_done, 1)
                        return
                    wait_par(pe, res_in, b, 16)
                    pe.matmul(Y[:, 0:P], oT[:], Wo, start=True, stop=False)
                    pe.matmul(Y[:, 0:P], c.onesrow[:], bo_pad[:], start=False, stop=False)
                    pe.matmul(Y[:, 0:P], c.ident[:], x_res[:, b.par, :], start=False, stop=True)\
                        .then_inc(y_done, 1)

                def slot(t):
                    ahead, prev, prev2 = t.plus(1), t.plus(-1), t.plus(-2)
                    for q in range(NQ):
                        if q == 0 and ahead.within(NB):
                            transposes(ahead)
                        b, j = scored_at(t, q)
                        if q < NQ - 1 and b.within(NB):
                            scores(b, j)
                        d, n = (t, q - 1) if q else (prev, NQ - 1)
                        if halved and d.within(NB):
                            count_ties(d, n)
                        if q == NQ - 1 and b.within(NB):
                            scores(b, j)
                        b, j = (t, q - 2) if q >= 2 else (prev, q + 2)
                        if b.within(NB):
                            transpose_p(b, j)
                        b, j = (t, q - 3) if q >= 3 else (prev, q + 1)
                        if b.within(NB):
                            weigh_v(b, j)
                        if q == 0 and prev2.within(NB) and not scrambled:
                            transpose_on(prev2)
                        if q == 1 and prev2.within(NB):
                            if scrambled:
                                unscramble(prev2)
                                transpose_on(prev2)
                            project_out(prev2)
                        if q == 1 and ahead.within(NB):
                            project(ahead)
                            if scrambled:
                                pick_heads(ahead, 0)
                        if scrambled and q == 2 and ahead.within(NB):
                            pick_heads(ahead, 1)
                        if scrambled and q == 3 and ahead.within(NB):
                            pick_heads(ahead, 2)
                            transpose_v(ahead)
                        if q == 3 and prev.within(NB):
                            transpose_o(prev, (t, q - 1) if t.within(NB) else (prev, NQ - 1))

                slots(pe, slot, NB)

            @block.scalar
            def _(act):
                act.wait_ge(weights_in, 16 * n_weight_dmas)
                act.mul(bq_s[:], bcol[:, 0:1], scale).then_inc(set_act, 1)
                if gates is not None:
                    act.activation(bv_g[:], bcol[:, 2:3], ACT.Identity, scale=bcol[:, 3:4]).then_inc(set_act, 1)
                if transposed:
                    act.wait_ge(set_pe, 1)
                    act.activation(w_t[:].rearrange("p a b -> p (a b)"), PROJ[:], ACT.Copy).then_inc(set_act, 1)

                def v_by_head(ahead):
                    src = PROJ[:, 2 * P:3 * P].rearrange("p (h d) -> p h d", h=H)
                    if scrambled:
                        wait(act, pick_done, ahead, 4, 3)
                        act.activation(v32[:], PROJ[:], ACT.Copy).then_inc(picked, 1)
                        wait(act, pick_done, ahead, 4, 4)
                        src = PROJ[:].rearrange("p (h d) -> p h d", h=H)[:, :, 0:HD]
                    wait(act, pv_done, ahead.plus(-2), NQ, NQ)
                    act.activation(v_pad[:, ahead.par, :, 0:HD], src, ACT.Copy).then_inc(v_ready, 1)

                def exponentials(t, q):
                    if topk:
                        b, j = (t, q - 1) if q else (t.plus(-1), NQ - 1)
                    else:
                        b, j = t, q
                    if b.within(NB):
                        wait(act, top_ready if halved else max_ready, b, NQ, j + 1)
                        for h in range(QH):
                            src = s_sb[:, j, h, :] if topk else S[j % 2][:, P * h:P * h + P]
                            op = act.activation(p_sb[:, j, h, :], src, ACT.Exp, bias=neg_max[:, j, h:h + 1])
                        op.then_inc(exp_done, 1)

                def slot(t):
                    ahead, prev, prev2 = t.plus(1), t.plus(-1), t.plus(-2)
                    for q in range(NQ):
                        if q == 0 and ahead.within(NB):
                            n = 2 if kv is not None else 1
                            wait(act, tr_done, ahead, 1, 1)
                            act.activation(xkT[:, 0:n, :], PROJ[:, 0:n * P], ACT.Copy).then_inc(xkT_ready, 1)
                        b, j = scored_at(t, q)
                        if topk and b.within(NB):
                            wait(act, s_done, b, NQ, j + 1)
                            if halved:
                                act.activation(s_neg[:, j, :, :],
                                               S[j % 2][:].rearrange("p (h k) -> p h k", h=QH)[:, :, HALF:],
                                               ACT.Copy, scale=-1.0)
                            act.activation(s_sb[:, j, :, :], S[j % 2][:], ACT.Copy).then_inc(s_copied, 1)
                        if q == 3 and ahead.within(NB) and not scrambled:
                            v_by_head(ahead)
                        if not halved:
                            exponentials(t, q)
                        b, j = (t, q - 2) if q >= 2 else (prev, q + 2)
                        if topk and b.within(NB):
                            wait(act, pt_done, b, NQ, j + 1)
                            p, n = (b, j - 2) if j >= 2 else (b.plus(-1), j + 2)
                            wait(act, pv_done, p, NQ, n + 1)
                            act.activation(pT[:, j % 2, :, :], PT[j % 2][:], ACT.Copy).then_inc(pT_ready, 1)
                        if q == 1 and scrambled and prev2.within(NB):
                            wait(act, r_done, prev2, 1, 1)
                            act.activation(o_tok[:], Y[:, 0:P], ACT.Copy).then_inc(otok_ready, 1)
                        if q == (1 if scrambled else 0) and prev2.within(NB):
                            wait(act, ont_done, prev2, 1, 1)
                            if scrambled:
                                op = act.activation(oT[:], Y[:, 0:P], ACT.Copy)
                            elif gates is not None:
                                op = act.activation(oT[:], Y[:, 0:P], ACT.Identity, bias=bv_g[:], scale=bcol[:, 3:4])
                            else:
                                op = act.activation(oT[:], Y[:, 0:P], ACT.Identity, bias=bcol[:, 2:3])
                            op.then_inc(oT_ready, 1)
                        if halved:
                            exponentials(t, q)
                        if q == 1 and ahead.within(NB):
                            wait(act, proj_done, ahead, 1, 1)
                            if scrambled:
                                act.activation(lin[:, 0, :], PROJ[:, 0:P], ACT.Identity, bias=bq_s[:], scale=scale)\
                                    .then_inc(qk_ready, 1)
                                for n in (1, 2):
                                    act.activation(lin[:, n, :], PROJ[:, P * n:P * n + P], ACT.Identity,
                                                   bias=bcol[:, n:n + 1]).then_inc(qk_ready, 1)
                                wait(act, pick_done, ahead, 4, 1)
                                act.activation(q32[:, ahead.par, :, :], PROJ[:], ACT.Copy).then_inc(picked, 1)
                            else:
                                act.activation(q_t[:, ahead.par, :], PROJ[:, 0:P], ACT.Identity,
                                               bias=bq_s[:], scale=scale).then_inc(qk_ready, 1)
                                wait(act, kbd_ready, t, NQ, NQ)
                                act.activation(k_t[:], PROJ[:, P:2 * P], ACT.Identity, bias=bcol[:, 1:2])\
                                    .then_inc(qk_ready, 1)
                        if q == 2 and scrambled and ahead.within(NB):
                            wait(act, pick_done, ahead, 4, 2)
                            wait(act, kbd_ready, t, NQ, NQ)
                            act.activation(k32[:], PROJ[:], ACT.Copy).then_inc(picked, 1)
                        if q == 2 and prev.within(NB):
                            wait(act, pv_done, prev, NQ, NQ)
                            wait(act, ot_done, prev2, 1, 1)
                            act.activation(o_raw[:], O[:], ACT.Copy).then_inc(o_copied, 1)
                        if q == 3 and ahead.within(NB) and scrambled:
                            v_by_head(ahead)

                act.wait_ge(set_act, n_set_act)
                act.wait_ge(set_pool, 3)
                slots(act, slot, NB)

            @block.vector
            def _(dve):
                steps = [0]

                def own(ins):
                    ins.then_inc(chain, 1)
                    steps[0] += 1
                    return steps[0]

                if scrambled:
                    dve.wait_ge(set_pool, 5)
                    dve.tensor_copy(pick[:, :, 0:HD], c.ident[:].rearrange("p (r d) -> p r d", r=H)).then_inc(set_dve, 1)
                    dve.tensor_reduce(rowmask[:], c.ident[:].rearrange("p (t r) -> p r t", t=HD), AX.X, ALU.add)\
                        .then_inc(set_dve, 1)
                    for hh in range(4):
                        op = dve.tensor_reduce(place[:, hh, HD * hh:HD * hh + HD],
                                               c.ident[:].rearrange("p (t r) -> p t r", t=HD), AX.X, ALU.add)
                        if hh >= 2:
                            op.then_inc(set_dve, 1)

                if rel_bias is not None:
                    dve.wait_ge(table_turned, 1)
                    dve.tensor_copy(rows_sb[:, 0:LO], Y[0:H, R - LO:R]).then_inc(rows_ready, 1)
                    dve.tensor_copy(rows_sb[:, LO:LO + R], Y[0:H, 0:R]).then_inc(rows_ready, 1)
                    dve.tensor_copy(rows_sb[:, LO + R:], Y[0:H, R - 1:R].to_broadcast([H, LO])).then_inc(rows_ready, 1)

                def top_k(b, j):
                    wait(dve, s_copied, b, NQ, j + 1)
                    dve.sem_inc(quad_begun, 1)
                    replaced = [0] * QH
                    for r in range(ROUNDS):
                        found = []
                        for h in range(QH):
                            src = work if r else s_sb
                            if r:
                                dve.wait_ge(chain, replaced[h])
                            op = dve.max(top8[:, j, h, r, :], src[:, j, h, :])
                            if r == ROUNDS - 1 and h == QH - 1:
                                op.then_inc(top_ready, 1)
                            else:
                                found.append(own(op))
                        if r == ROUNDS - 1:
                            break
                        for h in range(QH):
                            dve.wait_ge(chain, found[h])
                            op = dve.match_replace(out=work[:, j, h, :], in_to_replace=top8[:, j, h, r, :],
                                                   in_values=(work if r else s_sb)[:, j, h, :], imm_value=TAKEN)
                            replaced[h] = own(op)
                        if r == 0:
                            dve.tensor_scalar(neg_max[:, j, :], top8[:, j, :, 0, 0], -1.0, None, ALU.mult)\
                                .then_inc(max_ready, 1)

                def normalise(b):
                    wait(dve, ot_done, b, 1, 1)
                    o4 = OT[:].rearrange("p (h e) -> p h e", h=H)
                    n = own(dve.reciprocal(r_sum[:], o4[:, :, HD]))
                    dve.wait_ge(chain, n)
                    dve.tensor_tensor(o_n[:].rearrange("p (h d) -> p h d", h=H), o4[:, :, 0:HD],
                                      bcast(r_sum[:], 2, HD), ALU.mult).then_inc(on_ready, 1)

                def layer_norm(t, q):
                    b = t.plus(-2)
                    if q == 2 and b.within(NB):
                        wait(dve, y_done, b, 1, 1)
                        if not add_on_pe:
                            wait(dve, x_bo_ready, b, 1, 1)
                            n = own(dve.tensor_tensor(x_sum[:], Y[:, 0:P], x_bo[:], ALU.add))
                            dve.wait_ge(chain, n)
                        n = own(dve.bn_stats(stats[:], Y[:, 0:P] if add_on_pe else x_sum[:]))
                        dve.wait_ge(chain, n)
                        dve.bn_aggr(mv[:], stats[:]).then_inc(stats_ready, 1)
                    if q == 3 and b.within(NB):
                        wait_par(dve, stored, t.plus(-4), 16)
                        wait(dve, rstd_ready, b, 1, 1)
                        dve.tensor_scalar(x_new[:, t.par, :], Y[:, 0:P] if add_on_pe else x_sum[:], mv[:, 0:1], rstd[:, 0:1],
                                          ALU.subtract, ALU.mult).then_inc(x_ready, 1)

                def halve(b, j, last):
                    wait(dve, s_copied, b, NQ, j + 1)
                    dve.sem_inc(quad_begun, 1)
                    first, second = s_sb[:, j, :, 0:HALF], s_sb[:, j, :, HALF:]
                    lo = own(dve.tensor_tensor(pairs[:, 0, :, :], first, second, ALU.min))
                    hi = own(dve.scalar_tensor_tensor(out=pairs[:, 1, :, :], in0=first, scalar=-1.0,
                                                      in1=s_neg[:, j, :, :], op0=ALU.mult, op1=ALU.min))
                    chains = [(x, h) for x in range(2) for h in range(QH)]
                    replaced = {(x, h): hi if x else lo for x, h in chains}
                    for r in range(BEST // 8):
                        found = {}
                        for x, h in chains:
                            dve.wait_ge(chain, replaced[x, h])
                            found[x, h] = own(dve.max(best[:, x, h, 8 * r:8 * r + 8], pairs[:, x, h, :]))
                        if r == 0:
                            dve.wait_ge(chain, hi)
                            neg = own(dve.tensor_reduce(neg_max[:, j, :], pairs[:, 1, :, :], AX.X, ALU.min))
                            dve.wait_ge(chain, neg)
                        if r < BEST // 8 - 1:
                            for x, h in chains:
                                dve.wait_ge(chain, found[x, h])
                                replaced[x, h] = own(dve.match_replace(
                                    out=pairs[:, x, h, :], in_to_replace=best[:, x, h, 8 * r:8 * r + 8],
                                    in_values=pairs[:, x, h, :], imm_value=TAKEN))
                        if r == 0 and last is not None:
                            read_ties(*last)
                        if r == 1 and last is not None:
                            settle_ties(*last)
                        if r == 2:
                            layer_norm(b, j)
                    dve.wait_ge(chain, found[chains[-1]])
                    n = own(dve.scalar_tensor_tensor(out=cut[:], in0=best[:, ::-1, :, :], scalar=-1.0, in1=best[:],
                                                     op0=ALU.mult, op1=ALU.max))
                    dve.wait_ge(chain, n)
                    n = own(dve.tensor_reduce(edge[:, j, :, :], cut[:], AX.X, ALU.min))
                    dve.wait_ge(chain, n)
                    dve.scalar_tensor_tensor(out=tied[:], in0=edge[:, j, 1, :], scalar=-1.0, in1=edge[:, j, 0, :],
                                             op0=ALU.mult, op1=ALU.is_equal).then_inc(tied_ready, 1)

                def read_ties(b, j):
                    wait(dve, ties_counted, b, NQ, j + 1)
                    dve.tensor_reduce(tie_count[:], OT[0:1, TIES], AX.X, ALU.max).then_inc(ties_read, 1)

                def settle_ties(b, j):
                    wait(dve, ties_read, b, NQ, j + 1)
                    dve.sem_inc(ties_seen, 1)
                    ties = dve.value_load(tie_count[:])
                    with dve.If(ties > 0):
                        steps_done = 0
                        for r in range(ROUNDS):
                            for h in range(QH):
                                dve.max(top8[:, h, :], (work[:, h, :] if r else s_sb[:, j, h, :])).then_inc(redone, 1)
                            steps_done += QH
                            dve.wait_ge(redone, steps_done)
                            for h in range(QH):
                                dve.match_replace(out=work[:, h, :], in_to_replace=top8[:, h, :],
                                                  in_values=(work[:, h, :] if r else s_sb[:, j, h, :]),
                                                  imm_value=TAKEN).then_inc(redone, 1)
                            steps_done += QH
                            dve.wait_ge(redone, steps_done)
                        dve.tensor_scalar(work[:], work[:], 0.5 * TAKEN, TAKEN, ALU.is_ge, ALU.mult).then_inc(redone, 1)
                        dve.wait_ge(redone, steps_done + 1)
                        dve.tensor_tensor(s_sb[:, j, :, :], s_sb[:, j, :, :], work[:], ALU.add).then_inc(redone, 1)
                        dve.wait_ge(redone, steps_done + 2)
                        dve.sem_clear(redone)
                    dve.sem_inc(top_ready, 1)

                def slot(t):
                    prev, prev2 = t.plus(-1), t.plus(-2)
                    if steps[0]:
                        dve.wait_ge(chain, steps[0])
                        dve.sem_clear(chain)
                    steps[0] = 0
                    if mask is not None and t.plus(1).within(NB):
                        b = t.plus(1)
                        wait_par(dve, tok_in, b, 16 * tok_dmas)
                        wait(dve, s_done, prev, NQ, NQ)
                        dve.scalar_tensor_tensor(out=m_add[:, b.par, :], in0=m_raw[:, b.par, :], scalar=1.0,
                                                 in1=c.causal[:], op0=ALU.subtract, op1=ALU.min)\
                            .then_inc(m_ready, 1)
                    for q in range(NQ):
                        if q == 0 and prev2.within(NB):
                            normalise(prev2)
                        if not (halved and t.within(NB)):
                            layer_norm(t, q)
                        last = (t, q - 1) if q else (prev, NQ - 1)
                        if halved and t.within(NB):
                            halve(t, q, last if last[0].within(NB) else None)
                        elif halved and last[0].within(NB):
                            read_ties(*last)
                            settle_ties(*last)
                        elif t.within(NB) and topk:
                            top_k(t, q)
                        elif t.within(NB) and not topk:
                            wait(dve, s_done, t, NQ, q + 1)
                            dve.tensor_reduce(neg_max[:, q, :], S[q % 2][:].rearrange("p (h k) -> p h k", h=QH),
                                              AX.X, ALU.max, negate=True).then_inc(max_ready, 1)
                        b, j = (t, q - 2) if q >= 2 else (prev, q + 2)
                        if not topk and b.within(NB):
                            wait(dve, pt_done, b, NQ, j + 1)
                            p, n = (b, j - 2) if j >= 2 else (b.plus(-1), j + 2)
                            wait(dve, pv_done, p, NQ, n + 1)
                            dve.tensor_copy(pT[:, j % 2, :, :], PT[j % 2][:]).then_inc(pT_ready, 1)

                slots(dve, slot, NB)

        clear(nc, sems)


def experts(nc, name, c, x, out, router, wgate, wup, wdown, *, renormalise):
    NB = x.shape[0]
    TB = 4
    NT = NB // TB
    TW = TB * P
    E, _, F = wgate.shape
    NC = E * F // P
    PER = F // P if F % P == 0 else 1
    SPAN = P if F % P == 0 else F
    NW = NC // PER
    PARTS = 3
    with ExitStack() as ctx:
        def sb(nm, shape, dt=F32):
            return ctx.enter_context(nc.sbuf_tensor(f"{name}_{nm}", shape, dt))

        sems = []

        def sem(nm):
            sems.append(ctx.enter_context(nc.semaphore(f"{name}_{nm}")))
            return sems[-1]

        w_router = sb("w_router", [P, E])
        w_gate = sb("w_gate", [P, E, F])
        w_up = sb("w_up", [P, E, F])
        w_down = sb("w_down", [P, NC, P])
        x_all = sb("x_all", [P, NB, P])
        xT_all = sb("xT_all", [P, NT, TW])
        wT = sb("wT", [32 * PARTS, NT, TW], BF16)
        spread = sb("spread", [32 * PARTS, NW, P], BF16)

        x_in = [sem(f"x_in{u}") for u in range(NT)]
        w_in = sem("w_in")
        stored = [sem("stored0"), sem("stored1")]
        router_in = sem("router_in")

        gate_cols = w_gate[:].rearrange("p e f -> p (e f)")
        up_cols = w_up[:].rearrange("p e f -> p (e f)")

        with ExitStack() as rctx:
            def rsb(nm, shape, dt=F32):
                return rctx.enter_context(nc.sbuf_tensor(f"{name}_{nm}", shape, dt))

            logit = rsb("logit", [P, NB, E])
            prob = rsb("prob", [P, NB, E])
            order = rsb("order", [P, E])
            best = rsb("best", [P, 2, NB])
            hit = rsb("hit", [P, 2, NB, E])
            rank = rsb("rank", [P, NB, E])
            red = rsb("red", [P, NB])
            gap = rsb("gap", [P, NB])
            share = rsb("share", [P, 2, NB])
            weight = rsb("weight", [P, NB, E])
            part = rsb("part", [P, NB, PARTS, 32], BF16)
            identb = rsb("identb", [P, P], BF16)
            XT = c.banks[0:2]
            LG = c.banks[2]
            WT = [b[:].bitcast(BF16) for b in c.banks[3:7]]
            t_done = sem("t_done")
            t_copied = sem("t_copied")
            lg_done = sem("lg_done")
            shifted = sem("shifted")
            expd = sem("expd")
            gap_ready = sem("gap_ready")
            gap_expd = sem("gap_expd")
            step = sem("step")
            part_ready = sem("part_ready")
            wt_done = sem("wt_done")
            wt_copied = sem("wt_copied")
            base_set = sem("base_set")
            WB_PER = 1024 // P
            NWT = (NB + WB_PER - 1) // WB_PER

            with nc.Block() as block:
                @block.sync
                def _(sp):
                    with nc.allow_non_contiguous_dma("4 KB, once"):
                        sp.dma_start(w_router[:].unsqueeze(2), router.unsqueeze(2)).then_inc(router_in, 16)
                    for u in range(NT):
                        sp.dma_start(x_all[:, TB * u:TB * u + TB, :],
                                     x[TB * u:TB * u + TB].rearrange("b t d -> t b d")).then_inc(x_in[u], 16)
                    sp.dma_start(w_gate[:], wgate.rearrange("e d f -> d e f")).then_inc(w_in, 16)
                    sp.dma_start(w_up[:], wup.rearrange("e d f -> d e f")).then_inc(w_in, 16)
                    sp.dma_start(w_down[:], wdown.rearrange("e f d -> (e f) d").rearrange("(c p) d -> p c d", p=P))\
                        .then_inc(w_in, 16)

                @block.gpsimd
                def _(pool):
                    pool.memset(spread[:], 0.0).then_inc(base_set, 1)
                    pool.memset(part[:], 0.0).then_inc(base_set, 1)
                    pool.iota(order[:], pattern=[[-1, E]], base=E, channel_multiplier=0,
                              allow_small_or_imprecise_dtypes=True).then_inc(base_set, 1)
                    pool.wait_ge(base_set, 3)
                    first = spread[0:E]
                    pool.memset(first, 1.0).then_inc(base_set, 1)
                    pool.wait_ge(base_set, 4)
                    pool.affine_select(out=first, in_=first, compare_op=ALU.is_ge, fill=0.0,
                                       base=0, pattern=[[P, NW], [1, P]], channel_multiplier=-SPAN).then_inc(base_set, 1)
                    pool.wait_ge(base_set, 5)
                    pool.affine_select(out=first, in_=first, compare_op=ALU.is_ge, fill=0.0,
                                       base=SPAN - 1, pattern=[[-P, NW], [-1, P]], channel_multiplier=SPAN)\
                        .then_inc(base_set, 1)

                @block.tensor
                def _(pe):
                    for u in range(NT):
                        pe.wait_ge(x_in[u], 16)
                        if u >= 2:
                            pe.wait_ge(t_copied, u - 1)
                        for s in range(TB):
                            mm = pe.transpose(XT[u % 2][:, P * s:P * s + P], x_all[:, TB * u + s, :], c.ident[:])
                        mm.then_inc(t_done, 1)
                    pe.wait_ge(router_in, 16)
                    for b in range(NB):
                        if b % TB == 0:
                            pe.wait_ge(t_copied, b // TB + 1)
                        mm = pe.matmul(LG[:, E * b:E * b + E], xT_all[:, b // TB, P * (b % TB):P * (b % TB) + P],
                                       w_router[:], start=True, stop=True)
                    mm.then_inc(lg_done, 1)
                    pe.wait_ge(part_ready, PARTS)
                    for b in range(NB):
                        mm = pe.transpose(WT[b // WB_PER][0:32 * PARTS, P * (b % WB_PER):P * (b % WB_PER) + P],
                                          part[:, b, :, :].rearrange("p n e -> p (n e)"), identb[:])
                    mm.then_inc(wt_done, 1)

                @block.scalar
                def _(act):
                    for u in range(NT):
                        act.wait_ge(t_done, u + 1)
                        act.activation(xT_all[:, u, :], XT[u % 2][:], ACT.Copy).then_inc(t_copied, 1)
                    act.wait_ge(shifted, 1)
                    act.activation(prob[:], logit[:], ACT.Exp).then_inc(expd, 1)
                    if renormalise:
                        act.wait_ge(gap_ready, 1)
                        act.activation(share[:, 1, :], gap[:], ACT.Exp).then_inc(gap_expd, 1)

                @block.vector
                def _(dve):
                    steps = [0]

                    def then(ins):
                        ins.then_inc(step, 1)
                        steps[0] += 1
                        dve.wait_ge(step, steps[0])

                    def rows(ap):
                        return bcast(ap, 2, E)

                    then(dve.tensor_copy(identb[:], c.ident[:]))
                    dve.wait_ge(lg_done, 1)
                    lg = LG[:, 0:NB * E].rearrange("p (b e) -> p b e", b=NB)
                    then(dve.tensor_reduce(red[:], lg, AX.X, ALU.max))
                    dve.tensor_tensor(logit[:], lg, rows(red[:]), ALU.subtract).then_inc(shifted, 1)
                    dve.wait_ge(expd, 1)
                    then(dve.tensor_reduce(red[:], prob[:], AX.X, ALU.add))
                    then(dve.reciprocal(red[:], red[:]))
                    then(dve.tensor_tensor(prob[:], prob[:], rows(red[:]), ALU.mult))
                    dve.wait_ge(base_set, 6)
                    src = prob
                    for n in range(2):
                        then(dve.tensor_reduce(best[:, n, :], src[:], AX.X, ALU.max))
                        then(dve.tensor_tensor(rank[:], src[:], rows(best[:, n, :]), ALU.is_equal))
                        then(dve.tensor_tensor(rank[:], rank[:], bcast(order[:], 1, NB), ALU.mult))
                        then(dve.tensor_reduce(red[:], rank[:], AX.X, ALU.max))
                        then(dve.tensor_tensor(hit[:, n], rank[:], rows(red[:]), ALU.is_equal))
                        if n == 0:
                            then(dve.scalar_tensor_tensor(out=logit[:], in0=hit[:, 0], scalar=-2.0, in1=prob[:],
                                                          op0=ALU.mult, op1=ALU.add))
                            src = logit
                    if renormalise:
                        dve.tensor_tensor(gap[:], best[:, 1, :], best[:, 0, :], ALU.subtract).then_inc(gap_ready, 1)
                        dve.wait_ge(gap_expd, 1)
                        then(dve.tensor_scalar(red[:], share[:, 1, :], 1.0, None, ALU.add))
                        then(dve.reciprocal(share[:, 0, :], red[:]))
                        then(dve.tensor_tensor(share[:, 1, :], share[:, 1, :], share[:, 0, :], ALU.mult))
                    two = share if renormalise else best
                    then(dve.tensor_tensor(weight[:], hit[:, 0], rows(two[:, 0, :]), ALU.mult))
                    then(dve.tensor_tensor(rank[:], hit[:, 1], rows(two[:, 1, :]), ALU.mult))
                    then(dve.tensor_tensor(weight[:], weight[:], rank[:], ALU.add))
                    for n in range(PARTS):
                        dve.tensor_copy(part[:, :, n, 0:E], weight[:]).then_inc(part_ready, 1)
                        if n < PARTS - 1:
                            dve.wait_ge(part_ready, n + 1)
                            then(dve.tensor_tensor(weight[:], weight[:], part[:, :, n, 0:E], ALU.subtract))
                    for n in range(1, PARTS):
                        then(dve.tensor_copy(spread[32 * n:32 * n + E], spread[0:E]))
                    dve.wait_ge(wt_done, 1)
                    flat = wT[:].rearrange("p u t -> p (u t)")
                    for n in range(NWT):
                        w = min(1024, NB * P - 1024 * n)
                        dve.tensor_copy(flat[:, 1024 * n:1024 * n + w], WT[n][0:32 * PARTS, 0:w]).then_inc(wt_copied, 1)

        silu = sb("silu", [P, 2, TW])
        prod = sb("prod", [P, 2, TW])
        hid = sb("hid", [P, 2, TW])
        oT = sb("oT", [P, TW])
        z = sb("z", [P, TB, P])
        stats = sb("stats", [P, TB, 6])
        mv = sb("mv", [P, TB, 2])
        var_eps = sb("var_eps", [P, TB])
        rstd = sb("rstd", [P, TB])
        x_new = sb("x_new", [P, 2, TB, P])
        G, U, WB = c.banks[0:2], c.banks[2:4], c.banks[4:6]
        OUT, TOK = c.banks[6], c.banks[7]
        g_done = sem("g_done")
        u_done = sem("u_done")
        wb_done = sem("wb_done")
        d_done = sem("d_done")
        tok_done = sem("tok_done")
        silu_ready = sem("silu_ready")
        out_copied = sem("out_copied")
        prod_ready = sem("prod_ready")
        hid_ready = sem("hid_ready")
        z_ready = sem("z_ready")
        stats_ready = sem("stats_ready")
        x_ready = sem("x_ready")
        var_ready = sem("var_ready")
        rstd_ready = sem("rstd_ready")
        chain = sem("chain")

        def pairs(eng, body, tail=None):
            body(Batch(0))
            if NT > 2:
                with eng.Fori(0, NT // 2 - 1) as i:
                    body(Batch(1, i, 1))
            if tail:
                tail(Batch(NT // 2 - 1))

        def has_previous(pair):
            return pair.reg is not None

        def before(eng, sem, pair, each, n):
            if pair.reg is not None or n > 0:
                eng.wait_ge(sem, pair.count(each, n))

        def tile(pair, par):
            return 2 * pair.off + par if pair.reg is None else pair.reg * 2 + (2 * pair.off + par)

        with nc.Block() as block:
            @block.sync
            def _(sp):
                sp.sem_inc(stored[1], 16)
                def body(pair):
                    for par in range(2):
                        u = tile(pair, par)
                        before(sp, x_ready, pair, 2, par + 1)
                        sp.dma_start(out[bass.ds(u * TB, TB)].rearrange("b t d -> t b d"), x_new[:, par])\
                            .then_inc(stored[par], 16)

                pairs(sp, body)
                for par in range(2):
                    sp.wait_ge(stored[par], 16 * (NT // 2 + par))

            @block.gpsimd
            def _(pool):
                def body(pair):
                    for par in range(2):
                        before(pool, stats_ready, pair, 2, par + 1)
                        pool.tensor_tensor(var_eps[:], mv[:, :, 1], c.eps[:].to_broadcast([P, TB]), ALU.add)\
                            .then_inc(var_ready, 1)
                        before(pool, var_ready, pair, 2, par + 1)
                        pool.tensor_tensor(rstd[:], var_eps[:], c.minushalf[:].to_broadcast([P, TB]), ALU.pow)\
                            .then_inc(rstd_ready, 1)

                pairs(pool, body)

            @block.tensor
            def _(pe):
                pe.wait_ge(w_in, 48)

                def down(pair, n):
                    k = n % NC
                    before(pe, hid_ready, pair, 2 * NC, n + 1)
                    if k == 0:
                        before(pe, out_copied, pair, 2, n // NC)
                    pe.matmul(OUT[:], w_down[:, k, :], hid[:, n % 2, :], start=(k == 0), stop=(k == NC - 1))\
                        .then_inc(d_done, 1)

                def to_tokens(pair, par):
                    before(pe, out_copied, pair, 2, par + 1)
                    before(pe, z_ready, pair, 2, par)
                    for s in range(TB):
                        mm = pe.transpose(TOK[:, P * s:P * s + P], oT[:, P * s:P * s + P], c.ident[:])
                    mm.then_inc(tok_done, 1)

                def body(pair):
                    for n in range(2 * NC):
                        par, k = divmod(n, NC)
                        xT = xT_all[:, tile(pair, par), :]
                        before(pe, silu_ready, pair, 2 * NC, n - 1)
                        pe.matmul(G[n % 2][:], gate_cols[:, P * k:P * k + P], xT, start=True, stop=True)\
                            .then_inc(g_done, 1)
                        before(pe, prod_ready, pair, 2 * NC, n - 1)
                        pe.matmul(U[n % 2][:], up_cols[:, P * k:P * k + P], xT, start=True, stop=True)\
                            .then_inc(u_done, 1)
                        if k % PER == 0:
                            w = k // PER
                            m = par * NW + w
                            pm = m - 2
                            last = (pm // NW) * NC + (pm % NW) * PER + PER - 1
                            before(pe, hid_ready, pair, 2 * NC, last + 1)
                            pe.matmul(WB[m % 2][:], spread[:, w, :], wT[:, tile(pair, par), :],
                                      start=True, stop=True).then_inc(wb_done, 1)
                        if n:
                            down(pair, n - 1)
                        elif has_previous(pair):
                            down(pair.plus(-1), 2 * NC - 1)
                        if k == 2 and par == 1:
                            to_tokens(pair, 0)
                        if k == 2 and par == 0 and has_previous(pair):
                            to_tokens(pair.plus(-1), 1)

                def tail(pair):
                    down(pair, 2 * NC - 1)
                    to_tokens(pair, 1)

                pairs(pe, body, tail)

            @block.scalar
            def _(act):
                def copy_out(pair, par):
                    before(act, d_done, pair, 2 * NC, NC * (par + 1))
                    before(act, tok_done, pair, 2, par)
                    act.activation(oT[:], OUT[:], ACT.Copy).then_inc(out_copied, 1)

                def body(pair):
                    for n in range(2 * NC):
                        before(act, g_done, pair, 2 * NC, n + 1)
                        before(act, prod_ready, pair, 2 * NC, n - 1)
                        act.activation(silu[:, n % 2, :], G[n % 2][:], ACT.Silu).then_inc(silu_ready, 1)
                        if n == NC:
                            copy_out(pair, 0)
                        if n == 0 and has_previous(pair):
                            copy_out(pair.plus(-1), 1)

                pairs(act, body, lambda pair: copy_out(pair, 1))

            @block.vector
            def _(dve):
                def finish(pair, par, parts):
                    if 0 in parts:
                        before(dve, tok_done, pair, 2, par + 1)
                        dve.tensor_tensor(z[:], TOK[:].rearrange("p (b d) -> p b d", b=TB),
                                          x_all[:, bass.ds(tile(pair, par) * TB, TB), :], ALU.add).then_inc(z_ready, 1)
                    if 1 in parts:
                        before(dve, z_ready, pair, 2, par + 1)
                        for s in range(TB):
                            dve.bn_stats(stats[:, s, :], z[:, s, :]).then_inc(chain, 1)
                    if 2 in parts:
                        for s in range(TB):
                            dve.wait_ge(chain, s + 1)
                            op = dve.bn_aggr(mv[:, s, :], stats[:, s, :])
                            if s == TB - 1:
                                op.then_inc(stats_ready, 1)
                            else:
                                op.then_inc(chain, 1)
                    if 3 in parts:
                        before(dve, rstd_ready, pair, 2, par + 1)
                        if par == 1 or pair.reg is not None:
                            dve.wait_ge(stored[par], pair.count(16, 16 * par))
                        for s in range(TB):
                            op = dve.tensor_scalar(x_new[:, par, s, :], z[:, s, :], mv[:, s, 0:1], rstd[:, s:s + 1],
                                                   ALU.subtract, ALU.mult)
                        op.then_inc(x_ready, 1)
                        dve.wait_ge(chain, 2 * TB - 1)
                        dve.sem_clear(chain)

                def body(pair):
                    for n in range(2 * NC):
                        par, k = divmod(n, NC)
                        before(dve, silu_ready, pair, 2 * NC, n + 1)
                        before(dve, u_done, pair, 2 * NC, n + 1)
                        before(dve, hid_ready, pair, 2 * NC, n - 1)
                        dve.tensor_tensor(prod[:, n % 2, :], silu[:, n % 2, :], U[n % 2][:], ALU.mult)\
                            .then_inc(prod_ready, 1)
                        before(dve, prod_ready, pair, 2 * NC, n + 1)
                        m = par * NW + k // PER
                        before(dve, wb_done, pair, 2 * NW, m + 1)
                        before(dve, d_done, pair, 2 * NC, n - 1)
                        dve.tensor_tensor(hid[:, n % 2, :], prod[:, n % 2, :], WB[m % 2][:], ALU.mult)\
                            .then_inc(hid_ready, 1)
                        if 3 <= k < 7 and par == 1:
                            finish(pair, 0, [k - 3])
                        if 3 <= k < 7 and par == 0 and has_previous(pair):
                            finish(pair.plus(-1), 1, [k - 3])

                pairs(dve, body, lambda pair: finish(pair, 1, range(4)))

        clear(nc, sems)


def decoder(nc, a, out):
    NB = a["x"].shape[0]
    hop = [nc.dram_tensor(f"x_after_{n}", (NB, P, P), F32, kind="Internal").ap() for n in range(5)]
    R = a["L0_attn_rel_bias"].shape[0]
    bias_rows = nc.dram_tensor("bias_rows", (H, 2 * ((R + 1) // 2) + R), F32, kind="Internal").ap()
    ctx_tokens = a["ctx_1024"]

    def weights(prefix):
        return [a[prefix + w] for w in ("Wq", "bq", "Wk", "bk", "Wv", "bv", "Wo", "bo")]

    with ExitStack() as ctx:
        c = constants(nc, ctx)
        attention(nc, "L0_attn", c, a["x"], None, hop[0], *weights("L0_attn_"), transposed=True, topk=32,
                  gates=a["L0_attn_head_gates"], rel_bias=a["L0_attn_rel_bias"], bias_rows=bias_rows)
        attention(nc, "L0_xattn", c, hop[0], ctx_tokens, hop[1], *weights("L0_xattn_"), transposed=False,
                  mask=a["mask_BxSxS2_bf1"])
        experts(nc, "L0_ffn", c, hop[1], hop[2], a["L0_ffn_router_kernel_DE"], a["L0_ffn_kernel_gating_EDF"],
                a["L0_ffn_kernel_up_EDF"], a["L0_ffn_kernel_down_EFD"], renormalise=True)
        attention(nc, "L1_attn", c, hop[2], None, hop[3], *weights("L1_attn_"), transposed=False, causal=True)
        attention(nc, "L1_xattn", c, hop[3], ctx_tokens, hop[4], *weights("L1_xattn_"), transposed=True, topk=64,
                  scrambled=True)
        experts(nc, "L1_ffn", c, hop[4], out, a["L1_ffn_w_router"].rearrange("e d -> d e"), a["L1_ffn_w1"],
                a["L1_ffn_w3"], a["L1_ffn_w2"], renormalise=False)


def kernel(**inputs):
    import numpy as _np
    import concourse.bacc as _bacc
    from concourse import mybir as _mybir
    from concourse.bass_utils import run_bass_kernel_spmd as _run

    nc = _bacc.Bacc("TRN2", target_bir_lowering=False, num_devices=1)
    arrays, args = {}, {}
    for name, value in inputs.items():
        v = _np.ascontiguousarray(value)
        arrays[f"in_{name}_dram"] = v
        args[name] = nc.dram_tensor(f"in_{name}_dram", v.shape, _mybir.dt.from_np(v.dtype), kind="ExternalInput").ap()
    out = nc.dram_tensor("out_0_dram", inputs["x"].shape, F32, kind="ExternalOutput").ap()
    decoder(nc, args, out)
    r = _run(nc, [arrays], core_ids=[0])
    return r.results[0]["out_0_dram"]
```

```python
from contextlib import ExitStack

import numpy as np

import concourse.bass as bass
from concourse import mybir

F32 = mybir.dt.float32
BF16 = mybir.dt.bfloat16
F32R = mybir.dt.float32r
ALU = mybir.AluOpType
ACT = mybir.ActivationFunctionType
AX = mybir.AxisListType

P = 128
H = 16
HD = 8
NQ = 4
QH = 4
BIG = float(2.0 ** 60)
TAKEN = -3.0e38
EPS = 1e-5


class Batch:

    def __init__(self, off, reg=None, step=2):
        self.off, self.reg, self.step = off, reg, step

    def plus(self, n):
        return Batch(self.off + n, self.reg, self.step)

    @property
    def par(self):
        return self.off % 2

    def within(self, n):
        return self.reg is not None or 0 <= self.off < n

    def count(self, each, more=0):
        if self.reg is None:
            return each * self.off + more
        return self.reg * (self.step * each) + (each * self.off + more)

    def count_par(self, each):
        if self.reg is None:
            return each * (self.off // 2 + 1)
        return self.reg * each + each * (self.off // 2 + 1)

    @property
    def index(self):
        return self.off if self.reg is None else self.reg * 2 + self.off


def wait(eng, sem, batch, each, more):
    if batch.reg is None and batch.off < 0:
        return
    eng.wait_ge(sem, batch.count(each, more))


def wait_par(eng, sems, batch, each):
    if batch.reg is None and batch.off < 0:
        return
    eng.wait_ge(sems[batch.par], batch.count_par(each))


def slots(eng, body, nb):
    first, last = 4, nb - 2
    for t in range(-2, first):
        body(Batch(t))
    with eng.Fori(0, (last - first) // 2) as i:
        body(Batch(first, i))
        body(Batch(first + 1, i))
    for t in range(last, nb + 2):
        body(Batch(t))


def bcast(ap, axis, n):
    return ap.unsqueeze(axis).to_broadcast([*ap.shape[:axis], n, *ap.shape[axis:]])


class Consts:
    pass


def clear(nc, sems):
    with nc.Block() as block:
        @block.sync
        def _(sp):
            for s in sems[0::5]:
                sp.sem_clear(s)

        @block.gpsimd
        def _(pool):
            for s in sems[1::5]:
                pool.sem_clear(s)

        @block.tensor
        def _(pe):
            for s in sems[2::5]:
                pe.sem_clear(s)

        @block.scalar
        def _(act):
            for s in sems[3::5]:
                act.sem_clear(s)

        @block.vector
        def _(dve):
            for s in sems[4::5]:
                dve.sem_clear(s)


def constants(nc, ctx):
    c = Consts()

    def sb(name, shape, dt=F32):
        return ctx.enter_context(nc.sbuf_tensor(name, shape, dt))

    c.ident = sb("ident", [P, P])
    c.flip = sb("flip", [P, P])
    c.identbig = sb("identbig", [P, P], BF16)
    c.causal = sb("causal", [P, P], BF16)
    c.onesrow = sb("onesrow", [P, P])
    c.eps = sb("eps", [P, 1])
    c.minushalf = sb("minushalf", [P, 1])
    c.headmask = sb("headmask", [P, H])
    c.halfmask = sb("halfmask", [P, H // 2])
    c.groupmask = sb("groupmask", [P, QH])
    c.banks = [ctx.enter_context(nc.psum_tensor(f"bank{n}", [P, 512], F32)) for n in range(8)]
    built = ctx.enter_context(nc.semaphore("const_built"))
    vbuilt = ctx.enter_context(nc.semaphore("const_derived"))
    with nc.Block() as block:
        @block.gpsimd
        def _(pool):
            pool.memset(c.ident[:], 0.0).then_inc(built, 1)
            pool.memset(c.flip[:], 0.0).then_inc(built, 1)
            pool.memset(c.causal[:], 0.0).then_inc(built, 1)
            pool.memset(c.headmask[:], 1.0).then_inc(built, 1)
            pool.memset(c.groupmask[:], 1.0).then_inc(built, 1)
            pool.memset(c.onesrow[:], 1.0).then_inc(built, 1)
            pool.memset(c.eps[:], EPS).then_inc(built, 1)
            pool.memset(c.minushalf[:], -0.5).then_inc(built, 1)
            pool.wait_ge(built, 8)
            pool.affine_select(out=c.ident[:], in_=c.ident[:], compare_op=ALU.not_equal, fill=1.0,
                               base=0, pattern=[[-1, P]], channel_multiplier=1).then_inc(built, 1)
            pool.affine_select(out=c.flip[:], in_=c.flip[:], compare_op=ALU.not_equal, fill=1.0,
                               base=1 - P, pattern=[[1, P]], channel_multiplier=1).then_inc(built, 1)
            pool.affine_select(out=c.causal[:], in_=c.causal[:], compare_op=ALU.is_ge, fill=-1.0,
                               base=0, pattern=[[-1, P]], channel_multiplier=1).then_inc(built, 1)
            pool.affine_select(out=c.headmask[:], in_=c.headmask[:], compare_op=ALU.is_ge, fill=0.0,
                               base=0, pattern=[[-HD, H]], channel_multiplier=1).then_inc(built, 1)
            pool.affine_select(out=c.groupmask[:], in_=c.groupmask[:], compare_op=ALU.is_ge, fill=0.0,
                               base=0, pattern=[[-32, QH]], channel_multiplier=1).then_inc(built, 1)
            pool.wait_ge(built, 13)
            pool.affine_select(out=c.headmask[:], in_=c.headmask[:], compare_op=ALU.is_ge, fill=0.0,
                               base=HD - 1, pattern=[[HD, H]], channel_multiplier=-1).then_inc(built, 1)
            pool.affine_select(out=c.groupmask[:], in_=c.groupmask[:], compare_op=ALU.is_ge, fill=0.0,
                               base=31, pattern=[[32, QH]], channel_multiplier=-1).then_inc(built, 1)

        @block.vector
        def _(dve):
            dve.wait_ge(built, 15)
            dve.tensor_scalar(c.identbig[:], c.ident[:], BIG, None, ALU.mult).then_inc(vbuilt, 1)
            dve.tensor_tensor(c.halfmask[:], c.headmask[:, 0:H // 2], c.headmask[:, H // 2:], ALU.add)\
                .then_inc(vbuilt, 1)
    return c


def attention(nc, name, c, x, kv, out, wq, bq, wk, bk, wv, bv, wo, bo, *,
              transposed, mask=None, causal=False, topk=0, gates=None, rel_bias=None, bias_rows=None,
              scrambled=False, later=None):
    NB = x.shape[0]
    ROUNDS = topk // 8
    halved = scrambled
    add_on_pe = topk > 0
    in_parts = topk == 0
    scale = float(HD) ** -0.5
    with ExitStack() as ctx:
        def sb(nm, shape, dt=F32):
            return ctx.enter_context(nc.sbuf_tensor(f"{name}_{nm}", shape, dt))

        sems = []

        def sem(nm):
            sems.append(ctx.enter_context(nc.semaphore(f"{name}_{nm}")))
            return sems[-1]

        w_raw = sb("w_raw", [P, 4, P])
        w_t = sb("w_t", [P, 4, P]) if transposed else w_raw
        Wq, Wk, Wv, Wo = (w_t[:, n, :] for n in range(4))
        bcol = sb("bcol", [P, 4])
        bq_s = sb("bq_s", [P, 1])
        bv_g = sb("bv_g", [P, 1])
        bo_pad = sb("bo_pad", [P, P])
        x_tok = sb("x_tok", [P, 2, P])
        kv_tok = sb("kv_tok", [P, 2, P]) if kv is not None else None
        x_res = sb("x_res", [P, 2, P])
        xkT = sb("xkT", [P, 2, P])
        if in_parts:
            qk = sb("qk", [P, 2, P])
            qk_hi = sb("qk_hi", [P, 2, 2, P], F32R)
            qk_lo = sb("qk_lo", [P, 2, 2, P], F32R)
            k_bd = sb("k_bd", [P, 2, 2, H // 2, P], F32R)
        else:
            q_t = sb("q_t", [P, 2, P])
            k_t = sb("k_t", [P, P])
            k_bd = sb("k_bd", [P, 2, H, P])
        v_pad = sb("v_pad", [P, 2, H, 32])
        p_sb = sb("p", [P, NQ, QH, P])
        pT = sb("pT", [P, 2, QH, P])
        neg_max = sb("neg_max", [P, NQ, QH])
        o_raw = sb("o_raw", [P, NQ, P])
        r_sum = sb("r_sum", [P, H])
        o_n = sb("o_n", [P, P])
        oT = sb("oT", [P, P])
        stats = sb("stats", [P, 6])
        mv = sb("mv", [P, 2])
        var_eps = sb("var_eps", [P, 1])
        rstd = sb("rstd", [P, 1])
        x_bo = sb("x_bo", [P, P])
        x_sum = sb("x_sum", [P, P])
        x_new = sb("x_new", [P, 2, P])
        if topk:
            s_sb = sb("s", [P, NQ, QH, P])
            work = sb("work", [P, QH, P] if halved else [P, NQ, QH, P])
            top8 = sb("top8", [P, QH, 8] if halved else [P, NQ, QH, ROUNDS, 8])
            keep = sb("keep", [P, QH, P])
        if halved:
            HALF = P // 2
            BEST = HALF // 2
            s_neg = sb("s_neg", [P, NQ, QH, HALF])
            pairs = sb("pairs", [P, 2, 2, QH, HALF])
            best = sb("best", [P, 2, QH, BEST])
            cut = sb("cut", [P, 2, QH, BEST])
            edge = sb("edge", [P, NQ, 2, QH])
            tied = sb("tied", [P, QH])
            tie_count = sb("tie_count", [1, 1], mybir.dt.int32)
        if rel_bias is not None:
            bias_sb = sb("bias_sb", [P, H, P])
            R = rel_bias.shape[0]
            LO = (R + 1) // 2
            table = sb("table", [R, H])
            rows_sb = sb("rows", [H, 2 * LO + R])
        if mask is not None:
            m_raw = sb("m_raw", [P, 2, P], mybir.dt.uint8)
            m_add = sb("m_add", [P, 2, P], BF16)
        if scrambled:
            pick = sb("pick", [P, H, 32])
            lin = sb("lin", [P, 3, P])
            q32 = sb("q32", [P, 2, NQ, P])
            k32 = sb("k32", [P, NQ, P])
            v32 = sb("v32", [P, NQ, P])
            rowmask = sb("rowmask", [P, H])
            place = sb("place", [P, 4, 32])
            o_x = sb("o_x", [P, H, H, HD])
            o_tok = sb("o_tok", [P, P])

        S = c.banks[0:2]
        PT = c.banks[2:4]
        PROJ = c.banks[4]
        O = c.banks[5]
        OT = c.banks[6]
        Y = c.banks[7]
        TIES = slice(P, P + QH)

        weights_in = sem("weights_in")
        tok_in = [sem("tok_in0"), sem("tok_in1")]
        res_in = [sem("res_in0"), sem("res_in1")]
        stored = [sem("stored0"), sem("stored1")]
        set_pool = sem("set_pool")
        set_pe = sem("set_pe")
        set_act = sem("set_act")
        set_dve = sem("set_dve")
        if rel_bias is not None:
            table_in = sem("table_in")
            table_turned = sem("table_turned")
            rows_ready = sem("rows_ready")
            rows_out = sem("rows_out")
            bias_in = sem("bias_in")
        tr_done = sem("tr_done")
        proj_done = sem("proj_done")
        s_done = sem("s_done")
        pt_done = sem("pt_done")
        pv_done = sem("pv_done")
        ot_done = sem("ot_done")
        ont_done = sem("ont_done")
        y_done = sem("y_done")
        xkT_ready = sem("xkT_ready")
        qk_ready = sem("qk_ready")
        lo_ready = sem("lo_ready")
        v_ready = sem("v_ready")
        s_copied = sem("s_copied")
        exp_done = sem("exp_done")
        pT_ready = sem("pT_ready")
        o_copied = sem("o_copied")
        oT_ready = sem("oT_ready")
        chain = sem("chain")
        quad_begun = sem("quad_begun")
        max_ready = sem("max_ready")
        top_ready = sem("top_ready")
        on_ready = sem("on_ready")
        stats_ready = sem("stats_ready")
        x_ready = sem("x_ready")
        m_ready = sem("m_ready")
        if halved:
            tied_ready = sem("tied_ready")
            ties_counted = sem("ties_counted")
            ties_read = sem("ties_read")
            ties_seen = sem("ties_seen")
            redone = sem("redone")
        kbd_ready = sem("kbd_ready")
        p_ready = sem("p_ready")
        keep_ready = sem("keep_ready")
        step_begun = sem("step_begun")
        var_ready = sem("var_ready")
        rstd_ready = sem("rstd_ready")
        x_summed = sem("x_summed")
        x_bo_ready = sem("x_bo_ready")
        if scrambled:
            pick_done = sem("pick_done")
            picked = sem("picked")
            ox_ready = sem("ox_ready")
            r_done = sem("r_done")
            otok_ready = sem("otok_ready")

        n_weight_dmas = 4 + 4 + (1 if gates is not None else 0)
        tok_dmas = 1 + (kv is not None) + (mask is not None)
        n_qk = 4 if in_parts else 2
        n_set_act = 1 + (gates is not None) + transposed

        def scored_at(t, q):
            if not halved:
                return t, q
            return (t, q + 1) if q < NQ - 1 else (t.plus(1), 0)

        with nc.Block() as block:
            @block.sync
            def _(sp):
                if rel_bias is not None:
                    sp.dma_start(table[:], rel_bias).then_inc(table_in, 16)

                def load_weights():
                    for n, w in enumerate((wq, wk, wv, wo)):
                        sp.dma_start(w_raw[:, n, :], w).then_inc(weights_in, 16)
                    for n, b in enumerate((bq, bk, bv)):
                        sp.dma_start(bcol[:, n:n + 1], b.rearrange("(p a) -> p a", a=1)).then_inc(weights_in, 16)
                    if gates is not None:
                        sp.dma_start(bcol[:, 3:4], bcast(gates, 1, HD).unsqueeze(2)).then_inc(weights_in, 16)
                    if add_on_pe:
                        sp.wait_ge(set_pool, 1)
                        sp.dma_start(bo_pad[0:1, :], bo.rearrange("(a n) -> a n", a=1)).then_inc(weights_in, 16)
                    else:
                        sp.dma_start(bo_pad[:], bo.rearrange("(a n) -> a n", a=1).to_broadcast([P, P])).then_inc(weights_in, 16)

                def load_bias():
                    sp.wait_ge(rows_ready, 3)
                    sp.dma_start(bias_rows, rows_sb[:]).then_inc(rows_out, 16)
                    sp.wait_ge(rows_out, 16)
                    rows = bass.AP(bias_rows.tensor, 0, [[1, P], [bias_rows.shape[1], H], [1, P]])
                    sp.dma_start(bias_sb[:], rows).then_inc(bias_in, 16)

                def slot(t):
                    if t.reg is None and t.off == -1:
                        load_weights()
                    if t.reg is None and t.off == 0 and rel_bias is not None:
                        load_bias()
                    if later is not None and t.reg is None and t.off == 2:
                        later.load(sp)
                    load = t.plus(2)
                    if load.within(NB):
                        wait(sp, tr_done, t, 1, 1)
                        if mask is not None:
                            wait(sp, m_ready, t, 1, 1)
                        sp.dma_start(x_tok[:, t.par, :], x[load.index]).then_inc(tok_in[t.par], 16)
                        if kv is not None:
                            sp.dma_start(kv_tok[:, t.par, :], kv[load.index]).then_inc(tok_in[t.par], 16)
                        if mask is not None:
                            sp.dma_start(m_raw[:, t.par, :], mask[load.index]).then_inc(tok_in[t.par], 16)
                    if t.within(NB):
                        wait(sp, y_done if add_on_pe else x_bo_ready, t.plus(-2), 1, 1)
                        sp.dma_start(x_res[:, t.par, :], x[t.index]).then_inc(res_in[t.par], 16)
                    done = t.plus(-2)
                    if done.within(NB):
                        wait(sp, x_ready, done, 1, 1)
                        sp.dma_start(out[done.index], x_new[:, t.par, :]).then_inc(stored[t.par], 16)

                slots(sp, slot, NB)
                for par in range(2):
                    sp.wait_ge(stored[par], 16 * (NB // 2))

            @block.gpsimd
            def _(pool):
                if add_on_pe:
                    pool.memset(bo_pad[:], 0.0).then_inc(set_pool, 1)
                else:
                    pool.wait_ge(weights_in, 16 * n_weight_dmas)
                    pool.sem_inc(set_pool, 1)
                pool.memset(v_pad[:], 0.0).then_inc(set_pool, 1)
                pool.wait_ge(set_pool, 2)
                pool.memset(v_pad[:, :, :, HD:HD + 1], 1.0).then_inc(set_pool, 1)
                if scrambled:
                    pool.memset(pick[:], 0.0).then_inc(set_pool, 1)
                    pool.memset(place[:], 0.0).then_inc(set_pool, 1)

                def keep_top(t, q):
                    b, j = (t, q - 1) if q else (t.plus(-1), NQ - 1)
                    if topk and b.within(NB):
                        wait(pool, top_ready, b, NQ, j + 1)
                        p, n = (b, j - 1) if j else (b.plus(-1), NQ - 1)
                        wait(pool, p_ready, p, NQ, n + 1)
                        pool.sem_inc(step_begun, 1)
                        for h in range(QH):
                            least = edge[:, j, 0, h:h + 1] if halved else top8[:, j, h, ROUNDS - 1, 7:8]
                            op = pool.tensor_scalar(keep[:, h, :], s_sb[:, j, h, :], least, None, ALU.is_ge)
                        op.then_inc(keep_ready, 1)
                        wait(pool, exp_done, b, NQ, j + 1)
                        wait(pool, keep_ready, b, NQ, j + 1)
                        op = pool.tensor_tensor(p_sb[:, j, :, :], p_sb[:, j, :, :], keep[:], ALU.mult)
                        op.then_inc(p_ready, 1)

                def slot(t):
                    for q in range(NQ):
                        if not halved:
                            keep_top(t, q)
                        b = t.plus(-2)
                        if q == 1 and not add_on_pe and b.within(NB):
                            wait_par(pool, res_in, b, 16)
                            wait(pool, stats_ready, b.plus(-1), 1, 1)
                            pool.tensor_tensor(x_bo[:], x_res[:, b.par, :], bo_pad[:], ALU.add)\
                                .then_inc(x_bo_ready, 1)
                        if scrambled and q == 0 and b.within(NB):
                            wait(pool, on_ready, b, 1, 1)
                            wait(pool, r_done, b.plus(-1), 1, 1)
                            pool.tensor_tensor(
                                o_x[:], bcast(o_n[:].rearrange("p (h d) -> p h d", h=H), 2, H),
                                bcast(bcast(rowmask[:], 1, H), 3, HD), ALU.mult).then_inc(ox_ready, 1)
                        if halved:
                            keep_top(t, q)
                        b = t.plus(1)
                        if q >= 2 and b.within(NB):
                            if q == 2:
                                if scrambled:
                                    wait(pool, picked, b, 3, 2)
                                else:
                                    wait(pool, qk_ready, b, n_qk, n_qk)
                                if in_parts:
                                    pool.tensor_tensor(qk_lo[:, b.par], qk[:], qk_hi[:, b.par].bitcast(F32),
                                                       ALU.subtract).then_inc(lo_ready, 1)
                                    wait(pool, lo_ready, b, 1, 1)
                            for part in range(2) if in_parts else ():
                                kk = (qk_lo if part else qk_hi)[:, b.par, 1, :].bitcast(F32)
                                heads = slice(QH * (q - 2), QH * (q - 2) + QH)
                                pool.tensor_tensor(k_bd[:, b.par, part, heads, :], bcast(kk, 1, QH),
                                                   bcast(c.halfmask[:, heads], 2, P), ALU.mult).then_inc(kbd_ready, 1)
                            for j in () if in_parts else (0, 1) if q == 2 else (2, 3):
                                if scrambled:
                                    kk, mm = k32[:, j, :], c.groupmask[:]
                                else:
                                    kk, mm = k_t[:], c.headmask[:, QH * j:QH * j + QH]
                                pool.tensor_tensor(k_bd[:, b.par, QH * j:QH * j + QH, :], bcast(kk, 1, QH),
                                                   bcast(mm, 2, P), ALU.mult).then_inc(kbd_ready, 1)
                        b = t.plus(-2)
                        if q == 2 and b.within(NB):
                            wait(pool, stats_ready, b, 1, 1)
                            pool.tensor_tensor(var_eps[:], mv[:, 1:2], c.eps[:], ALU.add).then_inc(var_ready, 1)
                            wait(pool, var_ready, b, 1, 1)
                            pool.tensor_tensor(rstd[:], var_eps[:], c.minushalf[:], ALU.pow)\
                                .then_inc(rstd_ready, 1)

                slots(pool, slot, NB)

            @block.tensor
            def _(pe):
                if rel_bias is not None:
                    pe.wait_ge(table_in, 16)
                    pe.transpose(Y[0:H, 0:R], table[:], c.ident[0:R, 0:R]).then_inc(table_turned, 1)
                pe.wait_ge(weights_in, 16 * n_weight_dmas)
                if transposed:
                    for n in range(4):
                        mm = pe.transpose(PROJ[:, P * n:P * n + P], w_raw[:, n, :], c.ident[:])
                    mm.then_inc(set_pe, 1)
                pe.wait_ge(set_act, n_set_act)
                pe.wait_ge(set_pool, 3)
                if scrambled:
                    pe.wait_ge(set_dve, 4)

                def transposes(b):
                    wait_par(pe, tok_in, b, 16 * tok_dmas)
                    wait(pe, v_ready, b.plus(-1), 1, 1)
                    mm = pe.transpose(PROJ[:, 0:P], x_tok[:, b.par, :], c.ident[:])
                    if kv is not None:
                        mm = pe.transpose(PROJ[:, P:2 * P], kv_tok[:, b.par, :], c.ident[:])
                    mm.then_inc(tr_done, 1)

                def project(b):
                    xT, kT = xkT[:, 0, :], xkT[:, 1 if kv is not None else 0, :]
                    wait(pe, xkT_ready, b, 1, 1)
                    pe.matmul(PROJ[:, 0:P], Wq, xT, start=True, stop=True)
                    pe.matmul(PROJ[:, P:2 * P], Wk, kT, start=True, stop=True)
                    if scrambled:
                        mm = pe.matmul(PROJ[:, 2 * P:3 * P], Wv, kT, start=True, stop=True)
                    else:
                        mm = pe.matmul(PROJ[:, 2 * P:3 * P], kT, Wv, start=True, stop=True)
                    mm.then_inc(proj_done, 1)

                def pick_heads(b, n):
                    src = lin[:, n, :].rearrange("p (j g t) -> p g j t", j=NQ, g=QH)
                    dst = PROJ[:].rearrange("p (j t r) -> p j t r", j=NQ, r=H)
                    if n == 0:
                        wait(pe, qk_ready, b, 3, 3)
                    else:
                        wait(pe, picked, b, 3, n)
                    for r in range(H):
                        for g in range(QH):
                            mm = pe.matmul(dst[32 * g:32 * g + 32, :, :, r], pick[:, r, :], src[:, g],
                                           start=True, stop=True)
                    mm.then_inc(pick_done, 1)

                def transpose_v(b):
                    wait(pe, picked, b, 3, 3)
                    for j in range(NQ):
                        mm = pe.transpose(PROJ[:, P * j:P * j + P], v32[:, j, :], c.ident[:])
                    mm.then_inc(pick_done, 1)

                def scores(b, j):
                    if rel_bias is not None and b.reg is None and b.off == 0 and j == 0:
                        pe.wait_ge(bias_in, 16)
                    wait(pe, kbd_ready, b, NQ, 2 * (j % 2) + 2 if in_parts else j + 1)
                    if mask is not None and j == 0:
                        wait(pe, m_ready, b, 1, 1)
                    p, n = (b, j - 2) if j >= 2 else (b.plus(-1), j + 2)
                    wait(pe, s_copied if topk else exp_done, p, NQ, n + 1)
                    dst = S[j % 2][:]
                    added = mask is not None or causal or rel_bias is not None
                    if in_parts:
                        rows = slice(64 * (j // 2), 64 * (j // 2) + 64)
                        heads = slice(QH * (j % 2), QH * (j % 2) + QH)
                        for n, (qp, kp) in enumerate(((0, 0), (0, 1), (1, 0))):
                            mm = pe.matmul(dst, (qk_lo if qp else qk_hi)[rows, b.par, 0, :],
                                           k_bd[rows, b.par, kp, heads, :], start=(n == 0), stop=(n == 2 and not added))
                    else:
                        lhs = q32[:, b.par, j, :] if scrambled else q_t[:, b.par, :]
                        mm = pe.matmul(dst, lhs, k_bd[:, b.par, QH * j:QH * j + QH, :], start=True, stop=not added)
                    if mask is not None:
                        mm = pe.matmul(dst, c.identbig[:], bcast(m_add[:, b.par, :], 1, QH), start=False, stop=True)
                    elif causal:
                        mm = pe.matmul(dst, c.identbig[:], bcast(c.causal[:], 1, QH), start=False, stop=True)
                    elif rel_bias is not None:
                        mm = pe.matmul(dst, c.flip[:], bias_sb[:, QH * j:QH * j + QH, :], start=False, stop=True)
                    mm.then_inc(s_done, 1)

                def count_ties(b, j):
                    wait(pe, tied_ready, b, NQ, j + 1)
                    if j == 1:
                        wait(pe, otok_ready, b.plus(-2), 1, 1)
                    pe.matmul(Y[0:1, TIES], c.onesrow[:, 0:1], tied[:], start=True, stop=True)\
                        .then_inc(ties_counted, 1)

                def transpose_p(b, j):
                    wait(pe, p_ready if topk else exp_done, b, NQ, j + 1)
                    p, n = (b, j - 2) if j >= 2 else (b.plus(-1), j + 2)
                    wait(pe, pT_ready, p, NQ, n + 1)
                    for h in range(QH):
                        mm = pe.transpose(PT[j % 2][:, P * h:P * h + P], p_sb[:, j, h, :], c.ident[:])
                    mm.then_inc(pt_done, 1)

                def weigh_v(b, j):
                    wait(pe, pT_ready, b, NQ, j + 1)
                    if j == 0:
                        wait(pe, v_ready, b, 1, 1)
                        wait(pe, o_copied, b.plus(-1), 1, 1)
                    for g in range(QH):
                        mm = pe.matmul(O[32 * g:32 * g + 32, P * j:P * j + P], v_pad[:, b.par, QH * j + g, :],
                                       pT[:, j % 2, g, :], start=True, stop=True)
                    mm.then_inc(pv_done, 1)

                def transpose_o(b):
                    wait(pe, o_copied, b, 1, 1)
                    wait(pe, on_ready, b.plus(-1), 1, 1)
                    for j in range(NQ):
                        mm = pe.transpose(OT[:, P * j:P * j + P], o_raw[:, j, :], c.ident[:])
                    mm.then_inc(ot_done, 1)

                def ties_seen_in(t, j):
                    if t.within(NB):
                        wait(pe, ties_read, t, NQ, j + 1)
                    elif t.plus(-1).within(NB):
                        wait(pe, ties_read, t.plus(-1), NQ, NQ)

                def unscramble(b):
                    wait(pe, ox_ready, b, 1, 1)
                    ties_seen_in(b.plus(2), 0)
                    wait(pe, x_ready, b.plus(-1), 1, 1)
                    for hh in range(4):
                        for j in range(NQ):
                            mm = pe.matmul(Y[32 * j:32 * j + 32, 0:P], place[:, hh, :],
                                           o_x[:, 4 * j + hh, :, :], start=(hh == 0), stop=(hh == 3),
                                           skip_group_check=True)
                    mm.then_inc(r_done, 1)

                def transpose_on(b):
                    if scrambled:
                        wait(pe, otok_ready, b, 1, 1)
                        ties_seen_in(b.plus(2), 1)
                    else:
                        wait(pe, on_ready, b, 1, 1)
                        wait(pe, x_ready if add_on_pe else x_summed, b.plus(-1), 1, 1)
                    pe.transpose(Y[:, 0:P], (o_tok if scrambled else o_n)[:], c.ident[:]).then_inc(ont_done, 1)

                def project_out(b):
                    wait(pe, oT_ready, b, 1, 1)
                    if not add_on_pe:
                        pe.matmul(Y[:, 0:P], oT[:], Wo, start=True, stop=True).then_inc(y_done, 1)
                        return
                    wait_par(pe, res_in, b, 16)
                    pe.matmul(Y[:, 0:P], oT[:], Wo, start=True, stop=False)
                    pe.matmul(Y[:, 0:P], c.onesrow[:], bo_pad[:], start=False, stop=False)
                    pe.matmul(Y[:, 0:P], c.ident[:], x_res[:, b.par, :], start=False, stop=True)\
                        .then_inc(y_done, 1)

                def slot(t):
                    ahead, prev, prev2 = t.plus(1), t.plus(-1), t.plus(-2)
                    for q in range(NQ):
                        if q == 0 and ahead.within(NB):
                            transposes(ahead)
                        b, j = scored_at(t, q)
                        if q < NQ - 1 and b.within(NB):
                            scores(b, j)
                        d, n = (t, q - 1) if q else (prev, NQ - 1)
                        if halved and d.within(NB):
                            count_ties(d, n)
                        if q == NQ - 1 and b.within(NB):
                            scores(b, j)
                        b, j = (t, q - 2) if q >= 2 else (prev, q + 2)
                        if b.within(NB):
                            transpose_p(b, j)
                        b, j = (t, q - 3) if q >= 3 else (prev, q + 1)
                        if b.within(NB):
                            weigh_v(b, j)
                        if q == 0 and prev2.within(NB) and not scrambled:
                            transpose_on(prev2)
                        if q == 1 and prev2.within(NB) and not scrambled:
                            project_out(prev2)
                        if q == (0 if in_parts else 1) and ahead.within(NB):
                            project(ahead)
                        if q == 1 and prev2.within(NB) and scrambled:
                            unscramble(prev2)
                        if q == 2 and prev2.within(NB) and scrambled:
                            transpose_on(prev2)
                        if scrambled and q in (1, 2) and ahead.within(NB):
                            pick_heads(ahead, q - 1)
                        if q == 2 and prev2.within(NB) and scrambled:
                            project_out(prev2)
                        if q == 3 and prev.within(NB):
                            transpose_o(prev)
                        if scrambled and q == 3 and ahead.within(NB):
                            pick_heads(ahead, 2)
                            transpose_v(ahead)

                slots(pe, slot, NB)

            @block.scalar
            def _(act):
                act.wait_ge(weights_in, 16 * n_weight_dmas)
                act.mul(bq_s[:], bcol[:, 0:1], scale).then_inc(set_act, 1)
                if gates is not None:
                    act.activation(bv_g[:], bcol[:, 2:3], ACT.Identity, scale=bcol[:, 3:4]).then_inc(set_act, 1)
                if transposed:
                    act.wait_ge(set_pe, 1)
                    act.activation(w_t[:].rearrange("p a b -> p (a b)"), PROJ[:], ACT.Copy).then_inc(set_act, 1)

                def v_by_head(ahead):
                    src = PROJ[:, 2 * P:3 * P].rearrange("p (h d) -> p h d", h=H)
                    if scrambled:
                        wait(act, pick_done, ahead, 4, 3)
                        act.activation(v32[:], PROJ[:], ACT.Copy).then_inc(picked, 1)
                        wait(act, pick_done, ahead, 4, 4)
                        src = PROJ[:].rearrange("p (h d) -> p h d", h=H)[:, :, 0:HD]
                    wait(act, pv_done, ahead.plus(-2), NQ, NQ)
                    act.activation(v_pad[:, ahead.par, :, 0:HD], src, ACT.Copy).then_inc(v_ready, 1)

                def token_order(b):
                    if b.within(NB):
                        wait(act, r_done, b, 1, 1)
                        act.activation(o_tok[:], Y[:, 0:P], ACT.Copy).then_inc(otok_ready, 1)

                def exponentials(t, q):
                    if topk:
                        b, j = (t, q - 1) if q else (t.plus(-1), NQ - 1)
                    else:
                        b, j = t, q
                    if b.within(NB):
                        wait(act, top_ready if halved else max_ready, b, NQ, j + 1)
                        for h in range(QH):
                            src = s_sb[:, j, h, :] if topk else S[j % 2][:, P * h:P * h + P]
                            op = act.activation(p_sb[:, j, h, :], src, ACT.Exp, bias=neg_max[:, j, h:h + 1])
                        op.then_inc(exp_done, 1)

                def slot(t):
                    ahead, prev, prev2 = t.plus(1), t.plus(-1), t.plus(-2)
                    for q in range(NQ):
                        if q == 0 and ahead.within(NB):
                            n = 2 if kv is not None else 1
                            wait(act, tr_done, ahead, 1, 1)
                            act.activation(xkT[:, 0:n, :], PROJ[:, 0:n * P], ACT.Copy).then_inc(xkT_ready, 1)
                        b, j = scored_at(t, q)
                        if topk and b.within(NB):
                            wait(act, s_done, b, NQ, j + 1)
                            if halved:
                                act.activation(s_neg[:, j, :, :],
                                               S[j % 2][:].rearrange("p (h k) -> p h k", h=QH)[:, :, HALF:],
                                               ACT.Copy, scale=-1.0)
                            act.activation(s_sb[:, j, :, :], S[j % 2][:], ACT.Copy).then_inc(s_copied, 1)
                        if q == 3 and ahead.within(NB) and not scrambled:
                            v_by_head(ahead)
                        if q == 1 and ahead.within(NB) and in_parts:
                            wait(act, proj_done, ahead, 1, 1)
                            wait(act, kbd_ready, t, NQ, NQ)
                            for dst in (qk, qk_hi[:, ahead.par]):
                                act.activation(dst[:, 0, :], PROJ[:, 0:P], ACT.Identity, bias=bq_s[:], scale=scale)\
                                    .then_inc(qk_ready, 1)
                                act.activation(dst[:, 1, :], PROJ[:, P:2 * P], ACT.Identity, bias=bcol[:, 1:2])\
                                    .then_inc(qk_ready, 1)
                        if not halved:
                            exponentials(t, q)
                        b, j = (t, q - 2) if q >= 2 else (prev, q + 2)
                        if topk and b.within(NB):
                            wait(act, pt_done, b, NQ, j + 1)
                            p, n = (b, j - 2) if j >= 2 else (b.plus(-1), j + 2)
                            wait(act, pv_done, p, NQ, n + 1)
                            act.activation(pT[:, j % 2, :, :], PT[j % 2][:], ACT.Copy).then_inc(pT_ready, 1)
                        if q == (2 if scrambled else 0) and prev2.within(NB):
                            wait(act, ont_done, prev2, 1, 1)
                            if scrambled:
                                op = act.activation(oT[:], Y[:, 0:P], ACT.Copy)
                            elif gates is not None:
                                op = act.activation(oT[:], Y[:, 0:P], ACT.Identity, bias=bv_g[:], scale=bcol[:, 3:4])
                            else:
                                op = act.activation(oT[:], Y[:, 0:P], ACT.Identity, bias=bcol[:, 2:3])
                            op.then_inc(oT_ready, 1)
                        if q == 1 and ahead.within(NB) and not in_parts:
                            wait(act, proj_done, ahead, 1, 1)
                            if scrambled:
                                act.activation(lin[:, 0, :], PROJ[:, 0:P], ACT.Identity, bias=bq_s[:], scale=scale)\
                                    .then_inc(qk_ready, 1)
                                for n in (1, 2):
                                    act.activation(lin[:, n, :], PROJ[:, P * n:P * n + P], ACT.Identity,
                                                   bias=bcol[:, n:n + 1]).then_inc(qk_ready, 1)
                                token_order(prev2)
                                exponentials(t, q)
                                wait(act, pick_done, ahead, 4, 1)
                                act.activation(q32[:, ahead.par, :, :], PROJ[:], ACT.Copy).then_inc(picked, 1)
                            else:
                                act.activation(q_t[:, ahead.par, :], PROJ[:, 0:P], ACT.Identity,
                                               bias=bq_s[:], scale=scale).then_inc(qk_ready, 1)
                                wait(act, kbd_ready, t, NQ, NQ)
                                act.activation(k_t[:], PROJ[:, P:2 * P], ACT.Identity, bias=bcol[:, 1:2])\
                                    .then_inc(qk_ready, 1)
                        elif q == 1 and scrambled:
                            token_order(prev2)
                            exponentials(t, q)
                        if q != 1 and halved:
                            exponentials(t, q)
                        if q == 2 and scrambled and ahead.within(NB):
                            wait(act, pick_done, ahead, 4, 2)
                            wait(act, kbd_ready, t, NQ, NQ)
                            act.activation(k32[:], PROJ[:], ACT.Copy).then_inc(picked, 1)
                        if q == 2 and prev.within(NB):
                            wait(act, pv_done, prev, NQ, NQ)
                            wait(act, ot_done, prev2, 1, 1)
                            act.activation(o_raw[:], O[:], ACT.Copy).then_inc(o_copied, 1)
                        if q == 3 and ahead.within(NB) and scrambled:
                            v_by_head(ahead)

                act.wait_ge(set_act, n_set_act)
                act.wait_ge(set_pool, 3)
                slots(act, slot, NB)

            @block.vector
            def _(dve):
                steps = [0]
                found_by = [0]

                def own(ins):
                    ins.then_inc(chain, 1)
                    steps[0] += 1
                    return steps[0]

                if scrambled:
                    dve.wait_ge(set_pool, 5)
                    dve.tensor_copy(pick[:, :, 0:HD], c.ident[:].rearrange("p (r d) -> p r d", r=H)).then_inc(set_dve, 1)
                    dve.tensor_reduce(rowmask[:], c.ident[:].rearrange("p (t r) -> p r t", t=HD), AX.X, ALU.add)\
                        .then_inc(set_dve, 1)
                    for hh in range(4):
                        op = dve.tensor_reduce(place[:, hh, HD * hh:HD * hh + HD],
                                               c.ident[:].rearrange("p (t r) -> p t r", t=HD), AX.X, ALU.add)
                        if hh >= 2:
                            op.then_inc(set_dve, 1)

                if rel_bias is not None:
                    dve.wait_ge(table_turned, 1)
                    dve.tensor_copy(rows_sb[:, 0:LO], Y[0:H, R - LO:R]).then_inc(rows_ready, 1)
                    dve.tensor_copy(rows_sb[:, LO:LO + R], Y[0:H, 0:R]).then_inc(rows_ready, 1)
                    dve.tensor_copy(rows_sb[:, LO + R:], Y[0:H, R - 1:R].to_broadcast([H, LO])).then_inc(rows_ready, 1)

                def top_k(b, j):
                    wait(dve, s_copied, b, NQ, j + 1)
                    dve.sem_inc(quad_begun, 1)
                    replaced = [0] * QH
                    for r in range(ROUNDS):
                        found = []
                        for h in range(QH):
                            src = work if r else s_sb
                            if r:
                                dve.wait_ge(chain, replaced[h])
                            op = dve.max(top8[:, j, h, r, :], src[:, j, h, :])
                            if r == ROUNDS - 1 and h == QH - 1:
                                op.then_inc(top_ready, 1)
                            else:
                                found.append(own(op))
                        if r == ROUNDS - 1:
                            break
                        for h in range(QH):
                            dve.wait_ge(chain, found[h])
                            op = dve.match_replace(out=work[:, j, h, :], in_to_replace=top8[:, j, h, r, :],
                                                   in_values=(work if r else s_sb)[:, j, h, :], imm_value=TAKEN)
                            replaced[h] = own(op)
                        if r == 0:
                            dve.tensor_scalar(neg_max[:, j, :], top8[:, j, :, 0, 0], -1.0, None, ALU.mult)\
                                .then_inc(max_ready, 1)

                def normalise(b):
                    wait(dve, ot_done, b, 1, 1)
                    o4 = OT[:].rearrange("p (h e) -> p h e", h=H)
                    n = own(dve.reciprocal(r_sum[:], o4[:, :, HD]))
                    dve.wait_ge(chain, n)
                    dve.tensor_tensor(o_n[:].rearrange("p (h d) -> p h d", h=H), o4[:, :, 0:HD],
                                      bcast(r_sum[:], 2, HD), ALU.mult).then_inc(on_ready, 1)

                def layer_norm(t, q):
                    b = t.plus(-2)
                    if q == 2 and b.within(NB):
                        wait(dve, y_done, b, 1, 1)
                        if not add_on_pe:
                            wait(dve, x_bo_ready, b, 1, 1)
                            wait(dve, x_ready, b.plus(-1), 1, 1)
                            dve.tensor_tensor(x_sum[:], Y[:, 0:P], x_bo[:], ALU.add).then_inc(x_summed, 1)
                            wait(dve, x_summed, b, 1, 1)
                        n = own(dve.bn_stats(stats[:], Y[:, 0:P] if add_on_pe else x_sum[:]))
                        dve.wait_ge(chain, n)
                        dve.bn_aggr(mv[:], stats[:]).then_inc(stats_ready, 1)
                    if in_parts:
                        if q == 0 and t.plus(-3).within(NB):
                            apply(t.plus(-3))
                        if q == 3 and t.reg is None and t.off == NB + 1:
                            apply(b)
                    elif q == 3 and b.within(NB):
                        apply(b)

                def apply(b):
                    wait_par(dve, stored, b.plus(-2), 16)
                    wait(dve, rstd_ready, b, 1, 1)
                    dve.tensor_scalar(x_new[:, b.par, :], Y[:, 0:P] if add_on_pe else x_sum[:], mv[:, 0:1],
                                      rstd[:, 0:1], ALU.subtract, ALU.mult).then_inc(x_ready, 1)

                def halve(b, j, last):
                    wait(dve, s_copied, b, NQ, j + 1)
                    dve.sem_inc(quad_begun, 1)
                    first, second = s_sb[:, j, :, 0:HALF], s_sb[:, j, :, HALF:]
                    own(dve.tensor_tensor(pairs[:, j % 2, 0, :, :], first, second, ALU.min))
                    if last is not None:
                        if found_by[0]:
                            dve.wait_ge(chain, found_by[0])
                        n = own(compare())
                    hi = own(dve.scalar_tensor_tensor(out=pairs[:, j % 2, 1, :, :], in0=first, scalar=-1.0,
                                                      in1=s_neg[:, j, :, :], op0=ALU.mult, op1=ALU.min))
                    if last is not None:
                        dve.wait_ge(chain, n)
                        n = own(edges(last[1]))
                    dve.wait_ge(chain, hi)
                    neg = own(dve.tensor_reduce(neg_max[:, j, :], pairs[:, j % 2, 1, :, :], AX.X, ALU.min))
                    if last is not None:
                        dve.wait_ge(chain, n)
                        find_ties(last[1])
                    chains = [(x, h) for x in range(2) for h in range(QH)]
                    replaced = {k: hi for k in chains}
                    for r in range(BEST // 8):
                        found = {}
                        for x, h in chains:
                            dve.wait_ge(chain, replaced[x, h])
                            found[x, h] = own(dve.max(best[:, x, h, 8 * r:8 * r + 8], pairs[:, j % 2, x, h, :]))
                        if r == 0:
                            dve.wait_ge(chain, neg)
                        if r < BEST // 8 - 1:
                            for x, h in chains:
                                dve.wait_ge(chain, found[x, h])
                                replaced[x, h] = own(dve.match_replace(
                                    out=pairs[:, j % 2, x, h, :], in_to_replace=best[:, x, h, 8 * r:8 * r + 8],
                                    in_values=pairs[:, j % 2, x, h, :], imm_value=TAKEN))
                        if r == 0 and last is not None:
                            read_ties(*last)
                        if r == 1 and last is not None:
                            settle_ties(*last)
                        if r == 2:
                            layer_norm(b, j)
                    found_by[0] = found[chains[-1]]

                def compare():
                    return dve.scalar_tensor_tensor(out=cut[:], in0=best[:, ::-1, :, :], scalar=-1.0, in1=best[:],
                                                    op0=ALU.mult, op1=ALU.max)

                def edges(j):
                    return dve.tensor_reduce(edge[:, j, :, :], cut[:], AX.X, ALU.min)

                def find_ties(j):
                    dve.scalar_tensor_tensor(out=tied[:], in0=edge[:, j, 1, :], scalar=-1.0, in1=edge[:, j, 0, :],
                                             op0=ALU.mult, op1=ALU.is_equal).then_inc(tied_ready, 1)

                def read_ties(b, j):
                    wait(dve, ties_counted, b, NQ, j + 1)
                    dve.tensor_reduce(tie_count[:], Y[0:1, TIES], AX.X, ALU.max).then_inc(ties_read, 1)

                def settle_ties(b, j):
                    wait(dve, ties_read, b, NQ, j + 1)
                    dve.sem_inc(ties_seen, 1)
                    ties = dve.value_load(tie_count[:])
                    with dve.If(ties > 0):
                        steps_done = 0
                        for r in range(ROUNDS):
                            for h in range(QH):
                                dve.max(top8[:, h, :], (work[:, h, :] if r else s_sb[:, j, h, :])).then_inc(redone, 1)
                            steps_done += QH
                            dve.wait_ge(redone, steps_done)
                            for h in range(QH):
                                dve.match_replace(out=work[:, h, :], in_to_replace=top8[:, h, :],
                                                  in_values=(work[:, h, :] if r else s_sb[:, j, h, :]),
                                                  imm_value=TAKEN).then_inc(redone, 1)
                            steps_done += QH
                            dve.wait_ge(redone, steps_done)
                        dve.tensor_scalar(work[:], work[:], 0.5 * TAKEN, TAKEN, ALU.is_ge, ALU.mult).then_inc(redone, 1)
                        dve.wait_ge(redone, steps_done + 1)
                        dve.tensor_tensor(s_sb[:, j, :, :], s_sb[:, j, :, :], work[:], ALU.add).then_inc(redone, 1)
                        dve.wait_ge(redone, steps_done + 2)
                        dve.sem_clear(redone)
                    dve.sem_inc(top_ready, 1)

                def slot(t):
                    prev, prev2 = t.plus(-1), t.plus(-2)
                    if steps[0]:
                        dve.wait_ge(chain, steps[0])
                        dve.sem_clear(chain)
                    steps[0] = 0
                    found_by[0] = 0
                    if mask is not None and t.plus(1).within(NB):
                        b = t.plus(1)
                        wait_par(dve, tok_in, b, 16 * tok_dmas)
                        wait(dve, s_done, prev, NQ, NQ)
                        dve.scalar_tensor_tensor(out=m_add[:, b.par, :], in0=m_raw[:, b.par, :], scalar=1.0,
                                                 in1=c.causal[:], op0=ALU.subtract, op1=ALU.min)\
                            .then_inc(m_ready, 1)
                    for q in range(NQ):
                        if q == 0 and prev2.within(NB):
                            normalise(prev2)
                        if topk and not (halved and t.within(NB)):
                            layer_norm(t, q)
                        last = (t, q - 1) if q else (prev, NQ - 1)
                        if halved and t.within(NB):
                            halve(t, q, last if last[0].within(NB) else None)
                        elif halved and last[0].within(NB):
                            n = own(compare())
                            dve.wait_ge(chain, n)
                            n = own(edges(last[1]))
                            dve.wait_ge(chain, n)
                            find_ties(last[1])
                            read_ties(*last)
                            settle_ties(*last)
                        elif t.within(NB) and topk:
                            top_k(t, q)
                        elif t.within(NB) and not topk:
                            wait(dve, s_done, t, NQ, q + 1)
                            dve.tensor_reduce(neg_max[:, q, :], S[q % 2][:].rearrange("p (h k) -> p h k", h=QH),
                                              AX.X, ALU.max, negate=True).then_inc(max_ready, 1)
                        b, j = (t, q - 2) if q >= 2 else (prev, q + 2)
                        if not topk and b.within(NB):
                            wait(dve, pt_done, b, NQ, j + 1)
                            p, n = (b, j - 2) if j >= 2 else (b.plus(-1), j + 2)
                            wait(dve, pv_done, p, NQ, n + 1)
                            dve.tensor_copy(pT[:, j % 2, :, :], PT[j % 2][:]).then_inc(pT_ready, 1)
                        if not topk:
                            layer_norm(t, q)

                slots(dve, slot, NB)

        clear(nc, sems)


class ExpertWeights:

    def __init__(self, nc, ctx, name, wgate, wup, wdown):
        E, _, F = wgate.shape
        NC = E * F // P
        self.E, self.F = E, F
        self.gate = ctx.enter_context(nc.sbuf_tensor(f"{name}_w_gate", [P, E, F], F32))
        self.up = ctx.enter_context(nc.sbuf_tensor(f"{name}_w_up", [P, E, F], F32))
        self.down = ctx.enter_context(nc.sbuf_tensor(f"{name}_w_down", [P, NC, P], F32))
        self.loaded = ctx.enter_context(nc.semaphore(f"{name}_w_loaded"))
        self.sources = wgate, wup, wdown

    def load(self, sp):
        wgate, wup, wdown = self.sources
        sp.dma_start(self.gate[:], wgate.rearrange("e d f -> d e f")).then_inc(self.loaded, 16)
        sp.dma_start(self.up[:], wup.rearrange("e d f -> d e f")).then_inc(self.loaded, 16)
        sp.dma_start(self.down[:], wdown.rearrange("e f d -> (e f) d").rearrange("(c p) d -> p c d", p=P))\
            .then_inc(self.loaded, 16)


def experts(nc, name, c, x, out, router, weights, *, renormalise):
    NB = x.shape[0]
    TB = 4
    NT = NB // TB
    TW = TB * P
    E, F = weights.E, weights.F
    NC = E * F // P
    PER = F // P if F % P == 0 else 1
    SPAN = P if F % P == 0 else F
    NW = NC // PER
    PARTS = 3
    with ExitStack() as ctx:
        def sb(nm, shape, dt=F32):
            return ctx.enter_context(nc.sbuf_tensor(f"{name}_{nm}", shape, dt))

        sems = []

        def sem(nm):
            sems.append(ctx.enter_context(nc.semaphore(f"{name}_{nm}")))
            return sems[-1]

        w_router = sb("w_router", [P, E])
        gate_hi = sb("gate_hi", [P, E * F], F32R)
        up_hi = sb("up_hi", [P, E * F], F32R)
        down_hi = sb("down_hi", [P, NC * P], F32R)
        gate_lo = sb("gate_lo", [P, E * F], F32R)
        up_lo = sb("up_lo", [P, E * F], F32R)
        down_lo = sb("down_lo", [P, NC * P], F32R)
        x_all = sb("x_all", [P, NB, P])
        xT_hi = sb("xT_hi", [P, NT, TW], F32R)
        xT_lo = sb("xT_lo", [P, NT, TW], F32R)
        wT = sb("wT", [32 * PARTS, NT, TW], BF16)
        spread = sb("spread", [32 * PARTS, NW, P], BF16)

        def by_fours(tokens):
            return tokens.rearrange("b t d -> (b t) d").rearrange("(p s) d -> p s d", s=TB)

        x_in = [sem(f"x_in{u}") for u in range(NT)]
        stored = [sem("stored0"), sem("stored1")]
        router_in = sem("router_in")

        halves = [(weights.gate[:].rearrange("p e f -> p (e f)"), gate_hi, gate_lo),
                  (weights.up[:].rearrange("p e f -> p (e f)"), up_hi, up_lo),
                  (weights.down[:].rearrange("p c d -> p (c d)"), down_hi, down_lo)]

        with ExitStack() as rctx:
            def rsb(nm, shape, dt=F32):
                return rctx.enter_context(nc.sbuf_tensor(f"{name}_{nm}", shape, dt))

            xT_all = rsb("xT_all", [P, NT, TW])
            logit = rsb("logit", [P, NB, E])
            prob = rsb("prob", [P, NB, E])
            order = rsb("order", [P, E])
            best = rsb("best", [P, 2, NB])
            hit = rsb("hit", [P, 2, NB, E])
            rank = rsb("rank", [P, NB, E])
            red = rsb("red", [P, NB])
            gap = rsb("gap", [P, NB])
            share = rsb("share", [P, 2, NB])
            weight = rsb("weight", [P, NB, E])
            part = rsb("part", [P, NB, PARTS, 32], BF16)
            identb = rsb("identb", [P, P], BF16)
            XT = c.banks[0:2]
            LG = c.banks[2]
            WT = [b[:].bitcast(BF16) for b in c.banks[3:7]]
            t_done = sem("t_done")
            t_copied = sem("t_copied")
            hi_ready = sem("hi_ready")
            lo_ready = sem("lo_ready")
            w_hi_ready = sem("w_hi_ready")
            w_lo_ready = sem("w_lo_ready")
            lg_done = sem("lg_done")
            shifted = sem("shifted")
            expd = sem("expd")
            gap_ready = sem("gap_ready")
            gap_expd = sem("gap_expd")
            step = sem("step")
            part_ready = sem("part_ready")
            wt_done = sem("wt_done")
            wt_copied = sem("wt_copied")
            base_set = sem("base_set")
            WB_PER = 1024 // P
            NWT = (NB + WB_PER - 1) // WB_PER

            with nc.Block() as block:
                @block.sync
                def _(sp):
                    with nc.allow_non_contiguous_dma("4 KB, once"):
                        sp.dma_start(w_router[:].unsqueeze(2), router.unsqueeze(2)).then_inc(router_in, 16)
                    for u in range(NT):
                        sp.dma_start(x_all[:, TB * u:TB * u + TB, :],
                                     by_fours(x[TB * u:TB * u + TB])).then_inc(x_in[u], 16)

                @block.gpsimd
                def _(pool):
                    pool.memset(spread[:], 0.0).then_inc(base_set, 1)
                    pool.memset(part[:], 0.0).then_inc(base_set, 1)
                    pool.iota(order[:], pattern=[[-1, E]], base=E, channel_multiplier=0,
                              allow_small_or_imprecise_dtypes=True).then_inc(base_set, 1)
                    pool.wait_ge(base_set, 3)
                    first = spread[0:E]
                    pool.memset(first, 1.0).then_inc(base_set, 1)
                    pool.wait_ge(base_set, 4)
                    pool.affine_select(out=first, in_=first, compare_op=ALU.is_ge, fill=0.0,
                                       base=0, pattern=[[P, NW], [1, P]], channel_multiplier=-SPAN).then_inc(base_set, 1)
                    pool.wait_ge(base_set, 5)
                    pool.affine_select(out=first, in_=first, compare_op=ALU.is_ge, fill=0.0,
                                       base=SPAN - 1, pattern=[[-P, NW], [-1, P]], channel_multiplier=SPAN)\
                        .then_inc(base_set, 1)
                    for u in range(NT):
                        pool.wait_ge(hi_ready, u + 1)
                        pool.tensor_tensor(xT_lo[:, u, :], xT_all[:, u, :], xT_hi[:, u, :].bitcast(F32), ALU.subtract)\
                            .then_inc(lo_ready, 1)

                @block.tensor
                def _(pe):
                    for u in range(NT):
                        pe.wait_ge(x_in[u], 16)
                        if u >= 2:
                            pe.wait_ge(t_copied, u - 1)
                        for s in range(TB):
                            mm = pe.transpose(XT[u % 2][:, P * s:P * s + P], x_all[:, TB * u + s, :], c.ident[:])
                        mm.then_inc(t_done, 1)
                    pe.wait_ge(router_in, 16)
                    for b in range(NB):
                        if b % TB == 0:
                            pe.wait_ge(t_copied, b // TB + 1)
                        mm = pe.matmul(LG[:, E * b:E * b + E], xT_all[:, b // TB, P * (b % TB):P * (b % TB) + P],
                                       w_router[:], start=True, stop=True)
                    mm.then_inc(lg_done, 1)
                    pe.wait_ge(part_ready, PARTS)
                    for b in range(NB):
                        mm = pe.transpose(WT[b // WB_PER][0:32 * PARTS, P * (b % WB_PER):P * (b % WB_PER) + P],
                                          part[:, b, :, :].rearrange("p n e -> p (n e)"), identb[:])
                    mm.then_inc(wt_done, 1)

                @block.scalar
                def _(act):
                    act.wait_ge(weights.loaded, 48)
                    for w, hi, _ in halves:
                        act.activation(hi[:], w, ACT.Copy).then_inc(w_hi_ready, 1)
                    for u in range(NT):
                        act.wait_ge(t_done, u + 1)
                        act.activation(xT_all[:, u, :], XT[u % 2][:], ACT.Copy).then_inc(t_copied, 1)
                    act.wait_ge(shifted, 1)
                    act.activation(prob[:], logit[:], ACT.Exp).then_inc(expd, 1)
                    if renormalise:
                        act.wait_ge(gap_ready, 1)
                        act.activation(share[:, 1, :], gap[:], ACT.Exp).then_inc(gap_expd, 1)
                    act.wait_ge(wt_done, 1)
                    flat = wT[:].rearrange("p u t -> p (u t)")
                    for n in range(1, NWT, 2):
                        w = min(1024, NB * P - 1024 * n)
                        act.activation(flat[:, 1024 * n:1024 * n + w], WT[n][0:32 * PARTS, 0:w], ACT.Copy)\
                            .then_inc(wt_copied, 1)

                @block.vector
                def _(dve):
                    steps = [0]

                    def then(ins):
                        ins.then_inc(step, 1)
                        steps[0] += 1
                        dve.wait_ge(step, steps[0])

                    def rows(ap):
                        return bcast(ap, 2, E)

                    then(dve.tensor_copy(identb[:], c.ident[:]))
                    for n, (w, hi, lo) in enumerate(halves):
                        dve.wait_ge(w_hi_ready, n + 1)
                        dve.tensor_tensor(lo[:], w, hi[:].bitcast(F32), ALU.subtract).then_inc(w_lo_ready, 1)
                    for u in range(NT):
                        dve.wait_ge(t_copied, u + 1)
                        dve.tensor_copy(xT_hi[:, u, :], xT_all[:, u, :]).then_inc(hi_ready, 1)
                    dve.wait_ge(lg_done, 1)
                    lg = LG[:, 0:NB * E].rearrange("p (b e) -> p b e", b=NB)
                    then(dve.tensor_reduce(red[:], lg, AX.X, ALU.max))
                    dve.tensor_tensor(logit[:], lg, rows(red[:]), ALU.subtract).then_inc(shifted, 1)
                    dve.wait_ge(expd, 1)
                    then(dve.tensor_reduce(red[:], prob[:], AX.X, ALU.add))
                    then(dve.reciprocal(red[:], red[:]))
                    then(dve.tensor_tensor(prob[:], prob[:], rows(red[:]), ALU.mult))
                    dve.wait_ge(base_set, 6)
                    src = prob
                    for n in range(2):
                        then(dve.tensor_reduce(best[:, n, :], src[:], AX.X, ALU.max))
                        then(dve.tensor_tensor(rank[:], src[:], rows(best[:, n, :]), ALU.is_equal))
                        then(dve.tensor_tensor(rank[:], rank[:], bcast(order[:], 1, NB), ALU.mult))
                        then(dve.tensor_reduce(red[:], rank[:], AX.X, ALU.max))
                        then(dve.tensor_tensor(hit[:, n], rank[:], rows(red[:]), ALU.is_equal))
                        if n == 0:
                            then(dve.scalar_tensor_tensor(out=logit[:], in0=hit[:, 0], scalar=-2.0, in1=prob[:],
                                                          op0=ALU.mult, op1=ALU.add))
                            src = logit
                    if renormalise:
                        dve.tensor_tensor(gap[:], best[:, 1, :], best[:, 0, :], ALU.subtract).then_inc(gap_ready, 1)
                        dve.wait_ge(gap_expd, 1)
                        then(dve.tensor_scalar(red[:], share[:, 1, :], 1.0, None, ALU.add))
                        then(dve.reciprocal(share[:, 0, :], red[:]))
                        then(dve.tensor_tensor(share[:, 1, :], share[:, 1, :], share[:, 0, :], ALU.mult))
                    two = share if renormalise else best
                    then(dve.tensor_tensor(weight[:], hit[:, 0], rows(two[:, 0, :]), ALU.mult))
                    then(dve.tensor_tensor(rank[:], hit[:, 1], rows(two[:, 1, :]), ALU.mult))
                    then(dve.tensor_tensor(weight[:], weight[:], rank[:], ALU.add))
                    for n in range(PARTS):
                        dve.tensor_copy(part[:, :, n, 0:E], weight[:]).then_inc(part_ready, 1)
                        if n < PARTS - 1:
                            dve.wait_ge(part_ready, n + 1)
                            then(dve.tensor_tensor(weight[:], weight[:], part[:, :, n, 0:E], ALU.subtract))
                    for n in range(1, PARTS):
                        then(dve.tensor_copy(spread[32 * n:32 * n + E], spread[0:E]))
                    dve.wait_ge(wt_done, 1)
                    flat = wT[:].rearrange("p u t -> p (u t)")
                    for n in range(NWT):
                        w = min(1024, NB * P - 1024 * n)
                        if n % 2 == 0:
                            dve.tensor_copy(flat[:, 1024 * n:1024 * n + w], WT[n][0:32 * PARTS, 0:w])\
                                .then_inc(wt_copied, 1)

        silu = sb("silu", [P, 2, TW])
        prod = sb("prod", [P, 2, TW])
        hid = sb("hid", [P, 2, TW])
        hid_hi = sb("hid_hi", [P, 2, TW], F32R)
        hid_lo = sb("hid_lo", [P, 2, TW], F32R)
        oT = sb("oT", [P, TW])
        z = sb("z", [P, TB, P])
        stats = sb("stats", [P, TB, 6])
        mv = sb("mv", [P, TB, 2])
        var_eps = sb("var_eps", [P, TB])
        rstd = sb("rstd", [P, TB])
        x_new = sb("x_new", [P, 2, TB, P])
        G, U, WB = c.banks[0:2], c.banks[2:4], c.banks[4:6]
        OUT, TOK = c.banks[6], c.banks[7]
        g_done = sem("g_done")
        u_done = sem("u_done")
        wb_done = sem("wb_done")
        d_done = sem("d_done")
        tok_done = sem("tok_done")
        silu_ready = sem("silu_ready")
        out_copied = sem("out_copied")
        prod_ready = sem("prod_ready")
        hid_ready = sem("hid_ready")
        hid_hi_ready = sem("hid_hi_ready")
        hid_lo_ready = sem("hid_lo_ready")
        z_ready = sem("z_ready")
        stats_ready = sem("stats_ready")
        x_ready = sem("x_ready")
        var_ready = sem("var_ready")
        rstd_ready = sem("rstd_ready")
        chain = sem("chain")

        def pairs(eng, body, tail=None):
            body(Batch(0))
            if NT > 2:
                with eng.Fori(0, NT // 2 - 1) as i:
                    body(Batch(1, i, 1))
            if tail:
                tail(Batch(NT // 2 - 1))

        def has_previous(pair):
            return pair.reg is not None

        def before(eng, sem, pair, each, n):
            if pair.reg is not None or n > 0:
                eng.wait_ge(sem, pair.count(each, n))

        def tile(pair, par):
            return 2 * pair.off + par if pair.reg is None else pair.reg * 2 + (2 * pair.off + par)

        with nc.Block() as block:
            @block.sync
            def _(sp):
                sp.sem_inc(stored[1], 16)

                def body(pair):
                    for par in range(2):
                        u = tile(pair, par)
                        before(sp, x_ready, pair, 2, par + 1)
                        sp.dma_start(by_fours(out[bass.ds(u * TB, TB)]), x_new[:, par])\
                            .then_inc(stored[par], 16)

                pairs(sp, body)
                for par in range(2):
                    sp.wait_ge(stored[par], 16 * (NT // 2 + par))

            @block.gpsimd
            def _(pool):
                def inverse_std(pair, par):
                    before(pool, stats_ready, pair, 2, par + 1)
                    pool.tensor_tensor(var_eps[:], mv[:, :, 1], c.eps[:].to_broadcast([P, TB]), ALU.add)\
                        .then_inc(var_ready, 1)
                    before(pool, var_ready, pair, 2, par + 1)
                    pool.tensor_tensor(rstd[:], var_eps[:], c.minushalf[:].to_broadcast([P, TB]), ALU.pow)\
                        .then_inc(rstd_ready, 1)

                def body(pair):
                    for n in range(2 * NC):
                        par, k = divmod(n, NC)
                        before(pool, hid_hi_ready, pair, 2 * NC, n + 1)
                        pool.tensor_tensor(hid_lo[:, n % 2, :], hid[:, n % 2, :], hid_hi[:, n % 2, :].bitcast(F32),
                                           ALU.subtract).then_inc(hid_lo_ready, 1)
                        if k == 6 and par == 1:
                            inverse_std(pair, 0)
                        if k == 6 and par == 0 and has_previous(pair):
                            inverse_std(pair.plus(-1), 1)

                pairs(pool, body, lambda pair: inverse_std(pair, 1))

            @block.tensor
            def _(pe):
                def product(dst, hi, lo, cols, v_hi, v_lo, start, stop):
                    pe.matmul(dst, hi[:, cols], v_hi, start=start, stop=False)
                    pe.matmul(dst, hi[:, cols], v_lo, start=False, stop=False)
                    return pe.matmul(dst, lo[:, cols], v_hi, start=False, stop=stop)

                def down(pair, n):
                    k = n % NC
                    before(pe, hid_lo_ready, pair, 2 * NC, n + 1)
                    if k == 0:
                        before(pe, out_copied, pair, 2, n // NC)
                    product(OUT[:], down_hi, down_lo, slice(P * k, P * k + P), hid_hi[:, n % 2, :], hid_lo[:, n % 2, :],
                            k == 0, k == NC - 1).then_inc(d_done, 1)

                def to_tokens(pair, par):
                    before(pe, out_copied, pair, 2, par + 1)
                    before(pe, z_ready, pair, 2, par)
                    for s in range(TB):
                        mm = pe.transpose(TOK[:, P * s:P * s + P], oT[:, P * s:P * s + P], c.ident[:])
                    mm.then_inc(tok_done, 1)

                def body(pair):
                    for n in range(2 * NC):
                        par, k = divmod(n, NC)
                        cols = slice(P * k, P * k + P)
                        x_hi, x_lo = xT_hi[:, tile(pair, par), :], xT_lo[:, tile(pair, par), :]
                        before(pe, silu_ready, pair, 2 * NC, n - 1)
                        product(G[n % 2][:], gate_hi, gate_lo, cols, x_hi, x_lo, True, True).then_inc(g_done, 1)
                        before(pe, prod_ready, pair, 2 * NC, n - 1)
                        product(U[n % 2][:], up_hi, up_lo, cols, x_hi, x_lo, True, True).then_inc(u_done, 1)
                        if k % PER == 0:
                            w = k // PER
                            m = par * NW + w
                            pm = m - 2
                            last = (pm // NW) * NC + (pm % NW) * PER + PER - 1
                            before(pe, hid_ready, pair, 2 * NC, last + 1)
                            pe.matmul(WB[m % 2][:], spread[:, w, :], wT[:, tile(pair, par), :],
                                      start=True, stop=True).then_inc(wb_done, 1)
                        if n >= 2:
                            down(pair, n - 2)
                        elif has_previous(pair):
                            down(pair.plus(-1), 2 * NC + n - 2)
                        if k == 3 and par == 1:
                            to_tokens(pair, 0)
                        if k == 3 and par == 0 and has_previous(pair):
                            to_tokens(pair.plus(-1), 1)

                def tail(pair):
                    down(pair, 2 * NC - 2)
                    down(pair, 2 * NC - 1)
                    to_tokens(pair, 1)

                pairs(pe, body, tail)

            @block.scalar
            def _(act):
                def copy_out(pair, par):
                    before(act, d_done, pair, 2 * NC, NC * (par + 1))
                    before(act, tok_done, pair, 2, par)
                    act.activation(oT[:], OUT[:], ACT.Copy).then_inc(out_copied, 1)

                def high_part(pair, n):
                    before(act, hid_ready, pair, 2 * NC, n + 1)
                    before(act, d_done, pair, 2 * NC, n - 1)
                    act.activation(hid_hi[:, n % 2, :], hid[:, n % 2, :], ACT.Copy).then_inc(hid_hi_ready, 1)

                def body(pair):
                    for n in range(2 * NC):
                        if n == NC + 2:
                            copy_out(pair, 0)
                        if n == 2 and has_previous(pair):
                            copy_out(pair.plus(-1), 1)
                        before(act, g_done, pair, 2 * NC, n + 1)
                        before(act, prod_ready, pair, 2 * NC, n - 1)
                        act.activation(silu[:, n % 2, :], G[n % 2][:], ACT.Silu).then_inc(silu_ready, 1)
                        if n:
                            high_part(pair, n - 1)
                        elif has_previous(pair):
                            high_part(pair.plus(-1), 2 * NC - 1)

                def tail(pair):
                    high_part(pair, 2 * NC - 1)
                    copy_out(pair, 1)

                pairs(act, body, tail)

            @block.vector
            def _(dve):
                def finish(pair, par, parts):
                    if 0 in parts:
                        before(dve, tok_done, pair, 2, par + 1)
                        dve.tensor_tensor(z[:], TOK[:].rearrange("p (b d) -> p b d", b=TB),
                                          x_all[:, bass.ds(tile(pair, par) * TB, TB), :], ALU.add).then_inc(z_ready, 1)
                    if 1 in parts:
                        before(dve, z_ready, pair, 2, par + 1)
                        for s in range(TB):
                            dve.bn_stats(stats[:, s, :], z[:, s, :]).then_inc(chain, 1)
                    if 2 in parts:
                        for s in range(TB):
                            dve.wait_ge(chain, s + 1)
                            op = dve.bn_aggr(mv[:, s, :], stats[:, s, :])
                            if s == TB - 1:
                                op.then_inc(stats_ready, 1)
                            else:
                                op.then_inc(chain, 1)
                    if 3 in parts:
                        before(dve, rstd_ready, pair, 2, par + 1)
                        if par == 1 or pair.reg is not None:
                            dve.wait_ge(stored[par], pair.count(16, 16 * par))
                        for s in range(TB):
                            op = dve.tensor_scalar(x_new[:, par, s, :], z[:, s, :], mv[:, s, 0:1], rstd[:, s:s + 1],
                                                   ALU.subtract, ALU.mult)
                        op.then_inc(x_ready, 1)
                        dve.wait_ge(chain, 2 * TB - 1)
                        dve.sem_clear(chain)

                def body(pair):
                    for n in range(2 * NC):
                        par, k = divmod(n, NC)
                        before(dve, silu_ready, pair, 2 * NC, n + 1)
                        before(dve, u_done, pair, 2 * NC, n + 1)
                        before(dve, hid_ready, pair, 2 * NC, n - 1)
                        dve.tensor_tensor(prod[:, n % 2, :], silu[:, n % 2, :], U[n % 2][:], ALU.mult)\
                            .then_inc(prod_ready, 1)
                        before(dve, prod_ready, pair, 2 * NC, n + 1)
                        m = par * NW + k // PER
                        before(dve, wb_done, pair, 2 * NW, m + 1)
                        before(dve, hid_lo_ready, pair, 2 * NC, n - 1)
                        dve.tensor_tensor(hid[:, n % 2, :], prod[:, n % 2, :], WB[m % 2][:], ALU.mult)\
                            .then_inc(hid_ready, 1)
                        part = {4: 0, 5: 1, 6: 2, 8: 3}.get(k)
                        if part is not None and par == 1:
                            finish(pair, 0, [part])
                        if part is not None and par == 0 and has_previous(pair):
                            finish(pair.plus(-1), 1, [part])

                pairs(dve, body, lambda pair: finish(pair, 1, range(4)))

        clear(nc, sems)


def decoder(nc, a, out):
    NB = a["x"].shape[0]
    hop = [nc.dram_tensor(f"x_after_{n}", (NB, P, P), F32, kind="Internal").ap() for n in range(5)]
    R = a["L0_attn_rel_bias"].shape[0]
    bias_rows = nc.dram_tensor("bias_rows", (H, 2 * ((R + 1) // 2) + R), F32, kind="Internal").ap()
    ctx_tokens = a["ctx_1024"]

    def weights(prefix):
        return [a[prefix + w] for w in ("Wq", "bq", "Wk", "bk", "Wv", "bv", "Wo", "bo")]

    with ExitStack() as ctx:
        c = constants(nc, ctx)
        moe0 = ExitStack()
        w0 = ExpertWeights(nc, moe0, "L0_moe", a["L0_ffn_kernel_gating_EDF"], a["L0_ffn_kernel_up_EDF"],
                           a["L0_ffn_kernel_down_EFD"])
        attention(nc, "L0_attn", c, a["x"], None, hop[0], *weights("L0_attn_"), transposed=True, topk=32,
                  gates=a["L0_attn_head_gates"], rel_bias=a["L0_attn_rel_bias"], bias_rows=bias_rows,
                  later=w0)
        attention(nc, "L0_xattn", c, hop[0], ctx_tokens, hop[1], *weights("L0_xattn_"), transposed=False,
                  mask=a["mask_BxSxS2_bf1"])
        experts(nc, "L0_ffn", c, hop[1], hop[2], a["L0_ffn_router_kernel_DE"], w0, renormalise=True)
        moe0.close()
        w1 = ExpertWeights(nc, ctx, "L1_moe", a["L1_ffn_w1"], a["L1_ffn_w3"], a["L1_ffn_w2"])
        attention(nc, "L1_attn", c, hop[2], None, hop[3], *weights("L1_attn_"), transposed=False, causal=True,
                  later=w1)
        attention(nc, "L1_xattn", c, hop[3], ctx_tokens, hop[4], *weights("L1_xattn_"), transposed=True, topk=64,
                  scrambled=True)
        experts(nc, "L1_ffn", c, hop[4], out, a["L1_ffn_w_router"].rearrange("e d -> d e"), w1, renormalise=False)


def kernel(**inputs):
    import numpy as _np
    import concourse.bacc as _bacc
    from concourse import mybir as _mybir
    from concourse.bass_utils import run_bass_kernel_spmd as _run

    nc = _bacc.Bacc("TRN2", target_bir_lowering=False, num_devices=1)
    arrays, args = {}, {}
    for name, value in inputs.items():
        v = _np.ascontiguousarray(value)
        arrays[f"in_{name}_dram"] = v
        args[name] = nc.dram_tensor(f"in_{name}_dram", v.shape, _mybir.dt.from_np(v.dtype), kind="ExternalInput").ap()
    out = nc.dram_tensor("out_0_dram", inputs["x"].shape, F32, kind="ExternalOutput").ap()
    decoder(nc, args, out)
    r = _run(nc, [arrays], core_ids=[0])
    return r.results[0]["out_0_dram"]
```
